# Optimizing a Trainium2 kernel written in Bass

```python
import numpy as np
import jax
import jax.numpy as jnp

def _softmax(x, axis=-1):
    return jax.nn.softmax(x, axis=axis)

def _gelu(x):
    return jax.nn.gelu(x, approximate=True)

def _silu(x):
    return jax.nn.silu(x)

def _sigmoid(x):
    return jax.nn.sigmoid(x)

def _layernorm(x, axis=-1, eps=1e-05):
    m = jnp.mean(x, axis=axis, keepdims=True)
    v = jnp.var(x, axis=axis, keepdims=True)
    return (x - m) / jnp.sqrt(v + eps)

def _scatter_add(tgt, idx, src, axis=0):
    return tgt.at[idx].add(src)

def _segment_sum(src, seg, n):
    return jax.ops.segment_sum(src, seg, n)
kernel_name = 'mk_gps_d1_gnn_r32_5b6517'

def setup_inputs(seed: int=0):
    np.random.seed(seed)
    _w = jnp.asarray

    def _rec_inputs():
        import jax
        import jax.numpy as jnp
        _gk = jax.random.key(seed)
        x = -0.000202 + 1 * jax.random.normal(jax.random.fold_in(_gk, 1), (3125, 256), jnp.float32)
        _s = jax.random.randint(jax.random.fold_in(_gk, 2), (25000,), 0, 3125, jnp.int32)
        _d = jax.random.randint(jax.random.fold_in(_gk, 3), (25000,), 0, 3125, jnp.int32)
        _loop = jnp.arange(3125, dtype=jnp.int32)
        src = jnp.concatenate([_s, _d, _loop])
        dst = jnp.concatenate([_d, _s, _loop])
        _o = jnp.argsort(dst, stable=True)
        src = src[_o]
        dst = dst[_o]
        edge_attr_4 = 0.00121237 + 1.00026 * jax.random.normal(jax.random.fold_in(_gk, 12), (53125, 4), jnp.float32)
        edge_attr_8 = jax.random.uniform(jax.random.fold_in(_gk, 13), (53125, 8), jnp.float32, 0.0, 1)
        node_vec1 = jax.random.uniform(jax.random.fold_in(_gk, 14), (3125, 1), jnp.float32, 0.0, 1)
        return (x, src, dst, edge_attr_4, edge_attr_8, node_vec1)
    x, src, dst, edge_attr_4, edge_attr_8, node_vec1 = _rec_inputs()

    def _L0_gnn_setup():
        import jax, jax.numpy as jnp
        import numpy as np
        N = 25000
        E = 12500
        MUL = 64
        NB = 8
        RN = 64
        NUM_NEIGH = 16.0
        INV_SQRT3 = 1.0 / np.sqrt(3.0)

        def _forward(node_input, node_attr, edge_attr, edge_length_embedded, W_sc0, W_sc1, W_lin1_0, W_lin1_1, fc_w0, fc_w1, W_lin2_0, W_lin2_1, edge_src, edge_dst):
            Nn = node_input.shape[0]
            z = node_attr
            x0 = node_input[:, :MUL]
            x1 = node_input[:, MUL:].reshape(Nn, MUL, 3)
            inv_m = 1.0 / np.sqrt(MUL)
            s0 = x0 @ W_sc0 * z * inv_m
            s1 = jnp.einsum('nuc,uv->nvc', x1, W_sc1) * z[:, :, None] * inv_m
            h0 = x0 @ W_lin1_0 * z * inv_m
            h1 = jnp.einsum('nuc,uv->nvc', x1, W_lin1_1) * z[:, :, None] * inv_m
            hid = jax.nn.silu(edge_length_embedded @ fc_w0 / np.sqrt(NB))
            w = hid @ fc_w1 / np.sqrt(RN)
            wA, wB, wC, wD = (w[:, :MUL], w[:, MUL:2 * MUL], w[:, 2 * MUL:3 * MUL], w[:, 3 * MUL:])
            xs0 = h0[edge_src]
            xs1 = h1[edge_src]
            sh0 = edge_attr[:, :1]
            sh1 = edge_attr[:, 1:4]
            midA = wA * xs0 * sh0
            midD = wD * jnp.einsum('euc,ec->eu', xs1, sh1) * INV_SQRT3
            midB = (wB * xs0)[:, :, None] * sh1[:, None, :]
            midC = wC[:, :, None] * xs1 * sh0[:, None, :]
            mid0 = jnp.concatenate([midA, midD], axis=1)
            mid1 = jnp.concatenate([midB, midC], axis=1)
            inv_nb = 1.0 / np.sqrt(NUM_NEIGH)
            y0 = jax.ops.segment_sum(mid0, edge_dst, num_segments=Nn) * inv_nb
            y1 = jax.ops.segment_sum(mid1.reshape(mid1.shape[0], -1), edge_dst, num_segments=Nn).reshape(Nn, 2 * MUL, 3) * inv_nb
            inv_2m = 1.0 / np.sqrt(2 * MUL)
            o0 = y0 @ W_lin2_0 * z * inv_2m
            o1 = jnp.einsum('nuc,uv->nvc', y1, W_lin2_1) * z[:, :, None] * inv_2m
            c_s = np.float32(np.sin(np.pi / 8.0))
            c_x = np.float32(np.cos(np.pi / 8.0))
            out0 = c_s * s0 + c_x * o0
            out1 = c_s * s1 + c_x * o1
            return jnp.concatenate([out0, out1.reshape(Nn, 3 * MUL)], axis=1)
        key = jax.random.key(seed)
        ks = jax.random.split(key, 14)
        f32 = jnp.float32
        return {'node_input': jax.random.normal(ks[0], (N, 4 * MUL), f32), 'node_attr': jnp.ones((N, 1), f32), 'edge_src': jax.random.randint(ks[1], (E,), 0, N, dtype=jnp.int32), 'edge_dst': jax.random.randint(ks[2], (E,), 0, N, dtype=jnp.int32), 'edge_attr': jax.random.normal(ks[3], (E, 4), f32), 'edge_length_embedded': jax.random.uniform(ks[4], (E, NB), f32), 'W_sc0': jax.random.normal(ks[5], (MUL, MUL), f32), 'W_sc1': jax.random.normal(ks[6], (MUL, MUL), f32), 'W_lin1_0': jax.random.normal(ks[7], (MUL, MUL), f32), 'W_lin1_1': jax.random.normal(ks[8], (MUL, MUL), f32), 'fc_w0': jax.random.normal(ks[9], (NB, RN), f32), 'fc_w1': jax.random.normal(ks[10], (RN, 4 * MUL), f32), 'W_lin2_0': jax.random.normal(ks[11], (2 * MUL, MUL), f32), 'W_lin2_1': jax.random.normal(ks[12], (2 * MUL, MUL), f32)}
    _L0_gnn_all = _L0_gnn_setup()
    _L0_gnn_in = {k: v for k, v in _L0_gnn_all.items() if k in ('W_sc0', 'W_sc1', 'W_lin1_0', 'W_lin1_1', 'fc_w0', 'fc_w1', 'W_lin2_0', 'W_lin2_1')}
    del _L0_gnn_all

    def _L0_mix_setup():
        import jax, jax.numpy as jnp
        import numpy as np
        HEADS = 8
        DIM_HEAD = 64
        EPS = 1e-05

        def _inst_norm_lastdim(t):
            mu = jnp.mean(t, axis=-1, keepdims=True)
            var = jnp.mean(jnp.square(t - mu), axis=-1, keepdims=True)
            return (t - mu) * jax.lax.rsqrt(var + EPS)
        key = jax.random.key(seed)
        k1, k2, k3, k4 = jax.random.split(key, 4)
        b, n, dim = (4, 256, 256)
        inner = HEADS * DIM_HEAD
        x = jax.random.normal(k1, (b, n, dim), dtype=jnp.float32)
        Wqkv = jax.random.normal(k2, (3 * inner, dim), dtype=jnp.float32) * (1.0 / np.sqrt(dim))
        Wout = jax.random.normal(k3, (dim, inner), dtype=jnp.float32) * (1.0 / np.sqrt(inner))
        bout = jax.random.normal(k4, (dim,), dtype=jnp.float32) * 0.01
        return {'x': x, 'Wqkv': Wqkv, 'Wout': Wout, 'bout': bout}
    _L0_mix_all = _L0_mix_setup()
    _L0_mix_in = {k: v for k, v in _L0_mix_all.items() if k in ('Wqkv', 'Wout', 'bout')}
    del _L0_mix_all

    def _L0_ffn_setup():
        import jax, jax.numpy as jnp
        import numpy as np
        B, S, H, F, E, K = (8, 128, 256, 512, 16, 2)
        EPS = 1e-05
        key = jax.random.key(seed)
        ks = jax.random.split(key, 9)
        sc = 0.02
        return {'x': jax.random.normal(ks[0], (B, S, H), dtype=jnp.float32), 'gate_w': jax.random.normal(ks[1], (H, E), dtype=jnp.float32) * sc, 'gate_b': jnp.zeros((E,), dtype=jnp.float32), 'w1': jax.random.normal(ks[2], (E, H, F), dtype=jnp.float32) * sc, 'b1': jnp.zeros((E, F), dtype=jnp.float32), 'w2': jax.random.normal(ks[3], (E, F, H), dtype=jnp.float32) * sc, 'b2': jnp.zeros((E, H), dtype=jnp.float32), 'gamma': jnp.ones((H,), dtype=jnp.float32), 'beta': jnp.zeros((H,), dtype=jnp.float32)}
    _L0_ffn_all = _L0_ffn_setup()
    _L0_ffn_in = {k: v for k, v in _L0_ffn_all.items() if k in ('gate_w', 'gate_b', 'w1', 'b1', 'w2', 'b2', 'gamma', 'beta')}
    del _L0_ffn_all
    return {'x': x, 'src': src, 'dst': dst, 'edge_attr_4': edge_attr_4, 'edge_attr_8': edge_attr_8, 'node_vec1': node_vec1, 'L0_gnn_W_sc0': _L0_gnn_in['W_sc0'], 'L0_gnn_W_sc1': _L0_gnn_in['W_sc1'], 'L0_gnn_W_lin1_0': _L0_gnn_in['W_lin1_0'], 'L0_gnn_W_lin1_1': _L0_gnn_in['W_lin1_1'], 'L0_gnn_fc_w0': _L0_gnn_in['fc_w0'], 'L0_gnn_fc_w1': _L0_gnn_in['fc_w1'], 'L0_gnn_W_lin2_0': _L0_gnn_in['W_lin2_0'], 'L0_gnn_W_lin2_1': _L0_gnn_in['W_lin2_1'], 'L0_mix_Wqkv': _L0_mix_in['Wqkv'], 'L0_mix_Wout': _L0_mix_in['Wout'], 'L0_mix_bout': _L0_mix_in['bout'], 'L0_ffn_gate_w': _L0_ffn_in['gate_w'], 'L0_ffn_gate_b': _L0_ffn_in['gate_b'], 'L0_ffn_w1': _L0_ffn_in['w1'], 'L0_ffn_b1': _L0_ffn_in['b1'], 'L0_ffn_w2': _L0_ffn_in['w2'], 'L0_ffn_b2': _L0_ffn_in['b2'], 'L0_ffn_gamma': _L0_ffn_in['gamma'], 'L0_ffn_beta': _L0_ffn_in['beta']}

def reference(x, src, dst, edge_attr_4, edge_attr_8, node_vec1, L0_gnn_W_sc0, L0_gnn_W_sc1, L0_gnn_W_lin1_0, L0_gnn_W_lin1_1, L0_gnn_fc_w0, L0_gnn_fc_w1, L0_gnn_W_lin2_0, L0_gnn_W_lin2_1, L0_mix_Wqkv, L0_mix_Wout, L0_mix_bout, L0_ffn_gate_w, L0_ffn_gate_b, L0_ffn_w1, L0_ffn_b1, L0_ffn_w2, L0_ffn_b2, L0_ffn_gamma, L0_ffn_beta):
    import jax
    import jax.numpy as jnp

    def _L0_gnn_ref(node_input, node_attr, edge_src, edge_dst, edge_attr, edge_length_embedded, W_sc0, W_sc1, W_lin1_0, W_lin1_1, fc_w0, fc_w1, W_lin2_0, W_lin2_1):
        import jax, jax.numpy as jnp
        import numpy as np
        N = 25000
        E = 12500
        MUL = 64
        NB = 8
        RN = 64
        NUM_NEIGH = 16.0
        INV_SQRT3 = 1.0 / np.sqrt(3.0)

        def _forward(node_input, node_attr, edge_attr, edge_length_embedded, W_sc0, W_sc1, W_lin1_0, W_lin1_1, fc_w0, fc_w1, W_lin2_0, W_lin2_1, edge_src, edge_dst):
            Nn = node_input.shape[0]
            z = node_attr
            x0 = node_input[:, :MUL]
            x1 = node_input[:, MUL:].reshape(Nn, MUL, 3)
            inv_m = 1.0 / np.sqrt(MUL)
            s0 = x0 @ W_sc0 * z * inv_m
            s1 = jnp.einsum('nuc,uv->nvc', x1, W_sc1) * z[:, :, None] * inv_m
            h0 = x0 @ W_lin1_0 * z * inv_m
            h1 = jnp.einsum('nuc,uv->nvc', x1, W_lin1_1) * z[:, :, None] * inv_m
            hid = jax.nn.silu(edge_length_embedded @ fc_w0 / np.sqrt(NB))
            w = hid @ fc_w1 / np.sqrt(RN)
            wA, wB, wC, wD = (w[:, :MUL], w[:, MUL:2 * MUL], w[:, 2 * MUL:3 * MUL], w[:, 3 * MUL:])
            xs0 = h0[edge_src]
            xs1 = h1[edge_src]
            sh0 = edge_attr[:, :1]
            sh1 = edge_attr[:, 1:4]
            midA = wA * xs0 * sh0
            midD = wD * jnp.einsum('euc,ec->eu', xs1, sh1) * INV_SQRT3
            midB = (wB * xs0)[:, :, None] * sh1[:, None, :]
            midC = wC[:, :, None] * xs1 * sh0[:, None, :]
            mid0 = jnp.concatenate([midA, midD], axis=1)
            mid1 = jnp.concatenate([midB, midC], axis=1)
            inv_nb = 1.0 / np.sqrt(NUM_NEIGH)
            y0 = jax.ops.segment_sum(mid0, edge_dst, num_segments=Nn) * inv_nb
            y1 = jax.ops.segment_sum(mid1.reshape(mid1.shape[0], -1), edge_dst, num_segments=Nn).reshape(Nn, 2 * MUL, 3) * inv_nb
            inv_2m = 1.0 / np.sqrt(2 * MUL)
            o0 = y0 @ W_lin2_0 * z * inv_2m
            o1 = jnp.einsum('nuc,uv->nvc', y1, W_lin2_1) * z[:, :, None] * inv_2m
            c_s = np.float32(np.sin(np.pi / 8.0))
            c_x = np.float32(np.cos(np.pi / 8.0))
            out0 = c_s * s0 + c_x * o0
            out1 = c_s * s1 + c_x * o1
            return jnp.concatenate([out0, out1.reshape(Nn, 3 * MUL)], axis=1)
        return _forward(node_input, node_attr, edge_attr, edge_length_embedded, W_sc0, W_sc1, W_lin1_0, W_lin1_1, fc_w0, fc_w1, W_lin2_0, W_lin2_1, edge_src, edge_dst)

    def _L0_mix_ref(x, Wqkv, Wout, bout):
        import jax, jax.numpy as jnp
        import numpy as np
        HEADS = 8
        DIM_HEAD = 64
        EPS = 1e-05

        def _inst_norm_lastdim(t):
            mu = jnp.mean(t, axis=-1, keepdims=True)
            var = jnp.mean(jnp.square(t - mu), axis=-1, keepdims=True)
            return (t - mu) * jax.lax.rsqrt(var + EPS)
        b, n, dim = x.shape
        qkv = jnp.einsum('bnc,fc->bnf', x, Wqkv)
        q, k, v = jnp.split(qkv, 3, axis=-1)

        def to_heads(t):
            return t.reshape(b, n, HEADS, DIM_HEAD).transpose(0, 2, 1, 3)
        q, k, v = (to_heads(q), to_heads(k), to_heads(v))
        k = _inst_norm_lastdim(k)
        v = _inst_norm_lastdim(v)
        dots = jnp.einsum('bhnd,bhne->bhde', k, v)
        out = jnp.einsum('bhnd,bhde->bhne', q, dots) / n
        out = out.transpose(0, 2, 1, 3).reshape(b, n, HEADS * DIM_HEAD)
        return jnp.einsum('bnf,cf->bnc', out, Wout) + bout

    def _L0_ffn_ref(x, gate_w, gate_b, w1, b1, w2, b2, gamma, beta):
        import jax, jax.numpy as jnp
        import numpy as np
        B, S, H, F, E, K = (8, 128, 256, 512, 16, 2)
        EPS = 1e-05
        gate_logits = x @ gate_w + gate_b
        topk_vals, topk_idx = jax.lax.top_k(gate_logits, K)
        topk_w = jax.nn.softmax(topk_vals, axis=-1)
        h = jax.nn.relu(jnp.einsum('bsh,ehf->bsef', x, w1) + b1)
        expert_out = jnp.einsum('bsef,efh->bseh', h, w2) + b2
        sel = jnp.take_along_axis(expert_out, topk_idx[:, :, :, None], axis=2)
        moe = jnp.sum(topk_w[..., None] * sel, axis=2)
        y = x + moe
        mu = jnp.mean(y, axis=-1, keepdims=True)
        var = jnp.var(y, axis=-1, keepdims=True)
        return (y - mu) / jnp.sqrt(var + EPS) * gamma + beta
    xn = _layernorm(x, axis=-1)
    x = x + _L0_gnn_ref(xn, node_vec1, src, dst, edge_attr_4, edge_attr_8, L0_gnn_W_sc0, L0_gnn_W_sc1, L0_gnn_W_lin1_0, L0_gnn_W_lin1_1, L0_gnn_fc_w0, L0_gnn_fc_w1, L0_gnn_W_lin2_0, L0_gnn_W_lin2_1) + _L0_mix_ref(xn[None], L0_mix_Wqkv, L0_mix_Wout, L0_mix_bout)[0]
    x = x + _L0_ffn_ref(_layernorm(x, axis=-1)[None], L0_ffn_gate_w, L0_ffn_gate_b, L0_ffn_w1, L0_ffn_b1, L0_ffn_w2, L0_ffn_b2, L0_ffn_gamma, L0_ffn_beta)[0]
    return x

_drawn_inputs = setup_inputs


def setup_inputs(seed=0):
    import zlib

    import numpy as np

    out = dict(_drawn_inputs(seed))
    spreads = {'L0_ffn_gate_b': (0.0, 0.1),
     'L0_ffn_b1': (0.0, 0.765),
     'L0_ffn_b2': (0.0, 0.1),
     'L0_ffn_gamma': (1.0, 0.2),
     'L0_ffn_beta': (0.0, 0.1)}
    factors = {'L0_mix_bout': 5.955}
    for name, (base, spread) in spreads.items():
        noise = np.random.default_rng([zlib.crc32(name.encode()), seed]).standard_normal(out[name].shape)
        drawn = base * np.exp(spread * noise) if base else spread * noise
        out[name] = jnp.asarray(drawn.astype(out[name].dtype))
    for name, factor in factors.items():
        out[name] = (out[name] * factor).astype(out[name].dtype)
    return out
```

```python
from contextlib import ExitStack

import numpy as np

import concourse.bass as bass
import concourse.mybir as mybir

P = 128
N, D = 3125, 256
MUL, COMP, NB, RN = 64, 3, 8, 64
HEADS, DH = 8, 64
INNER = HEADS * DH
FF, E = 512, 16
E_ALL = 53125
NT = -(-N // P)
NPAD = NT * P
GT = 4
GE = GT * P
NG = -(-E_ALL // GE)
ET = NG * GT
WIN = 64
CH = 5
NBLK = (2 * N + E * (P - 1)) // P
NSLOT = NBLK * P
FAR_SLOT = 2 * NSLOT
EPS = 1e-5
C_S = float(np.float32(np.sin(np.pi / 8)))
C_X = float(np.float32(np.cos(np.pi / 8)))
SC_SCALE = C_S / np.sqrt(MUL)
LIN2_SCALE = C_X / np.sqrt(2 * MUL) / 4.0 / np.sqrt(MUL) / np.sqrt(RN)

F32 = mybir.dt.float32
I32 = mybir.dt.int32
U32 = mybir.dt.uint32
ALU = mybir.AluOpType
ACT = mybir.ActivationFunctionType
AX = mybir.AxisListType.X
ds = bass.ds


def from_step(t, k):
    return not isinstance(t, int) or t >= k


def steps(eng, n, step):
    step(0, 0)
    step(1, 1)
    with eng.Fori(1, n // 2) as i:
        step(i * 2, 0)
        step(i * 2 + 1, 1)
    if n % 2:
        step(n - 1, 0)


def passed(eng, m):
    eng.sem_inc(m.passed, 1)


class Memory:
    pass


class Region:

    def __init__(self, whole):
        self.whole, self.at, self.size = whole, 0, whole.shape[1]

    def take(self, n):
        assert self.at + n <= self.size, (self.at, n, self.size)
        self.at += n
        return self.whole[:, self.at - n:self.at]


def row_stats(dve, link, m, st, s):
    nc = m.nc
    even, odd, a, b = st[:, :, 1], st[:, :, 4], m.tmp_a, m.tmp_b
    link(nc.vector.tensor_tensor(a, even, odd, ALU.subtract))
    link(nc.vector.scalar_tensor_tensor(b, a, 0.25, a, ALU.mult, ALU.mult))
    link(nc.vector.tensor_tensor(a, st[:, :, 2], st[:, :, 5], ALU.add))
    nc.vector.scalar_tensor_tensor(b, a, 1.0 / D, b, ALU.mult, ALU.add).then_inc(s["var_ready"], 1)
    link(nc.vector.tensor_tensor(m.gap, even, odd, ALU.add))
    dve.wait_ge(s["std_ready"], 1)
    link(nc.vector.reciprocal(m.rstd, a))
    nc.vector.scalar_tensor_tensor(m.shift, m.gap, -0.5, m.rstd, ALU.mult, ALU.mult).then_inc(s["stats_ready"], 1)


def row_std(act, m, s):
    act.wait_ge(s["var_ready"], 1)
    m.nc.scalar.activation(m.tmp_a, m.tmp_b, ACT.Sqrt, bias=m.eps).then_inc(s["std_ready"], 1)
    act.wait_ge(s["stats_ready"], 1)


def chain(dve, sem):
    count = [0]

    def link(ins):
        count[0] += 1
        ins.then_inc(sem, 1)
        dve.wait_ge(sem, count[0])
    return link


def stage_load(nc, m):
    loaded, made, centred = nc.semaphore("loaded"), nc.semaphore("made"), nc.semaphore("centred")
    with loaded as loaded, made as made, centred as centred, nc.Block() as block:
        loads = [
            (m.x.rearrange("p (t d) -> p t d", t=NT), m.ins["x"].rearrange("(t p) d -> p t d", p=P)),
            (m.z, m.ins["z"]), (m.src, m.ins["src"]), (m.dst_i, m.ins["dst"]), (m.base_i[0:1], m.ins["base"]),
            (m.base_bc, m.ins["base"].broadcast_to([P, m.ins["base"].shape[1]])),
            (m.ea, m.ins["ea"]),
            (m.wkv.rearrange("p (k f) -> p k f", k=2), m.ins["wkv"].rearrange("(k p) f -> p k f", p=P)),
            (m.wq.rearrange("p (k f) -> p k f", k=4), m.ins["wq"].rearrange("(k p) f -> p k f", p=P)),
            (m.wout.rearrange("p (k f) -> p k f", k=4), m.ins["wout"].rearrange("(k p) f -> p k f", p=P)),
            (m.wlin1.rearrange("p (k f) -> p k f", k=2), m.ins["wlin1"].rearrange("(k p) f -> p k f", p=P)),
            (m.wsc.rearrange("p (k f) -> p k f", k=2), m.ins["wsc"].rearrange("(k p) f -> p k f", p=P)),
            (m.wlin2.rearrange("p (k f) -> p k f", k=CH), m.ins["wlin2"].rearrange("(k p) f -> p k f", p=P)),
            (m.bout, m.ins["bout"].broadcast_to([P, m.ins["bout"].shape[1]])),
            (m.fc0, m.ins["fc0"]), (m.fc1, m.ins["fc1"]),
            (m.gate.rearrange("p (k f) -> p k f", k=2), m.ins["gate"].rearrange("(k p) f -> p k f", p=P)),
            (m.gateb, m.ins["gateb"].broadcast_to([P, m.ins["gateb"].shape[1]])),
        ]

        @block.sync
        def _(sp):
            for dst, src in loads:
                sp.dma_start(dst, src).then_inc(loaded, 16)

        @block.gpsimd
        def _(pool):
            nc.gpsimd.memset(m.ident, 0.0).then_inc(made, 1)
            nc.gpsimd.memset(m.upper, 1.0).then_inc(made, 1)
            nc.gpsimd.memset(m.ones, 1.0).then_inc(made, 1)
            nc.gpsimd.memset(m.zeros, 0.0).then_inc(made, 1)
            nc.gpsimd.memset(m.eps, EPS).then_inc(made, 1)
            nc.gpsimd.iota(m.iota_i, pattern=[[1, P]], base=0, channel_multiplier=0).then_inc(made, 1)
            nc.gpsimd.iota(m.node_i, pattern=[[P, NT]], base=0, channel_multiplier=1).then_inc(made, 1)
            nc.gpsimd.iota(m.steps_i, pattern=[[P, NT]], base=0, channel_multiplier=0).then_inc(made, 1)
            nc.gpsimd.memset(m.ysum, 0.0).then_inc(made, 1)
            pool.wait_ge(made, 2)
            nc.gpsimd.affine_select(out=m.ident, in_=m.ident, compare_op=ALU.not_equal, fill=1.0, base=0,
                                    pattern=[[-1, P]], channel_multiplier=1).then_inc(made, 1)
            nc.gpsimd.affine_select(out=m.upper, in_=m.upper, compare_op=ALU.is_gt, fill=0.0, base=0,
                                    pattern=[[1, P]], channel_multiplier=-1).then_inc(made, 1)
            pool.wait_ge(made, 11)

        @block.vector
        def _(dve):
            link = chain(dve, centred)
            dve.wait_ge(loaded, 16 * len(loads))
            dve.wait_ge(made, 8)
            w = m.wkv.rearrange("p (g d) -> p g d", d=DH)
            link(nc.vector.tensor_reduce(m.wmean, w, AX, ALU.add))
            link(nc.vector.tensor_scalar(m.wmean, m.wmean, 1.0 / DH, None, ALU.mult))
            nc.vector.tensor_tensor(w, w, m.wmean.unsqueeze(2).broadcast_to([P, 4 * HEADS, DH]), ALU.subtract)
            nc.vector.tensor_scalar(m.wsc, m.wsc, SC_SCALE, None, ALU.mult)
            w2 = m.wlin2.rearrange("p (k f) -> p k f", k=CH)
            link(nc.vector.tensor_scalar(m.wlin2, m.wlin2, LIN2_SCALE, None, ALU.mult))
            for q in range(2, CH):
                d_rows = w2[0:MUL, q, :] if q == 2 else w2[MUL:P, q, :]
                nc.vector.tensor_scalar(d_rows, d_rows, 1.0 / np.sqrt(3.0), None, ALU.mult)
            nc.vector.tensor_copy(m.iota, m.iota_i)
            nc.vector.tensor_copy(m.steps_of, m.steps_i)
            link(nc.vector.tensor_copy(m.node_f, m.node_i))
            nc.vector.tensor_scalar(m.valid, m.node_f, float(N), None, ALU.is_lt)
            nc.vector.tensor_copy(m.base_f, m.base_bc)
            link(nc.vector.tensor_copy(m.rel, m.dst_i))
            rel = m.rel.rearrange("p (g k) -> p g k", k=GT)
            link(nc.vector.tensor_tensor(rel, rel, m.base_f.unsqueeze(2).broadcast_to([P, NG, GT]), ALU.subtract))


def stage_attention(nc, m, s):
    x = m.x.rearrange("p (t d) -> p t d", t=NT)
    xnt = m.xnt.rearrange("p (k n) -> p k n", k=2)
    st = m.st.rearrange("p (t s) -> p t s", t=NT)
    pt, pk, pv, ph, pd = m.bank[0:2], m.bank[2:4], m.bank[4:6], m.bank[6], m.bank[7]
    with nc.Block() as block:
        @block.sync
        def _(sp):
            for j in range(0, NBLK, 8):
                sp.dma_start(m.slots_in[j * P:(j + 8) * P, :].rearrange("(p r) d -> p (r d)", p=P),
                             m.zeros).then_inc(m.zeroed, 16)

            def store_h(t, b):
                sp.wait_ge(s["h_ready"], t + 1)
                sp.dma_start(m.h_table[ds(t * P, P), :], m.h_out[b]).then_inc(s["h_stored"][b], 16)
            steps(sp, NT, store_h)
            sp.wait_ge(s["h_stored"][0], 16 * (NT - NT // 2))
            sp.wait_ge(s["h_stored"][1], 16 * (NT // 2))

        @block.vector
        def _(dve):
            link = chain(dve, s["dve_chain"])
            with dve.Fori(0, NT) as t:
                nc.vector.bn_stats(st[:, ds(t, 1), :].rearrange("p a s -> p (a s)"),
                                   x[:, ds(t, 1), :].rearrange("p a d -> p (a d)")).then_inc(s["bn_done"], 1)
            dve.wait_ge(s["bn_done"], NT)
            row_stats(dve, link, m, st, s)

            def scaled_values(t, b):
                dve.wait_ge(s["squared"], t + 1)
                nc.vector.tensor_reduce(m.sumsq[b], m.sq[b].rearrange("p (g d) -> p g d", d=DH), AX,
                                        ALU.add).then_inc(s["sumsq_ready"], 1)
                dve.wait_ge(s["stds_ready"], t + 1)
                nc.vector.tensor_tensor(m.rk, m.stds[b][:, 0:HEADS], m.stds[b][:, HEADS:2 * HEADS], ALU.mult).then_inc(s["v_chain"], 1)
                dve.wait_ge(s["v_chain"], 2 * t + 1)
                nc.vector.reciprocal(m.rk, m.rk).then_inc(s["v_chain"], 1)
                dve.wait_ge(s["v_chain"], 2 * t + 2)
                if from_step(t, 2):
                    dve.wait_ge(s["dots_done"], t - 1)
                nc.vector.tensor_tensor(m.vs[b].rearrange("p (g d) -> p g d", d=DH),
                                        pv[b][:].rearrange("p (g d) -> p g d", d=DH),
                                        m.rk.unsqueeze(2).broadcast_to([P, HEADS, DH]), ALU.mult).then_inc(s["vs_ready"], 1)

            def copy_xnt(t, b):
                dve.wait_ge(s["turned"], t + 1)
                if from_step(t, 2):
                    dve.wait_ge(s["kv_done"], t - 1)
                    dve.wait_ge(s["xnt_kept"], t - 1)
                nc.vector.tensor_copy(m.xnt_t[b], pt[b][:, 0:2 * P]).then_inc(s["xnt_ready"], 1)

            copy_xnt(0, 0)

            def step(t, b):
                if not isinstance(t, int) or t < NT - 1:
                    copy_xnt(t + 1, 1 - b)
                scaled_values(t, b)
            steps(dve, NT, step)

        @block.scalar
        def _(act):
            row_std(act, m, s)

            def normalise(t, b):
                if from_step(t, 2):
                    act.wait_ge(s["turned"], t - 1)
                nc.scalar.activation(m.xn[b], x[:, ds(t, 1), :].rearrange("p a d -> p (a d)"), ACT.Identity,
                                     bias=m.shift[:, ds(t, 1)], scale=m.rstd[:, ds(t, 1)]).then_inc(s["xn_ready"], 1)
            normalise(0, 0)

            def step(t, b):
                if not isinstance(t, int) or t < NT - 1:
                    normalise(t + 1, 1 - b)
                act.wait_ge(s["kv_done"], t + 1)
                if from_step(t, 2):
                    act.wait_ge(s["vs_ready"], t - 1)
                nc.scalar.activation(m.sq[b][:, 0:INNER], pk[b][:], ACT.Square)
                nc.scalar.activation(m.sq[b][:, INNER:2 * INNER], pv[b][:], ACT.Square).then_inc(s["squared"], 1)
                if from_step(t, 2):
                    act.wait_ge(s["dots_done"], t - 1)
                nc.scalar.copy(m.kc[b], pk[b][:]).then_inc(s["k_ready"], 1)
                act.wait_ge(s["sumsq_ready"], t + 1)
                nc.scalar.activation(m.stds[b], m.sumsq[b], ACT.Sqrt, bias=m.eps, scale=1.0 / DH).then_inc(s["stds_ready"], 1)
                act.wait_ge(s["h_done"], t + 1)
                if from_step(t, 2):
                    act.wait_ge(s["h_stored"][b], 8 * (t - b))
                nc.scalar.activation(m.h_out[b], ph[:, 0:D], ACT.Copy, scale=m.z[:, ds(t, 1)]).then_inc(s["h_ready"], 1)
            steps(act, NT, step)

        @block.gpsimd
        def _(pool):
            def step(t, b):
                pool.wait_ge(s["xnt_ready"], t + 1)
                nc.gpsimd.tensor_copy(xnt[:, :, ds(t * P, P)], m.xnt_t[b].rearrange("p (k n) -> p k n", k=2)).then_inc(s["xnt_kept"], 1)
                pool.wait_ge(s["xn_ready"], t + 1)
                xt = x[:, ds(t, 1), :].rearrange("p a d -> p (a d)")
                nc.gpsimd.tensor_tensor(xt, xt, m.bout, ALU.add)
            steps(pool, NT, step)

        @block.tensor
        def _(pe):
            wkv = m.wkv.rearrange("p (k f) -> p k f", k=2)
            wl = m.wlin1.rearrange("p (k f) -> p k f", k=2)

            def turn(t, b):
                pe.wait_ge(s["xn_ready"], t + 1)
                if from_step(t, 2):
                    pe.wait_ge(s["xnt_ready"], t - 1)
                nc.tensor.transpose(pt[b][:, 0:P], m.xn[b][:, 0:P], m.ident)
                nc.tensor.transpose(pt[b][:, P:2 * P], m.xn[b][:, P:2 * P], m.ident).then_inc(s["turned"], 1)

            def keys_values(t, b):
                pe.wait_ge(s["xnt_ready"], t + 1)
                if from_step(t, 2):
                    pe.wait_ge(s["k_ready"], t - 1)
                    pe.wait_ge(s["vs_ready"], t - 1)
                for k in range(2):
                    nc.tensor.matmul(pk[b][:], m.xnt_t[b][:, k * P:(k + 1) * P], wkv[:, k, 0:INNER], start=k == 0, stop=k == 1)
                for k in range(2):
                    last = nc.tensor.matmul(pv[b][:], m.xnt_t[b][:, k * P:(k + 1) * P], wkv[:, k, INNER:2 * INNER],
                                            start=k == 0, stop=k == 1)
                last.then_inc(s["kv_done"], 1)
                if from_step(t, 1):
                    pe.wait_ge(s["h_ready"], t)
                for k in range(2):
                    last = nc.tensor.matmul(ph[:, k * P:(k + 1) * P], m.xnt_t[b][:, k * P:(k + 1) * P], wl[:, k, :],
                                            start=True, stop=True)
                last.then_inc(s["h_done"], 1)

            def dots(t, b, final=False):
                pe.wait_ge(s["vs_ready"], t + 1)
                pe.wait_ge(s["k_ready"], t + 1)
                for p in range(4):
                    last = nc.tensor.matmul(pd[:, p * P:(p + 1) * P], m.vs[b][:, p * P:(p + 1) * P], m.kc[b][:, p * P:(p + 1) * P],
                                            start=isinstance(t, int) and t == 0 and p == 0, stop=final,
                                            skip_group_check=True)
                last.then_inc(s["dots_done"], 1)

            turn(0, 0)

            def step(t, b):
                if not isinstance(t, int) or t < NT - 1:
                    turn(t + 1, 1 - b)
                keys_values(t, b)
                if from_step(t, 1):
                    dots(t - 1, 1 - b)
            steps(pe, NT, step)
            dots(NT - 1, (NT - 1) % 2, True)


def stage_mix(nc, m, s):
    x = m.x.rearrange("p (t d) -> p t d", t=NT)
    xnt = m.xnt.rearrange("p (k n) -> p k n", k=2)
    pd, pg, pm = m.bank[7], m.bank[0:2], m.bank[2]
    mix = m.mix.rearrange("p (k f) -> p k f", k=2)
    wsc = m.wsc.rearrange("p (k f) -> p k f", k=2)
    px = m.bank[3:5]
    with nc.Block() as block:
        @block.vector
        def _(dve):
            nc.vector.memset(m.dots, 0.0).then_inc(s["cleared"], 1)
            dve.wait_ge(s["cleared"], 1)
            for hh in range(2):
                q = slice(hh * DH, (hh + 1) * DH)
                d = m.dots.rearrange("p (a d) -> p a d", a=4)[q, :, q]
                last = nc.vector.tensor_scalar(d, pd[:].rearrange("p (a d) -> p a d", a=4)[q, :, q], 1.0 / N, None, ALU.mult)
                last.then_inc(s["dots_ready"], 1)
            for a in range(2):
                dve.wait_ge(s["g_done"], a + 1)
                nc.vector.tensor_copy(m.g[:, a * 512:(a + 1) * 512], pg[a][:]).then_inc(s["g_ready"], 1)
            dve.wait_ge(s["m_done"], 1)
            nc.vector.tensor_copy(m.mix, pm[:]).then_inc(s["mix_ready"], 1)

            def step(t, b):
                xt = x[:, ds(t, 1), :].rearrange("p a d -> p (a d)")
                dve.wait_ge(s["mixed"], t + 1)
                nc.vector.tensor_tensor(xt, px[b][:, 0:D], xt, ALU.add).then_inc(s["x_mixed"], 1)
                dve.wait_ge(s["x_mixed"], t + 1)
                nc.vector.scalar_tensor_tensor(xt, px[b][:, D:2 * D], m.z[:, ds(t, 1)], xt, ALU.mult,
                                               ALU.add).then_inc(s["x_ready"], 1)
            steps(dve, NT, step)

        @block.scalar
        def _(act):
            def step(t, b):
                if from_step(t, 2):
                    act.wait_ge(s["mixed"], t - 1)
                nc.scalar.copy(m.xnt_t[b].rearrange("p (k n) -> p k n", k=2), xnt[:, :, ds(t * P, P)]).then_inc(s["staged"], 1)
            steps(act, NT, step)

        @block.tensor
        def _(pe):
            pe.wait_ge(s["dots_ready"], 2)
            for p in range(4):
                last = nc.tensor.matmul(pg[p // 2][:, (p % 2) * D:(p % 2 + 1) * D], m.dots[:, p * P:(p + 1) * P],
                                        m.wout[:, p * D:(p + 1) * D], start=True, stop=True)
                if p % 2:
                    last.then_inc(s["g_done"], 1)
            pe.wait_ge(s["g_ready"], 2)
            for c in range(2):
                for p in range(4):
                    last = nc.tensor.matmul(pm[:, c * D:(c + 1) * D], m.wq[:, p * D + c * P:p * D + (c + 1) * P],
                                            m.g[:, p * D:(p + 1) * D], start=p == 0, stop=p == 3)
            last.then_inc(s["m_done"], 1)
            pe.wait_ge(s["mix_ready"], 1)

            def step(t, b):
                pe.wait_ge(s["staged"], t + 1)
                if from_step(t, 2):
                    pe.wait_ge(s["x_ready"], t - 1)
                for k in range(2):
                    nc.tensor.matmul(px[b][:, 0:D], m.xnt_t[b][:, k * P:(k + 1) * P], mix[:, k, :], start=k == 0, stop=k == 1)
                for k in range(2):
                    last = nc.tensor.matmul(px[b][:, D + k * P:D + (k + 1) * P], m.xnt_t[b][:, k * P:(k + 1) * P], wsc[:, k, :],
                                            start=False, stop=True, skip_group_check=True)
                last.then_inc(s["mixed"], 1)
            steps(pe, NT, step)


PCOLS = 9 * MUL
CHUNK_AT = [0, 2 * MUL, 4 * MUL, 5 * MUL, 7 * MUL]
CHUNK_BY = [0, 0, 1, 2, 3]


EARLY = E - 2


def load_w1(sp, m, e):
    sp.dma_start(m.w1[:, e * 1024:(e + 2) * 1024].rearrange("p (e k f) -> p e k f", e=2, k=2),
                 m.ins["w1"][e:e + 2].rearrange("e (k p) f -> p e k f", p=P)).then_inc(m.w1_loaded, 16)


def stage_edges(nc, m, s):
    pre, wp, seg = m.bank[0:2], [m.bank[2:4], m.bank[4:6]], m.bank[6:8]
    ysum = m.ysum.rearrange("p (q n) -> p q n", q=CH)
    with nc.Block() as block:
        @block.sync
        def _(sp):
            for e in range(0, EARLY, 2):
                load_w1(sp, m, e)

            def step(g, b):
                if from_step(g, 2):
                    sp.wait_ge(s["pre_done"], g - 1)
                sp.dma_start(m.e8[b], m.ins["e8"][:, ds(g * 2 * P, 2 * P)]).then_inc(s["e8_loaded"][b], 16)
            steps(sp, NG, step)

        @block.gpsimd
        def _(pool):
            def gather(g, b):
                if from_step(g, 2):
                    pool.wait_ge(s["product_done"], 2 * g - 2)
                nc.gpsimd.tensor_copy(m.idx[b], m.src[:, ds(g * GT, GT)]).then_inc(s["idx_ready"], 1)
                pool.wait_ge(s["idx_ready"], g + 1)
                passed(pool, m)
                for k in range(GT):
                    nc.gpsimd.indirect_dma_start(
                        out=m.xs[b][:, k * D:(k + 1) * D], out_offset=None, in_=m.h_table,
                        in_offset=bass.IndirectOffsetOnAxis(ap=m.idx[b][:, k:k + 1], axis=0)).then_inc(s["xs_loaded"][b][k], 16)

            def select(g, b):
                pool.wait_ge(s["onehot_ready"], g + 1)
                if from_step(g, 2):
                    pool.wait_ge(s["seg_done"], g - 1)
                nc.gpsimd.tensor_tensor(
                    m.sel[b].rearrange("p (k c n) -> p k c n", k=GT, c=4),
                    m.onehot[b].rearrange("p (k n) -> p k n", k=GT).unsqueeze(2).broadcast_to([P, GT, 4, WIN]),
                    m.ea[:, ds(g * 4 * GT, 4 * GT)].rearrange("p (k c) -> p k c", k=GT).unsqueeze(3).broadcast_to([P, GT, 4, WIN]),
                    ALU.mult).then_inc(s["sel_ready"], 1)

            gather(0, 0)

            def step(g, b):
                if not isinstance(g, int) or g < NG - 1:
                    gather(g + 1, 1 - b)
                select(g, b)
            steps_even(pool, NG, step)

        @block.scalar
        def _(act):
            def step(g, b):
                act.wait_ge(s["pre_done"], g + 1)
                if from_step(g, 2):
                    act.wait_ge(s["w_done"], 2 * g - 2)
                nc.scalar.activation(m.hid[b], pre[b][:, 0:2 * P], ACT.Silu, scale=1.0 / np.sqrt(NB)).then_inc(s["hid_ready"], 1)

            def again(g, b):
                for h in range(2):
                    act.wait_ge(s["b_done"], 2 * g + h + 1)
                    pr = m.prod[b][:, 2 * h * PCOLS:2 * (h + 1) * PCOLS].rearrange("p (k q d) -> p k q d", k=2, q=9)
                    nc.scalar.copy(pr[:, :, 7, :], pr[:, :, 5, :]).then_inc(s["b_again"], 1)
            step(0, 0)
            step(1, 1)

            def both(g, b):
                again(g, b)
                if not isinstance(g, int) or g < NG - 2:
                    step(g + 2, b)
            steps_even(act, NG, both)

        @block.vector
        def _(dve):
            def onehot(g, b):
                if from_step(g, 2):
                    dve.wait_ge(s["sel_ready"], g - 1)
                nc.vector.tensor_tensor(
                    m.onehot[b].rearrange("p (k n) -> p k n", k=GT),
                    m.iota[:, 0:WIN].unsqueeze(1).broadcast_to([P, GT, WIN]),
                    m.rel[:, ds(g * GT, GT)].unsqueeze(2).broadcast_to([P, GT, WIN]), ALU.is_equal).then_inc(s["onehot_ready"], 1)

            def products(g, b):
                if from_step(g, 2):
                    dve.wait_ge(s["seg_done"], g - 1)
                for h in range(2):
                    dve.wait_ge(s["w_done"], 2 * g + h + 1)
                    for k in range(2 * h, 2 * h + 2):
                        dve.wait_ge(s["xs_loaded"][b][k], 8 * (g - b) + 16)
                    w = wp[b][h][:].rearrange("p (k q d) -> p k q d", k=2, q=4)
                    xs = m.xs[b][:, 2 * h * D:2 * (h + 1) * D].rearrange("p (k q d) -> p k q d", k=2, q=4)
                    pr = m.prod[b][:, 2 * h * PCOLS:2 * (h + 1) * PCOLS].rearrange("p (k q d) -> p k q d", k=2, q=9)
                    nc.vector.tensor_tensor(pr[:, :, 0:6:5, :], w[:, :, 0:2, :], xs[:, :, 0:1, :].broadcast_to([P, 2, 2, MUL]),
                                            ALU.mult).then_inc(s["b_done"], 1)
                    nc.vector.tensor_tensor(pr[:, :, 1:4, :], w[:, :, 2:3, :].broadcast_to([P, 2, 3, MUL]), xs[:, :, 1:4, :], ALU.mult)
                    nc.vector.tensor_tensor(pr[:, :, 4:9:2, :], w[:, :, 3:4, :].broadcast_to([P, 2, 3, MUL]), xs[:, :, 1:4, :],
                                            ALU.mult).then_inc(s["product_done"], 1)

            def add_window(g, b, base=None):
                if base is None:
                    base = dve.value_load(m.base_i[0:1, ds(g, 1)], min_val=0, max_val=NPAD - WIN)
                dve.wait_ge(s["seg_done"], g + 1)
                if from_step(g, 1):
                    dve.wait_ge(s["added"], g)
                y = ysum[:, :, ds(base, WIN)]
                nc.vector.tensor_tensor(y, seg[b][:, 0:CH * WIN].rearrange("p (q n) -> p q n", q=CH), y, ALU.add).then_inc(s["added"], 1)

            onehot(0, 0)

            def step(g, b):
                if not isinstance(g, int) or g < NG - 1:
                    onehot(g + 1, 1 - b)
                products(g, b)
                if from_step(g, 1):
                    add_window(g - 1, 1 - b)
            steps_even(dve, NG, step)
            add_window(NG - 1, (NG - 1) % 2)

        @block.tensor
        def _(pe):
            def radial_in(g, b):
                pe.wait_ge(s["e8_loaded"][b], 8 * (g - b) + 16)
                if from_step(g, 2):
                    pe.wait_ge(s["hid_ready"], g - 1)
                nc.tensor.matmul(pre[b][:, 0:2 * P], m.fc0, m.e8[b], start=True, stop=True).then_inc(s["pre_done"], 1)

            def radial_out(g, b):
                pe.wait_ge(s["hid_ready"], g + 1)
                if from_step(g, 2):
                    pe.wait_ge(s["product_done"], 2 * g - 2)
                for k in range(GT):
                    h = slice((k // 2) * RN, (k // 2 + 1) * RN)
                    last = nc.tensor.matmul(wp[b][k // 2][:, (k % 2) * D:(k % 2 + 1) * D], m.hid[b][h, (k % 2) * P:(k % 2 + 1) * P],
                                            m.fc1[h, :], start=True, stop=True)
                    if k % 2:
                        last.then_inc(s["w_done"], 1)

            def segments(g, b):
                pe.wait_ge(s["sel_ready"], g + 1)
                if from_step(g, 2):
                    pe.wait_ge(s["added"], g - 1)
                sel = m.sel[b].rearrange("p (k c n) -> p k c n", k=GT, c=4)
                for k in range(GT):
                    if k % 2 == 0:
                        pe.wait_ge(s["product_done"], 2 * g + k // 2 + 1)
                        pe.wait_ge(s["b_again"], 2 * g + k // 2 + 1)
                    for q, (at, by) in enumerate(zip(CHUNK_AT, CHUNK_BY)):
                        last = nc.tensor.matmul(seg[b][:, q * WIN:(q + 1) * WIN],
                                                m.prod[b][:, k * PCOLS + at:k * PCOLS + at + P], sel[:, k, by, :],
                                                start=k == 0 and q == 0, stop=k == GT - 1, skip_group_check=True)
                last.then_inc(s["seg_done"], 1)

            radial_in(0, 0)
            radial_in(1, 1)
            radial_out(0, 0)

            def step(g, b):
                if not isinstance(g, int) or g < NG - 2:
                    radial_in(g + 2, b)
                if not isinstance(g, int) or g < NG - 1:
                    radial_out(g + 1, 1 - b)
                segments(g, b)
            steps_even(pe, NG, step)


def steps_even(eng, n, step):
    assert n % 2 == 0
    step(0, 0)
    step(1, 1)
    with eng.Fori(1, n // 2 - 1) as i:
        step(i * 2, 0)
        step(i * 2 + 1, 1)
    step(n - 2, 0)
    step(n - 1, 1)


def stage_nodes(nc, m, s):
    x = m.x.rearrange("p (t d) -> p t d", t=NT)
    st = m.st.rearrange("p (t s) -> p t s", t=NT)
    ysum = m.ysum.rearrange("p (q n) -> p q n", q=CH)
    po, pt, pl = m.bank[0:2], m.bank[2:4], m.bank[4]
    w2 = m.wlin2.rearrange("p (k f) -> p k f", k=CH)
    gate = m.gate.rearrange("p (k f) -> p k f", k=2)
    with nc.Block() as block:
        @block.scalar
        def _(act):
            def stage(t, b):
                if from_step(t, 2):
                    act.wait_ge(s["out_done"], t - 1)
                nc.scalar.copy(m.y_t[b].rearrange("p (q n) -> p q n", q=CH), ysum[:, :, ds(t * P, P)]).then_inc(s["staged"], 1)
            steps(act, NT, stage)
            row_std(act, m, s)

            def normalise(t, b):
                if from_step(t, 2):
                    act.wait_ge(s["turned"], t - 1)
                nc.scalar.activation(m.yn[b], x[:, ds(t, 1), :].rearrange("p a d -> p (a d)"), ACT.Identity,
                                     bias=m.shift[:, ds(t, 1)], scale=m.rstd[:, ds(t, 1)]).then_inc(s["yn_ready"], 1)
            steps(act, NT, normalise)

        @block.tensor
        def _(pe):
            def second_map(t, b):
                pe.wait_ge(s["staged"], t + 1)
                if from_step(t, 2):
                    pe.wait_ge(s["x_ready"], t - 1)
                o = po[b][:, 0:D].rearrange("p (a d) -> p a d", a=4)
                for q in range(CH):
                    out = o[:, 2 * q:2 * q + 2, :] if q < 2 else o[:, 0:q:q - 1, :]
                    last = nc.tensor.matmul(out, m.y_t[b][:, q * P:(q + 1) * P], w2[:, q, :].rearrange("p (a d) -> p a d", a=2),
                                            start=q == 0, stop=q == CH - 1, skip_group_check=True)
                last.then_inc(s["out_done"], 1)
            steps(pe, NT, second_map)

            def turn(t, b):
                pe.wait_ge(s["yn_ready"], t + 1)
                if from_step(t, 2):
                    pe.wait_ge(s["ynt_ready"], t - 1)
                nc.tensor.transpose(pt[b][:, 0:P], m.yn[b][:, 0:P], m.ident)
                nc.tensor.transpose(pt[b][:, P:2 * P], m.yn[b][:, P:2 * P], m.ident).then_inc(s["turned"], 1)

            def logits(t, b):
                pe.wait_ge(s["ynt_ready"], t + 1)
                for k in range(2):
                    last = nc.tensor.matmul(pl[:, ds(t * E, E)], m.yn_t[b][:, k * P:(k + 1) * P], gate[:, k, :],
                                            start=k == 0, stop=k == 1)
                last.then_inc(s["logits_done"], 1)
            turn(0, 0)

            def step(t, b):
                if not isinstance(t, int) or t < NT - 1:
                    turn(t + 1, 1 - b)
                logits(t, b)
            steps(pe, NT, step)

        @block.vector
        def _(dve):
            link = chain(dve, s["dve_chain"])

            def residual(t, b):
                xt = x[:, ds(t, 1), :].rearrange("p a d -> p (a d)")
                dve.wait_ge(s["out_done"], t + 1)
                nc.vector.scalar_tensor_tensor(xt, po[b][:, 0:D], m.z[:, ds(t, 1)], xt, ALU.mult, ALU.add).then_inc(s["x_ready"], 1)
                dve.wait_ge(s["x_ready"], t + 1)
                nc.vector.bn_stats(st[:, ds(t, 1), :].rearrange("p a s -> p (a s)"), xt).then_inc(s["bn_done"], 1)
            steps(dve, NT, residual)
            dve.wait_ge(s["bn_done"], NT)
            row_stats(dve, link, m, st, s)

            def copy(t, b):
                dve.wait_ge(s["turned"], t + 1)
                if from_step(t, 2):
                    dve.wait_ge(s["logits_done"], t - 1)
                nc.vector.tensor_copy(m.yn_t[b], pt[b][:, 0:2 * P]).then_inc(s["ynt_ready"], 1)
            steps(dve, NT, copy)

            dve.wait_ge(s["logits_done"], NT)
            lg = m.logits.rearrange("p (t e) -> p t e", t=NT)
            link(nc.vector.tensor_tensor(lg, pl[:, 0:NT * E].rearrange("p (t e) -> p t e", t=NT),
                                         m.gateb.unsqueeze(1).broadcast_to([P, NT, E]), ALU.add))


def stage_route(nc, m, s):
    lg = m.logits.rearrange("p (t e) -> p t e", t=NT)
    ohs = [v.rearrange("p (t e) -> p t e", t=NT) for v in m.oh]
    both = m.both.rearrange("p (t e) -> p t e", t=NT)
    pos = m.pos.rearrange("p (t e) -> p t e", t=NT)
    tot = m.tot.rearrange("p (t e) -> p t e", t=NT)
    top = m.top.rearrange("p (t j) -> p t j", t=NT)
    topi = m.topi.rearrange("p (t j) -> p t j", t=NT)
    ppre, ptot = m.bank[0], m.bank[1]
    iota_e = m.iota[:, 0:E].unsqueeze(1).broadcast_to([P, NT, E])
    with nc.Block() as block:
        @block.sync
        def _(sp):
            load_w1(sp, m, EARLY)
            for e in range(0, E, 2):
                sp.dma_start(m.w2[:, e * 1024:(e + 2) * 1024].rearrange("p (e k f) -> p e k f", e=2, k=4),
                             m.ins["w2"][e:e + 2].rearrange("e (k p) f -> p e k f", p=P)).then_inc(m.w2_loaded, 16)
            sp.dma_start(m.b1, m.ins["b1"]).then_inc(m.w2_loaded, 16)
            sp.dma_start(m.b2, m.ins["b2"].broadcast_to([P, m.ins["b2"].shape[1]])).then_inc(m.w2_loaded, 16)
            sp.dma_start(m.gamma, m.ins["gamma"].broadcast_to([P, m.ins["gamma"].shape[1]])).then_inc(m.w2_loaded, 16)
            sp.dma_start(m.beta, m.ins["beta"].broadcast_to([P, m.ins["beta"].shape[1]])).then_inc(m.w2_loaded, 16)

        @block.scalar
        def _(act):
            act.wait_ge(s["gap_ready"], 1)
            nc.scalar.activation(m.gw[1], m.gap, ACT.Exp).then_inc(s["exp_done"], 1)

        @block.tensor
        def _(pe):
            pe.wait_ge(s["both_ready"], 1)
            nc.tensor.matmul(ppre[:, 0:NT * E], m.upper, m.both, start=True, stop=True)
            nc.tensor.matmul(ptot[:, 0:NT * E], m.ones, m.both, start=True, stop=True).then_inc(s["counted"], 1)

        @block.vector
        def _(dve):
            link = chain(dve, s["dve_chain"])
            for t in range(NT):
                last = nc.vector.max(top[:, t, :], lg[:, t, :])
            link(last)
            for t in range(NT):
                last = nc.vector.max_index(topi[:, t, :], top[:, t, :], lg[:, t, :])
            nc.vector.tensor_tensor(m.gap, top[:, :, 1], top[:, :, 0], ALU.subtract).then_inc(s["gap_ready"], 1)
            link(last)
            for k in range(2):
                link(nc.vector.tensor_copy(m.tmp_a, topi[:, :, k]))
                link(nc.vector.tensor_tensor(ohs[k], iota_e, m.tmp_a.unsqueeze(2).broadcast_to([P, NT, E]), ALU.is_equal))
                link(nc.vector.tensor_tensor(ohs[k], ohs[k], m.valid.unsqueeze(2).broadcast_to([P, NT, E]), ALU.mult))
            nc.vector.tensor_tensor(both, ohs[0], ohs[1], ALU.add).then_inc(s["both_ready"], 1)
            dve.wait_ge(s["exp_done"], 1)
            link(nc.vector.tensor_scalar(m.tmp_a, m.gw[1], 1.0, None, ALU.add))
            link(nc.vector.reciprocal(m.gw[0], m.tmp_a))
            link(nc.vector.tensor_tensor(m.gw[1], m.gw[1], m.gw[0], ALU.mult))
            dve.wait_ge(s["counted"], 1)
            link(nc.vector.tensor_copy(m.tot, ptot[:, 0:NT * E]))
            for t in range(1, NT):
                link(nc.vector.tensor_tensor(tot[:, t, :], tot[:, t, :], tot[:, t - 1, :], ALU.add))
            more = m.more.rearrange("p (e j) -> p e j", e=E)
            link(nc.vector.tensor_tensor(more, tot[:, NT - 1, :].unsqueeze(2).broadcast_to([P, E, NT]),
                                         m.steps_of.unsqueeze(1).broadcast_to([P, E, NT]), ALU.is_gt))
            link(nc.vector.tensor_reduce(m.nblk, more, AX, ALU.add))
            link(nc.vector.tensor_tensor_scan(m.blk_end, m.ones[:, 0:E], m.nblk, 0.0, ALU.mult, ALU.add))
            link(nc.vector.tensor_tensor(m.nblk, m.blk_end, m.nblk, ALU.subtract))
            link(nc.vector.tensor_scalar(m.nblk, m.nblk, float(P), None, ALU.mult))
            link(nc.vector.tensor_tensor(pos, ppre[:, 0:NT * E].rearrange("p (t e) -> p t e", t=NT),
                                         m.nblk.unsqueeze(1).broadcast_to([P, NT, E]), ALU.add))
            link(nc.vector.tensor_tensor(pos[:, 1:NT, :], pos[:, 1:NT, :], tot[:, 0:NT - 1, :], ALU.add))
            link(nc.vector.tensor_scalar(m.gap, m.valid, -float(FAR_SLOT), float(FAR_SLOT), ALU.mult, ALU.add))
            for k in range(2):
                link(nc.vector.tensor_tensor(ohs[k], ohs[k], pos, ALU.mult))
                link(nc.vector.tensor_reduce(m.tmp_a, ohs[k], AX, ALU.add))
                link(nc.vector.tensor_tensor(m.tmp_a, m.tmp_a, m.gap, ALU.add))
                link(nc.vector.tensor_copy(m.slot[:, :, k], m.tmp_a))
            before = m.before.rearrange("p (j e) -> p j e", j=NBLK)
            link(nc.vector.tensor_tensor(before, m.blk_end.unsqueeze(1).broadcast_to([P, NBLK, E]),
                                         m.iota[:, 0:NBLK].unsqueeze(2).broadcast_to([P, NBLK, E]), ALU.is_le))
            link(nc.vector.tensor_reduce(m.blk_f, before, AX, ALU.add))
            link(nc.vector.tensor_scalar(m.blk_f, m.blk_f, float(E - 1), None, ALU.min))
            link(nc.vector.tensor_copy(m.blk_expert, m.blk_f))


def stage_dispatch(nc, m, s):
    x = m.x.rearrange("p (t d) -> p t d", t=NT)
    with nc.Block() as block:
        @block.scalar
        def _(act):
            def step(t, b):
                if from_step(t, 2):
                    act.wait_ge(s["sent"][b], 16 * (t - b))
                nc.scalar.activation(m.yn[b], x[:, ds(t, 1), :].rearrange("p a d -> p (a d)"), ACT.Identity,
                                     bias=m.shift[:, ds(t, 1)], scale=m.rstd[:, ds(t, 1)]).then_inc(s["yn_ready"], 1)
            steps(act, NT, step)

        @block.gpsimd
        def _(pool):
            pool.wait_ge(m.zeroed, 16 * (NBLK // 8))

            def step(t, b):
                if from_step(t, 2):
                    pool.wait_ge(s["sent"][b], 16 * (t - b))
                nc.gpsimd.tensor_copy(m.slot_t[b], m.slot[:, ds(t, 1), :].rearrange("p a k -> p (a k)")).then_inc(s["idx_ready"], 1)
                pool.wait_ge(s["idx_ready"], t + 1)
                pool.wait_ge(s["yn_ready"], t + 1)
                passed(pool, m)
                for k in range(2):
                    nc.gpsimd.indirect_dma_start(
                        out=m.slots_in, out_offset=bass.IndirectOffsetOnAxis(ap=m.slot_t[b][:, k:k + 1], axis=0),
                        in_=m.yn[b], in_offset=None, bounds_check=NSLOT - 1, oob_is_err=False).then_inc(s["sent"][b], 16)
            steps(pool, NT, step)
            pool.wait_ge(s["sent"][0], 32 * (NT - NT // 2))
            pool.wait_ge(s["sent"][1], 32 * (NT // 2))


def stage_experts(nc, m, s):
    px, ph, pt, py = m.bank[0:2], m.bank[2:4], m.bank[4:6], m.bank[6:8]
    with nc.Block() as block:
        @block.sync
        def _(sp):
            def load(j, b):
                if from_step(j, 2):
                    sp.wait_ge(s["x_turned"], j - 1)
                sp.dma_start(m.xb[b], m.slots_in[ds(j * P, P), :]).then_inc(s["x_loaded"][b], 16)

            def store(j, b):
                sp.wait_ge(s["y_ready"], j + 1)
                sp.dma_start(m.slots_out[ds(j * P, P), :], m.yb[b]).then_inc(s["y_stored"][b], 16)
            load(0, 0)
            load(1, 1)

            def step(j, b):
                if not isinstance(j, int) or j < NBLK - 2:
                    load(j + 2, b)
                store(j, b)
            steps_even(sp, NBLK, step)
            sp.wait_ge(s["y_stored"][0], 8 * NBLK)
            sp.wait_ge(s["y_stored"][1], 8 * NBLK)

        @block.tensor
        def _(pe):
            pe.wait_ge(m.w1_loaded, 16 * (E // 2))
            pe.wait_ge(m.w2_loaded, 16 * (E // 2 + 4))

            def turn_x(j, b):
                pe.wait_ge(s["x_loaded"][b], 8 * (j - b) + 16)
                if from_step(j, 2):
                    pe.wait_ge(s["xt_ready"], j - 1)
                nc.tensor.transpose(px[b][:, 0:P], m.xb[b][:, 0:P], m.ident)
                nc.tensor.transpose(px[b][:, P:2 * P], m.xb[b][:, P:2 * P], m.ident).then_inc(s["x_turned"], 1)

            def first(j, b):
                e = pe.value_load(m.blk_expert[0:1, ds(j, 1)], min_val=0, max_val=E - 1)
                pe.wait_ge(s["xt_ready"], j + 1)
                if from_step(j, 2):
                    pe.wait_ge(s["hr_ready"], j - 1)
                for k in range(2):
                    last = nc.tensor.matmul(ph[b][:], m.xbt[b][:, k * P:(k + 1) * P], m.w1[:, ds(e * 1024 + k * FF, FF)],
                                            start=k == 0, stop=k == 1)
                last.then_inc(s["h_done"], 1)

            def turn_h(j, b):
                pe.wait_ge(s["hr_ready"], j + 1)
                if from_step(j, 2):
                    pe.wait_ge(s["ht_ready"], j - 1)
                for k in range(4):
                    last = nc.tensor.transpose(pt[b][:, k * P:(k + 1) * P], m.hr[b][:, k * P:(k + 1) * P], m.ident)
                last.then_inc(s["h_turned"], 1)

            def second(j, b):
                e = pe.value_load(m.blk_expert[0:1, ds(j, 1)], min_val=0, max_val=E - 1)
                pe.wait_ge(s["ht_ready"], j + 1)
                if from_step(j, 2):
                    pe.wait_ge(s["y_ready"], j - 1)
                for k in range(4):
                    last = nc.tensor.matmul(py[b][:, 0:D], m.hbt[b][:, k * P:(k + 1) * P], m.w2[:, ds(e * 1024 + k * D, D)],
                                            start=k == 0, stop=k == 3)
                last.then_inc(s["y_done"], 1)

            turn_x(0, 0)
            turn_x(1, 1)
            first(0, 0)

            def step(j, b):
                turn_h(j, b)
                if not isinstance(j, int) or j < NBLK - 2:
                    turn_x(j + 2, b)
                if not isinstance(j, int) or j < NBLK - 1:
                    first(j + 1, 1 - b)
                second(j, b)
            steps_even(pe, NBLK, step)

        @block.scalar
        def _(act):
            act.wait_ge(m.w2_loaded, 16 * (E // 2 + 4))

            def copy_xt(j, b):
                act.wait_ge(s["x_turned"], j + 1)
                if from_step(j, 2):
                    act.wait_ge(s["h_done"], j - 1)
                nc.scalar.copy(m.xbt[b], px[b][:, 0:2 * P]).then_inc(s["xt_ready"], 1)

            def relu(j, b):
                e = act.value_load(m.blk_expert[0:1, ds(j, 1)], min_val=0, max_val=E - 1)
                act.wait_ge(s["h_turned"], j + 1)
                if from_step(j, 2):
                    act.wait_ge(s["y_done"], j - 1)
                for k in range(4):
                    last = nc.scalar.activation(m.hbt[b][:, k * P:(k + 1) * P], pt[b][:, k * P:(k + 1) * P], ACT.Relu,
                                                bias=m.b1[:, ds(e * 4 + k, 1)])
                last.then_inc(s["ht_ready"], 1)
            copy_xt(0, 0)
            copy_xt(1, 1)

            def step(j, b):
                relu(j, b)
                if not isinstance(j, int) or j < NBLK - 2:
                    copy_xt(j + 2, b)
            steps_even(act, NBLK, step)

        @block.vector
        def _(dve):
            dve.wait_ge(m.w2_loaded, 16 * (E // 2 + 4))

            def raw_h(j, b):
                dve.wait_ge(s["h_done"], j + 1)
                if from_step(j, 2):
                    dve.wait_ge(s["h_turned"], j - 1)
                nc.vector.tensor_copy(m.hr[b], ph[b][:]).then_inc(s["hr_ready"], 1)

            def rows_out(j, b):
                e = dve.value_load(m.blk_expert[0:1, ds(j, 1)], min_val=0, max_val=E - 1)
                dve.wait_ge(s["y_done"], j + 1)
                if from_step(j, 2):
                    dve.wait_ge(s["y_stored"][b], 8 * (j - b))
                nc.vector.tensor_tensor(m.yb[b], py[b][:, 0:D], m.b2[:, ds(e * D, D)], ALU.add).then_inc(s["y_ready"], 1)
            raw_h(0, 0)

            def step(j, b):
                if not isinstance(j, int) or j < NBLK - 1:
                    raw_h(j + 1, 1 - b)
                rows_out(j, b)
            steps_even(dve, NBLK, step)


def stage_combine(nc, m, s):
    x = m.x.rearrange("p (t d) -> p t d", t=NT)
    with nc.Block() as block:
        @block.gpsimd
        def _(pool):
            def fetch(t, b):
                if from_step(t, 2):
                    pool.wait_ge(s["summed"], t - 1)
                nc.gpsimd.tensor_copy(m.slot_t[b], m.slot[:, ds(t, 1), :].rearrange("p a k -> p (a k)")).then_inc(s["idx_ready"], 1)
                pool.wait_ge(s["idx_ready"], t + 1)
                passed(pool, m)
                for k in range(2):
                    nc.gpsimd.indirect_dma_start(
                        out=m.got[b][k], out_offset=None, in_=m.slots_out,
                        in_offset=bass.IndirectOffsetOnAxis(ap=m.slot_t[b][:, k:k + 1], axis=0),
                        bounds_check=NSLOT - 1, oob_is_err=False).then_inc(s["got"][b], 16)
            pool.wait_ge(s["cleared"], 4)
            fetch(0, 0)

            def step(t, b):
                if not isinstance(t, int) or t < NT - 1:
                    fetch(t + 1, 1 - b)
                pool.wait_ge(s["normed"], t + 1)
                if from_step(t, 2):
                    pool.wait_ge(s["x_out"], t - 1)
                nc.gpsimd.tensor_tensor(m.w[b], m.v[b], m.gamma, ALU.mult).then_inc(s["scaled"], 1)
                xt = x[:, ds(t, 1), :].rearrange("p a d -> p (a d)")
                nc.gpsimd.tensor_tensor(xt, xt, m.beta, ALU.add).then_inc(s["x_beta"], 1)
            steps(pool, NT, step)

        @block.scalar
        def _(act):
            def normalise(t, b):
                if from_step(t, 2):
                    act.wait_ge(s["summed"], t - 1)
                nc.scalar.activation(m.yn[b], x[:, ds(t, 1), :].rearrange("p a d -> p (a d)"), ACT.Identity,
                                     bias=m.shift[:, ds(t, 1)], scale=m.rstd[:, ds(t, 1)]).then_inc(s["yn_ready"], 1)
            normalise(0, 0)

            def step(t, b):
                if not isinstance(t, int) or t < NT - 1:
                    normalise(t + 1, 1 - b)
                act.wait_ge(s["var_ready"], t + 1)
                nc.scalar.activation(m.std[b], m.mv[b][:, 1:2], ACT.Sqrt, bias=m.eps).then_inc(s["std_ready"], 1)
            steps(act, NT, step)

        @block.vector
        def _(dve):
            for b in range(2):
                for k in range(2):
                    nc.vector.memset(m.got[b][k], 0.0).then_inc(s["cleared"], 1)

            def sums(t, b):
                dve.wait_ge(s["yn_ready"], t + 1)
                dve.wait_ge(s["got"][b], 16 * (t - b) + 32)
                if from_step(t, 2):
                    dve.wait_ge(s["normed"], t - 1)
                    dve.wait_ge(s["std_ready"], t - 1)
                nc.vector.scalar_tensor_tensor(m.u[b], m.got[b][0], m.gw[0][:, ds(t, 1)], m.yn[b], ALU.mult, ALU.add).then_inc(s["one_in"], 1)
                dve.wait_ge(s["one_in"], t + 1)
                nc.vector.scalar_tensor_tensor(m.u[b], m.got[b][1], m.gw[1][:, ds(t, 1)], m.u[b], ALU.mult, ALU.add).then_inc(s["summed"], 1)
                dve.wait_ge(s["summed"], t + 1)
                nc.vector.bn_stats(m.st1, m.u[b]).then_inc(s["bn_done"], 1)
                dve.wait_ge(s["bn_done"], t + 1)
                passed(dve, m)
                nc.vector.bn_aggr(m.mv[b][:, 0:2], m.st1).then_inc(s["var_ready"], 1)

            def normed(t, b):
                dve.wait_ge(s["std_ready"], t + 1)
                nc.vector.reciprocal(m.std[b], m.std[b]).then_inc(s["rstd_ready"], 1)
                dve.wait_ge(s["rstd_ready"], t + 1)
                if from_step(t, 2):
                    dve.wait_ge(s["scaled"], t - 1)
                nc.vector.tensor_scalar(m.v[b], m.u[b], m.mv[b][:, 0:1], m.std[b], ALU.subtract, ALU.mult).then_inc(s["normed"], 1)

            def finish(t, b):
                dve.wait_ge(s["scaled"], t + 1)
                dve.wait_ge(s["x_beta"], t + 1)
                xt = x[:, ds(t, 1), :].rearrange("p a d -> p (a d)")
                nc.vector.tensor_tensor(xt, m.w[b], xt, ALU.add).then_inc(s["x_out"], 1)
            sums(0, 0)

            def step(t, b):
                if not isinstance(t, int) or t < NT - 1:
                    sums(t + 1, 1 - b)
                normed(t, b)
                if from_step(t, 1):
                    finish(t - 1, 1 - b)
            steps(dve, NT, step)
            finish(NT - 1, (NT - 1) % 2)

        @block.sync
        def _(sp):
            def step(t, b):
                sp.wait_ge(s["x_out"], t + 1)
                sp.dma_start(m.out[ds(t * P, P), :], x[:, ds(t, 1), :].rearrange("p a d -> p (a d)")).then_inc(s["stored"], 16)
            steps(sp, NT, step)
            sp.wait_ge(s["stored"], 16 * NT)


def build(nc, m):
    m.nc = nc
    with ExitStack() as ctx:
        def sb(name, n, dt=F32):
            return ctx.enter_context(nc.sbuf_tensor(name, [P, n], dt))

        def sem(name):
            return ctx.enter_context(nc.semaphore(name))

        def sems(prefix, names, pairs=()):
            found = {n: sem(f"{prefix}_{n}") for n in names.split()}
            found.update({n: [sem(f"{prefix}_{n}{b}") for b in range(2)] for n in pairs})
            return found

        m.bank = [ctx.enter_context(nc.psum_tensor(f"bank{i}", [P, 512], F32)) for i in range(8)]
        m.h_table = nc.dram_tensor("h_table", [NPAD, D], F32, kind="Internal").ap()
        m.slots_in = nc.dram_tensor("slots_in", [NSLOT, D], F32, kind="Internal").ap()
        m.slots_out = nc.dram_tensor("slots_out", [NSLOT, D], F32, kind="Internal").ap()

        m.x = sb("x", NT * D)[:]
        keep = Region(sb("keep", 128 * 3 + 6 * NT + NT + 5 * 128 + 32 + 16 + 4 * NT + 6 * NT + 64))
        m.ident, m.upper, m.ones = keep.take(P), keep.take(P), keep.take(P)
        m.st = keep.take(6 * NT)
        m.z = keep.take(NT)
        m.wlin2 = keep.take(CH * P)
        m.gate, m.gateb = keep.take(2 * E), keep.take(E)
        m.rstd, m.shift, m.valid, m.node_f = keep.take(NT), keep.take(NT), keep.take(NT), keep.take(NT)
        m.tmp_a, m.tmp_b, m.gap = keep.take(NT), keep.take(NT), keep.take(NT)
        m.gw = [keep.take(NT), keep.take(NT)]
        m.steps_of, m.eps = keep.take(NT), keep.take(1)
        m.iota = sb("iota", P)[:]
        m.slot = sb("slot", NT * 2, I32)[:].rearrange("p (t k) -> p t k", k=2)
        m.slot_t = [sb(f"slot_t{b}", 2, I32)[:] for b in range(2)]
        m.blk_expert = sb("blk_expert", NBLK, I32)[:]

        low = sb("low", E * 1024)[:]
        m.ysum, m.w2 = low[:, 0:CH * NPAD], low
        high = sb("high", E * 1024)
        m.w1 = high[:]
        r = Region(high)
        m.wkv, m.wq, m.wout = r.take(2 * 2 * INNER), r.take(4 * D), r.take(4 * D)
        m.wlin1, m.wsc, m.bout, m.zeros = r.take(2 * P), r.take(2 * P), r.take(D), r.take(8 * D)
        m.wmean = r.take(4 * HEADS)
        m.dots, m.g, m.mix = r.take(4 * P), r.take(4 * D), r.take(2 * D)
        m.sumsq, m.stds = ([r.take(2 * HEADS) for _ in range(2)] for _ in range(2))
        m.rk = r.take(HEADS)
        m.xn, m.xnt_t, m.h_out = ([r.take(D) for _ in range(2)] for _ in range(3))
        m.sq = [r.take(2 * INNER) for _ in range(2)]
        m.vs, m.kc = ([r.take(INNER) for _ in range(2)] for _ in range(2))
        m.iota_i, m.node_i, m.steps_i = (r.take(n).bitcast(I32) for n in (P, NT, NT))
        m.dst_i, m.base_bc, m.base_f = r.take(ET).bitcast(I32), r.take(NG).bitcast(I32), r.take(NG)

        mid = sb("mid", 2 * GT * (PCOLS + 4 * WIN))
        m.xnt = mid[:, 0:2 * NPAD]
        r = Region(mid)
        m.prod = [r.take(GT * PCOLS) for _ in range(2)]
        m.sel = [r.take(GT * 4 * WIN) for _ in range(2)]
        r = Region(mid)
        m.b2, m.b1 = r.take(E * D), r.take(E * 4)
        m.gamma, m.beta = r.take(D), r.take(D)
        m.hr = [r.take(FF) for _ in range(2)]
        m.st1, m.mv, m.std = r.take(6), [r.take(2), r.take(2)], [r.take(1), r.take(1)]

        edge = sb("edge", 5430)
        r = Region(edge)
        m.ea, m.src, m.rel = r.take(4 * ET), r.take(ET).bitcast(I32), r.take(ET)
        m.base_i = r.take(NG).bitcast(I32)
        m.fc0, m.fc1 = r.take(P)[0:2 * NB], r.take(D)
        m.e8 = [v[0:2 * NB] for v in (r.take(2 * P), r.take(2 * P))]
        m.hid = [r.take(2 * P) for _ in range(2)]
        m.onehot = [r.take(GT * WIN) for _ in range(2)]
        m.idx = [r.take(GT).bitcast(I32) for _ in range(2)]
        r = Region(high)
        r.take(EARLY * 1024)
        m.xs = [r.take(GT * D) for _ in range(2)]
        r = Region(high)
        r.take(EARLY * 1024)
        m.y_t = [r.take(CH * P) for _ in range(2)]
        r = Region(edge)
        m.yn, m.yn_t = ([r.take(D) for _ in range(2)] for _ in range(2))
        m.logits, m.both, m.pos, m.tot = (r.take(NT * E) for _ in range(4))
        m.oh = [r.take(NT * E) for _ in range(2)]
        m.top, m.topi = r.take(NT * 8), r.take(NT * 8).bitcast(U32)
        m.more, m.before = r.take(E * NT), r.take(NBLK * E)[:, 0:NBLK * E]
        r = Region(mid)
        r.take(E * D + E * 4 + 2 * D)
        m.nblk, m.blk_end, m.blk_f = r.take(E), r.take(E), r.take(NBLK)
        r = Region(edge)
        r.take(2 * D)
        m.xb, m.xbt, m.yb = ([r.take(D) for _ in range(2)] for _ in range(3))
        m.hbt = [r.take(FF) for _ in range(2)]
        r = Region(edge)
        r.take(2 * D)
        m.got = [[r.take(D) for _ in range(2)] for _ in range(2)]
        m.u, m.v, m.w = ([r.take(D) for _ in range(2)] for _ in range(3))

        m.passed = sem("passed")
        m.zeroed, m.w1_loaded, m.w2_loaded = sem("zeroed"), sem("w1_loaded"), sem("w2_loaded")
        stage_load(nc, m)
        s = sems("att", "dve_chain bn_done var_ready std_ready stats_ready squared sumsq_ready stds_ready v_chain dots_done vs_ready turned kv_done xnt_kept "
                 "xnt_ready xn_ready k_ready h_done h_ready", ["h_stored"])
        stage_attention(nc, m, s)
        stage_mix(nc, m, sems("mix", "cleared dots_ready g_done g_ready m_done mix_ready mixed x_mixed x_ready staged"))
        s = sems("edge", "pre_done b_done b_again product_done idx_ready onehot_ready seg_done sel_ready w_done hid_ready added", ["e8_loaded"])
        s["xs_loaded"] = [[sem(f"edge_xs{b}_{k}") for k in range(GT)] for b in range(2)]
        stage_edges(nc, m, s)
        stage_nodes(nc, m, sems("node", "out_done staged var_ready std_ready stats_ready turned yn_ready x_ready ynt_ready logits_done "
                                "dve_chain bn_done"))
        stage_route(nc, m, sems("route", "gap_ready exp_done both_ready counted dve_chain"))
        stage_dispatch(nc, m, sems("send", "yn_ready idx_ready", ["sent"]))
        stage_experts(nc, m, sems("moe", "x_turned y_ready xt_ready hr_ready h_done ht_ready h_turned y_done",
                                  ["x_loaded", "y_stored"]))
        stage_combine(nc, m, sems("comb", "summed idx_ready cleared normed scaled x_beta yn_ready one_in bn_done "
                                  "var_ready std_ready rstd_ready x_out stored",
                                  ["got"]))


def kernel(x, src, dst, edge_attr_4, edge_attr_8, node_vec1, L0_gnn_W_sc0, L0_gnn_W_sc1, L0_gnn_W_lin1_0,
           L0_gnn_W_lin1_1, L0_gnn_fc_w0, L0_gnn_fc_w1, L0_gnn_W_lin2_0, L0_gnn_W_lin2_1, L0_mix_Wqkv, L0_mix_Wout,
           L0_mix_bout, L0_ffn_gate_w, L0_ffn_gate_b, L0_ffn_w1, L0_ffn_b1, L0_ffn_w2, L0_ffn_b2, L0_ffn_gamma,
           L0_ffn_beta):
    from concourse import bacc
    from concourse.bass_utils import run_bass_kernel_spmd

    perm = np.concatenate([np.arange(MUL)] + [MUL + c + COMP * np.arange(MUL) for c in range(COMP)])
    back = np.argsort(perm)
    f = np.float32

    def padded(a, rows, fill=0):
        out = np.full((rows,) + a.shape[1:], fill, a.dtype)
        out[:a.shape[0]] = a
        return out

    def diagonal(a, b):
        out = np.zeros((P, P), f)
        out[:MUL, :MUL], out[MUL:, MUL:] = a, b
        return out

    def crossed(a, b):
        out = np.zeros((P, P), f)
        out[:MUL, MUL:], out[MUL:, :MUL] = a, b
        return out

    x, src, dst, ea, e8, z = (np.asarray(v) for v in (x, src, dst, edge_attr_4, edge_attr_8, node_vec1))
    src_t = np.ascontiguousarray(padded(src, ET * P).reshape(ET, P).T)
    dst_p = padded(dst, ET * P, N - 1)
    wqkv = np.asarray(L0_mix_Wqkv)
    lin2_0, lin2_1 = np.asarray(L0_gnn_W_lin2_0), np.asarray(L0_gnn_W_lin2_1)
    fc0 = np.zeros((2 * NB, 2 * RN), f)
    fc0[:NB, :RN] = fc0[NB:, RN:] = np.asarray(L0_gnn_fc_w0)
    arrays = {
        "x": padded(x[:, perm], NPAD), "z": padded(z, NPAD).reshape(NT, P).T,
        "src": src_t, "dst": dst_p.reshape(ET, P).T, "base": dst_p[::GE].reshape(1, NG),
        "ea": padded(ea, ET * P).reshape(ET, P, 4).transpose(1, 0, 2).reshape(P, ET * 4),
        "e8": padded(e8, ET * P).reshape(NG, 2, 2 * P, NB).transpose(1, 3, 0, 2).reshape(2 * NB, NG * 2 * P),
        "wkv": wqkv[INNER:].T[perm], "wq": wqkv[:INNER][:, perm], "wout": np.asarray(L0_mix_Wout).T[:, perm],
        "bout": np.asarray(L0_mix_bout)[perm].reshape(1, D),
        "wlin1": np.concatenate([diagonal(L0_gnn_W_lin1_0, L0_gnn_W_lin1_1), diagonal(L0_gnn_W_lin1_1, L0_gnn_W_lin1_1)]),
        "wsc": np.concatenate([diagonal(L0_gnn_W_sc0, L0_gnn_W_sc1), diagonal(L0_gnn_W_sc1, L0_gnn_W_sc1)]),
        "wlin2": np.concatenate([diagonal(lin2_0[:MUL], lin2_1[MUL:]), diagonal(lin2_1[MUL:], lin2_1[MUL:])]
                                + [diagonal(lin2_0[MUL:], lin2_1[:MUL])] + [crossed(lin2_1[:MUL], lin2_0[MUL:])] * 2),
        "fc0": fc0, "fc1": np.concatenate([np.asarray(L0_gnn_fc_w1)] * 2),
        "gate": np.asarray(L0_ffn_gate_w)[perm], "gateb": np.asarray(L0_ffn_gate_b).reshape(1, E),
        "w1": np.asarray(L0_ffn_w1)[:, perm], "w2": np.asarray(L0_ffn_w2)[:, :, perm],
        "b1": np.asarray(L0_ffn_b1).reshape(E, 4, P).transpose(2, 0, 1).reshape(P, E * 4),
        "b2": np.asarray(L0_ffn_b2)[:, perm].reshape(1, E * D),
        "gamma": np.asarray(L0_ffn_gamma)[perm].reshape(1, D), "beta": np.asarray(L0_ffn_beta)[perm].reshape(1, D),
    }
    nc = bacc.Bacc("TRN2", target_bir_lowering=False, num_devices=1)
    held, fed = {}, {}
    for name, a in arrays.items():
        a = np.ascontiguousarray(a)
        fed[f"in_{name}"] = a
        held[name] = nc.dram_tensor(f"in_{name}", a.shape, mybir.dt.from_np(a.dtype), kind="ExternalInput").ap()
    m = Memory()
    m.ins = held
    m.out = nc.dram_tensor("out", (NPAD, D), F32, kind="ExternalOutput").ap()
    build(nc, m)
    r = run_bass_kernel_spmd(nc, [fed], core_ids=[0])
    return r.results[0]["out"][:N, back]
```

```python
from contextlib import ExitStack

import numpy as np

import concourse.bass as bass
import concourse.mybir as mybir

P = 128
N, D = 3125, 256
MUL, COMP, NB, RN = 64, 3, 8, 64
HEADS, DH = 8, 64
INNER = HEADS * DH
FF, E = 512, 16
E_ALL = 53125
NT = -(-N // P)
NPAD = NT * P
GT = 4
GE = GT * P
NG = -(-E_ALL // GE)
ET = NG * GT
WIN = 48
RING = 4
CH = 4
NBLK = (2 * N + E * (P - 1)) // P
NSLOT = NBLK * P
FAR_SLOT = 2 * NSLOT
EPS = 1e-5
C_S = float(np.float32(np.sin(np.pi / 8)))
C_X = float(np.float32(np.cos(np.pi / 8)))
SC_SCALE = C_S / np.sqrt(MUL)
LIN2_SCALE = C_X / np.sqrt(2 * MUL) / 4.0 / np.sqrt(MUL) / np.sqrt(RN)

F32 = mybir.dt.float32
I32 = mybir.dt.int32
U32 = mybir.dt.uint32
ALU = mybir.AluOpType
ACT = mybir.ActivationFunctionType
AX = mybir.AxisListType.X
ds = bass.ds


def from_step(t, k):
    return not isinstance(t, int) or t >= k


def steps(eng, n, step):
    step(0, 0)
    step(1, 1)
    with eng.Fori(1, n // 2) as i:
        step(i * 2, 0)
        step(i * 2 + 1, 1)
    if n % 2:
        step(n - 1, 0)


def steps_ring(eng, n, step):
    assert n % RING == 0
    for g in range(RING):
        step(g, g)
    with eng.Fori(1, n // RING - 1) as i:
        for q in range(RING):
            step(i * RING + q, q)
    for q in range(RING):
        step(n - RING + q, q)


def steps_tiles(eng, step):
    for t in range(RING):
        step(t, t)
    with eng.Fori(1, NT // RING) as i:
        for q in range(RING):
            step(i * RING + q, q)
    for t in range(NT // RING * RING, NT):
        step(t, t % RING)


def passed(eng, m):
    eng.sem_inc(m.passed, 1)


class Memory:
    pass


class Region:

    def __init__(self, whole):
        self.whole, self.at, self.size = whole, 0, whole.shape[1]

    def take(self, n):
        assert self.at + n <= self.size, (self.at, n, self.size)
        self.at += n
        return self.whole[:, self.at - n:self.at]


def row_stats(dve, link, m, st, s):
    nc = m.nc
    even, odd, a, b = st[:, :, 1], st[:, :, 4], m.tmp_a, m.tmp_b
    link(nc.vector.tensor_tensor(a, even, odd, ALU.subtract))
    link(nc.vector.scalar_tensor_tensor(b, a, 0.25, a, ALU.mult, ALU.mult))
    link(nc.vector.tensor_tensor(a, st[:, :, 2], st[:, :, 5], ALU.add))
    nc.vector.scalar_tensor_tensor(b, a, 1.0 / D, b, ALU.mult, ALU.add).then_inc(s["var_ready"], 1)
    link(nc.vector.tensor_tensor(m.gap, even, odd, ALU.add))
    dve.wait_ge(s["std_ready"], 1)
    link(nc.vector.reciprocal(m.rstd, a))
    nc.vector.scalar_tensor_tensor(m.shift, m.gap, -0.5, m.rstd, ALU.mult, ALU.mult).then_inc(s["stats_ready"], 1)


def row_std(act, m, s):
    act.wait_ge(s["var_ready"], 1)
    m.nc.scalar.activation(m.tmp_a, m.tmp_b, ACT.Sqrt, bias=m.eps).then_inc(s["std_ready"], 1)
    act.wait_ge(s["stats_ready"], 1)


def chain(dve, sem):
    count = [0]

    def link(ins):
        count[0] += 1
        ins.then_inc(sem, 1)
        dve.wait_ge(sem, count[0])
    return link


def stage_load(nc, m):
    loaded, made, centred = nc.semaphore("loaded"), nc.semaphore("made"), nc.semaphore("centred")
    with loaded as loaded, made as made, centred as centred, nc.Block() as block:
        loads = [
            (m.x.rearrange("p (t d) -> p t d", t=NT), m.ins["x"].rearrange("(t p) d -> p t d", p=P)),
            (m.z, m.ins["z"]), (m.src, m.ins["src"]), (m.dst_i, m.ins["dst"]), (m.base_i[0:1], m.ins["base"]),
            (m.base_bc, m.ins["base"].broadcast_to([P, m.ins["base"].shape[1]])),
            (m.ea, m.ins["ea"]),
            (m.wkv.rearrange("p (k f) -> p k f", k=2), m.ins["wkv"].rearrange("(k p) f -> p k f", p=P)),
            (m.wq.rearrange("p (k f) -> p k f", k=4), m.ins["wq"].rearrange("(k p) f -> p k f", p=P)),
            (m.wout.rearrange("p (k f) -> p k f", k=4), m.ins["wout"].rearrange("(k p) f -> p k f", p=P)),
            (m.wlin1.rearrange("p (k f) -> p k f", k=2), m.ins["wlin1"].rearrange("(k p) f -> p k f", p=P)),
            (m.wsc.rearrange("p (k f) -> p k f", k=2), m.ins["wsc"].rearrange("(k p) f -> p k f", p=P)),
            (m.wlin2.rearrange("p (k f) -> p k f", k=2), m.ins["wlin2"].rearrange("(k p) f -> p k f", p=P)),
            (m.bout, m.ins["bout"].broadcast_to([P, m.ins["bout"].shape[1]])),
            (m.fc0, m.ins["fc0"]), (m.fc1, m.ins["fc1"]),
            (m.gate.rearrange("p (k f) -> p k f", k=2), m.ins["gate"].rearrange("(k p) f -> p k f", p=P)),
            (m.gateb, m.ins["gateb"].broadcast_to([P, m.ins["gateb"].shape[1]])),
        ]

        @block.sync
        def _(sp):
            for dst, src in loads:
                sp.dma_start(dst, src).then_inc(loaded, 16)

        @block.gpsimd
        def _(pool):
            nc.gpsimd.memset(m.ident, 0.0).then_inc(made, 1)
            nc.gpsimd.memset(m.upper, 1.0).then_inc(made, 1)
            nc.gpsimd.memset(m.ones, 1.0).then_inc(made, 1)
            nc.gpsimd.memset(m.zeros, 0.0).then_inc(made, 1)
            nc.gpsimd.memset(m.eps, EPS).then_inc(made, 1)
            nc.gpsimd.iota(m.iota_i, pattern=[[1, P]], base=0, channel_multiplier=0).then_inc(made, 1)
            nc.gpsimd.iota(m.node_i, pattern=[[P, NT]], base=0, channel_multiplier=1).then_inc(made, 1)
            nc.gpsimd.iota(m.steps_i, pattern=[[P, NT]], base=0, channel_multiplier=0).then_inc(made, 1)
            nc.gpsimd.memset(m.ysum, 0.0).then_inc(made, 1)
            pool.wait_ge(made, 2)
            nc.gpsimd.affine_select(out=m.ident, in_=m.ident, compare_op=ALU.not_equal, fill=1.0, base=0,
                                    pattern=[[-1, P]], channel_multiplier=1).then_inc(made, 1)
            nc.gpsimd.affine_select(out=m.upper, in_=m.upper, compare_op=ALU.is_gt, fill=0.0, base=0,
                                    pattern=[[1, P]], channel_multiplier=-1).then_inc(made, 1)
            pool.wait_ge(made, 11)

        @block.vector
        def _(dve):
            link = chain(dve, centred)
            dve.wait_ge(loaded, 16 * len(loads))
            dve.wait_ge(made, 8)
            w = m.wkv.rearrange("p (g d) -> p g d", d=DH)
            link(nc.vector.tensor_reduce(m.wmean, w, AX, ALU.add))
            link(nc.vector.tensor_scalar(m.wmean, m.wmean, 1.0 / DH, None, ALU.mult))
            nc.vector.tensor_tensor(w, w, m.wmean.unsqueeze(2).broadcast_to([P, 4 * HEADS, DH]), ALU.subtract)
            nc.vector.tensor_scalar(m.wsc, m.wsc, SC_SCALE, None, ALU.mult)
            link(nc.vector.tensor_scalar(m.wlin2, m.wlin2, LIN2_SCALE, None, ALU.mult))
            d_rows = m.wlin2[MUL:P, 0:MUL]
            nc.vector.tensor_scalar(d_rows, d_rows, 1.0 / np.sqrt(3.0), None, ALU.mult)
            nc.vector.tensor_copy(m.iota, m.iota_i)
            nc.vector.tensor_copy(m.steps_of, m.steps_i)
            link(nc.vector.tensor_copy(m.node_f, m.node_i))
            nc.vector.tensor_scalar(m.valid, m.node_f, float(N), None, ALU.is_lt)
            nc.vector.tensor_copy(m.base_f, m.base_bc)
            link(nc.vector.tensor_copy(m.rel, m.dst_i))
            rel = m.rel.rearrange("p (g k) -> p g k", k=GT)
            link(nc.vector.tensor_tensor(rel, rel, m.base_f.unsqueeze(2).broadcast_to([P, NG, GT]), ALU.subtract))


def stage_attention(nc, m, s):
    x = m.x.rearrange("p (t d) -> p t d", t=NT)
    xnt = m.xnt.rearrange("p (k n) -> p k n", k=2)
    st = m.st.rearrange("p (t s) -> p t s", t=NT)
    pt, pk, pv, ph, pd = m.bank[0:2], m.bank[2:4], m.bank[4:6], m.bank[6], m.bank[7]
    with nc.Block() as block:
        @block.sync
        def _(sp):
            for j in range(0, NBLK, 8):
                sp.dma_start(m.slots_in[j * P:(j + 8) * P, :].rearrange("(p r) d -> p (r d)", p=P),
                             m.zeros).then_inc(m.zeroed, 16)

            def store_h(t, b):
                sp.wait_ge(s["h_ready"], t + 1)
                sp.dma_start(m.h_table[ds(t * P, P), :], m.h_out[b]).then_inc(s["h_stored"][b], 16)
            steps(sp, NT, store_h)
            sp.wait_ge(s["h_stored"][0], 16 * (NT - NT // 2))
            sp.wait_ge(s["h_stored"][1], 16 * (NT // 2))

        @block.vector
        def _(dve):
            link = chain(dve, s["dve_chain"])
            with dve.Fori(0, NT) as t:
                nc.vector.bn_stats(st[:, ds(t, 1), :].rearrange("p a s -> p (a s)"),
                                   x[:, ds(t, 1), :].rearrange("p a d -> p (a d)")).then_inc(s["bn_done"], 1)
            dve.wait_ge(s["bn_done"], NT)
            row_stats(dve, link, m, st, s)

            def scaled_values(t, b):
                dve.wait_ge(s["squared"], t + 1)
                nc.vector.tensor_reduce(m.sumsq[b], m.sq[b].rearrange("p (g d) -> p g d", d=DH), AX,
                                        ALU.add).then_inc(s["sumsq_ready"], 1)
                dve.wait_ge(s["stds_ready"], t + 1)
                nc.vector.tensor_tensor(m.rk, m.stds[b][:, 0:HEADS], m.stds[b][:, HEADS:2 * HEADS], ALU.mult).then_inc(s["v_chain"], 1)
                dve.wait_ge(s["v_chain"], 2 * t + 1)
                nc.vector.reciprocal(m.rk, m.rk).then_inc(s["v_chain"], 1)
                dve.wait_ge(s["v_chain"], 2 * t + 2)
                if from_step(t, 2):
                    dve.wait_ge(s["dots_done"], t - 1)
                nc.vector.tensor_tensor(m.vs[b].rearrange("p (g d) -> p g d", d=DH),
                                        pv[b][:].rearrange("p (g d) -> p g d", d=DH),
                                        m.rk.unsqueeze(2).broadcast_to([P, HEADS, DH]), ALU.mult).then_inc(s["vs_ready"], 1)

            def copy_xnt(t, b):
                dve.wait_ge(s["turned"], t + 1)
                if from_step(t, 2):
                    dve.wait_ge(s["kv_done"], t - 1)
                    dve.wait_ge(s["xnt_kept"], t - 1)
                nc.vector.tensor_copy(m.xnt_t[b], pt[b][:, 0:2 * P]).then_inc(s["xnt_ready"], 1)

            copy_xnt(0, 0)

            def step(t, b):
                if not isinstance(t, int) or t < NT - 1:
                    copy_xnt(t + 1, 1 - b)
                scaled_values(t, b)
            steps(dve, NT, step)

        @block.scalar
        def _(act):
            row_std(act, m, s)

            def normalise(t, b):
                if from_step(t, 2):
                    act.wait_ge(s["turned"], t - 1)
                nc.scalar.activation(m.xn[b], x[:, ds(t, 1), :].rearrange("p a d -> p (a d)"), ACT.Identity,
                                     bias=m.shift[:, ds(t, 1)], scale=m.rstd[:, ds(t, 1)]).then_inc(s["xn_ready"], 1)
            normalise(0, 0)

            def step(t, b):
                if not isinstance(t, int) or t < NT - 1:
                    normalise(t + 1, 1 - b)
                act.wait_ge(s["kv_done"], t + 1)
                if from_step(t, 2):
                    act.wait_ge(s["vs_ready"], t - 1)
                nc.scalar.activation(m.sq[b][:, 0:INNER], pk[b][:], ACT.Square)
                nc.scalar.activation(m.sq[b][:, INNER:2 * INNER], pv[b][:], ACT.Square).then_inc(s["squared"], 1)
                if from_step(t, 2):
                    act.wait_ge(s["dots_done"], t - 1)
                nc.scalar.copy(m.kc[b], pk[b][:]).then_inc(s["k_ready"], 1)
                act.wait_ge(s["sumsq_ready"], t + 1)
                nc.scalar.activation(m.stds[b], m.sumsq[b], ACT.Sqrt, bias=m.eps, scale=1.0 / DH).then_inc(s["stds_ready"], 1)
                act.wait_ge(s["h_done"], t + 1)
                if from_step(t, 2):
                    act.wait_ge(s["h_stored"][b], 8 * (t - b))
                nc.scalar.activation(m.h_out[b], ph[:, 0:D], ACT.Copy, scale=m.z[:, ds(t, 1)]).then_inc(s["h_ready"], 1)
            steps(act, NT, step)

        @block.gpsimd
        def _(pool):
            def step(t, b):
                pool.wait_ge(s["xnt_ready"], t + 1)
                nc.gpsimd.tensor_copy(xnt[:, :, ds(t * P, P)], m.xnt_t[b].rearrange("p (k n) -> p k n", k=2)).then_inc(s["xnt_kept"], 1)
                pool.wait_ge(s["xn_ready"], t + 1)
                xt = x[:, ds(t, 1), :].rearrange("p a d -> p (a d)")
                nc.gpsimd.tensor_tensor(xt, xt, m.bout, ALU.add)
            steps(pool, NT, step)

        @block.tensor
        def _(pe):
            wkv = m.wkv.rearrange("p (k f) -> p k f", k=2)
            wl = m.wlin1.rearrange("p (k f) -> p k f", k=2)

            def turn(t, b):
                pe.wait_ge(s["xn_ready"], t + 1)
                if from_step(t, 2):
                    pe.wait_ge(s["xnt_ready"], t - 1)
                nc.tensor.transpose(pt[b][:, 0:P], m.xn[b][:, 0:P], m.ident)
                nc.tensor.transpose(pt[b][:, P:2 * P], m.xn[b][:, P:2 * P], m.ident).then_inc(s["turned"], 1)

            def keys_values(t, b):
                pe.wait_ge(s["xnt_ready"], t + 1)
                if from_step(t, 2):
                    pe.wait_ge(s["k_ready"], t - 1)
                    pe.wait_ge(s["vs_ready"], t - 1)
                for k in range(2):
                    nc.tensor.matmul(pk[b][:], m.xnt_t[b][:, k * P:(k + 1) * P], wkv[:, k, 0:INNER], start=k == 0, stop=k == 1)
                for k in range(2):
                    last = nc.tensor.matmul(pv[b][:], m.xnt_t[b][:, k * P:(k + 1) * P], wkv[:, k, INNER:2 * INNER],
                                            start=k == 0, stop=k == 1)
                last.then_inc(s["kv_done"], 1)
                if from_step(t, 1):
                    pe.wait_ge(s["h_ready"], t)
                for k in range(2):
                    last = nc.tensor.matmul(ph[:, k * P:(k + 1) * P], m.xnt_t[b][:, k * P:(k + 1) * P], wl[:, k, :],
                                            start=True, stop=True)
                last.then_inc(s["h_done"], 1)

            def dots(t, b, final=False):
                pe.wait_ge(s["vs_ready"], t + 1)
                pe.wait_ge(s["k_ready"], t + 1)
                for p in range(4):
                    last = nc.tensor.matmul(pd[:, p * P:(p + 1) * P], m.vs[b][:, p * P:(p + 1) * P], m.kc[b][:, p * P:(p + 1) * P],
                                            start=isinstance(t, int) and t == 0 and p == 0, stop=final,
                                            skip_group_check=True)
                last.then_inc(s["dots_done"], 1)

            turn(0, 0)

            def step(t, b):
                if not isinstance(t, int) or t < NT - 1:
                    turn(t + 1, 1 - b)
                keys_values(t, b)
                if from_step(t, 1):
                    dots(t - 1, 1 - b)
            steps(pe, NT, step)
            dots(NT - 1, (NT - 1) % 2, True)


def stage_mix(nc, m, s):
    x = m.x.rearrange("p (t d) -> p t d", t=NT)
    xnt = m.xnt.rearrange("p (k n) -> p k n", k=2)
    pd, pg, pm = m.bank[7], m.bank[0:2], m.bank[2]
    mix = m.mix.rearrange("p (k f) -> p k f", k=2)
    wsc = m.wsc.rearrange("p (k f) -> p k f", k=2)
    px = m.bank[3:5]
    with nc.Block() as block:
        @block.vector
        def _(dve):
            nc.vector.memset(m.dots, 0.0).then_inc(s["cleared"], 1)
            dve.wait_ge(s["cleared"], 1)
            for hh in range(2):
                q = slice(hh * DH, (hh + 1) * DH)
                d = m.dots.rearrange("p (a d) -> p a d", a=4)[q, :, q]
                last = nc.vector.tensor_scalar(d, pd[:].rearrange("p (a d) -> p a d", a=4)[q, :, q], 1.0 / N, None, ALU.mult)
                last.then_inc(s["dots_ready"], 1)
            for a in range(2):
                dve.wait_ge(s["g_done"], a + 1)
                nc.vector.tensor_copy(m.g[:, a * 512:(a + 1) * 512], pg[a][:]).then_inc(s["g_ready"], 1)
            dve.wait_ge(s["m_done"], 1)
            nc.vector.tensor_copy(m.mix, pm[:]).then_inc(s["mix_ready"], 1)

            def step(t, b):
                xt = x[:, ds(t, 1), :].rearrange("p a d -> p (a d)")
                dve.wait_ge(s["mixed"], t + 1)
                nc.vector.tensor_tensor(xt, px[b][:, 0:D], xt, ALU.add).then_inc(s["x_mixed"], 1)
                dve.wait_ge(s["x_mixed"], t + 1)
                nc.vector.scalar_tensor_tensor(xt, px[b][:, D:2 * D], m.z[:, ds(t, 1)], xt, ALU.mult,
                                               ALU.add).then_inc(s["x_ready"], 1)
            steps(dve, NT, step)

        @block.scalar
        def _(act):
            def step(t, b):
                if from_step(t, 2):
                    act.wait_ge(s["mixed"], t - 1)
                nc.scalar.copy(m.xnt_t[b].rearrange("p (k n) -> p k n", k=2), xnt[:, :, ds(t * P, P)]).then_inc(s["staged"], 1)
            steps(act, NT, step)

        @block.tensor
        def _(pe):
            pe.wait_ge(s["dots_ready"], 2)
            for p in range(4):
                last = nc.tensor.matmul(pg[p // 2][:, (p % 2) * D:(p % 2 + 1) * D], m.dots[:, p * P:(p + 1) * P],
                                        m.wout[:, p * D:(p + 1) * D], start=True, stop=True)
                if p % 2:
                    last.then_inc(s["g_done"], 1)
            pe.wait_ge(s["g_ready"], 2)
            for c in range(2):
                for p in range(4):
                    last = nc.tensor.matmul(pm[:, c * D:(c + 1) * D], m.wq[:, p * D + c * P:p * D + (c + 1) * P],
                                            m.g[:, p * D:(p + 1) * D], start=p == 0, stop=p == 3)
            last.then_inc(s["m_done"], 1)
            pe.wait_ge(s["mix_ready"], 1)

            def step(t, b):
                pe.wait_ge(s["staged"], t + 1)
                if from_step(t, 2):
                    pe.wait_ge(s["x_ready"], t - 1)
                for k in range(2):
                    nc.tensor.matmul(px[b][:, 0:D], m.xnt_t[b][:, k * P:(k + 1) * P], mix[:, k, :], start=k == 0, stop=k == 1)
                for k in range(2):
                    last = nc.tensor.matmul(px[b][:, D + k * P:D + (k + 1) * P], m.xnt_t[b][:, k * P:(k + 1) * P], wsc[:, k, :],
                                            start=False, stop=True, skip_group_check=True)
                last.then_inc(s["mixed"], 1)
            steps(pe, NT, step)


PCOLS = 8 * MUL


EARLY = E - 4


def load_w1(sp, m, e):
    sp.dma_start(m.w1[:, e * 1024:(e + 2) * 1024].rearrange("p (e k f) -> p e k f", e=2, k=2),
                 m.ins["w1"][e:e + 2].rearrange("e (k p) f -> p e k f", p=P)).then_inc(m.w1_loaded, 16)


DVE_SEL = 2


def form_products(nc, prod, w, xs, h, s):
    w = w[:].rearrange("p (k q d) -> p k q d", k=2, q=4)
    xs = xs[:, 2 * h * D:2 * (h + 1) * D].rearrange("p (k q d) -> p k q d", k=2, q=4)
    pr = prod[:, 2 * h * PCOLS:2 * (h + 1) * PCOLS].rearrange("p (k q d) -> p k q d", k=2, q=8)
    nc.vector.tensor_tensor(pr[:, :, 0:2, :], w[:, :, 0:2, :], xs[:, :, 0:1, :].broadcast_to([P, 2, 2, MUL]), ALU.mult)
    for q in range(2):
        last = nc.vector.tensor_tensor(pr[:, :, 2 + q:8:2, :], w[:, :, 2 + q:3 + q, :].broadcast_to([P, 2, 3, MUL]),
                                       xs[:, :, 1:4, :], ALU.mult)
    last.then_inc(s["product_done"], 1)


def sum_tile(nc, seg, prod, sel, k, last_tile):
    wins = seg[:, 0:8 * WIN].rearrange("p (w n) -> p w n", w=8)
    sel = sel.rearrange("p (k c n) -> p k c n", k=GT, c=4)
    pr = prod[:, k * PCOLS:(k + 1) * PCOLS]
    nc.tensor.matmul(wins[:, 1:5, :], pr[:, 0:P], sel[:, k, :, :], start=k == 0, stop=last_tile, skip_group_check=True)
    for c in range(COMP):
        last = nc.tensor.matmul(wins[:, 0:6 + c:5 + c, :], pr[:, (c + 1) * P:(c + 2) * P], sel[:, k, c:4:3 - c, :],
                                start=False, stop=last_tile, skip_group_check=True)
    return last


def stage_edges(nc, m, s):
    pre, wp, seg = m.bank[0:2], [m.bank[2:4], m.bank[4:6]], m.bank[6:8]
    ysum = m.ysum.rearrange("p (q n) -> p q n", q=CH)
    with nc.Block() as block:
        @block.sync
        def _(sp):
            for e in range(0, EARLY, 2):
                load_w1(sp, m, e)

            def load_e8(g, q):
                b = q % 2
                if from_step(g, 2):
                    sp.wait_ge(s["pre_done"], g - 1)
                sp.dma_start(m.e8[b], m.ins["e8"][:, ds(g * 2 * P, 2 * P)]).then_inc(s["e8_loaded"][b], 16)
            steps_ring(sp, NG, load_e8)

        @block.gpsimd
        def _(pool):
            def gather(g, q):
                if from_step(g, RING):
                    pool.wait_ge(s["product_done"], 2 * (g - RING) + 2)
                pool.wait_ge(s["idx_ready"], g + 1)
                passed(pool, m)
                for k in range(GT):
                    nc.gpsimd.indirect_dma_start(
                        out=m.xs[q][:, k * D:(k + 1) * D], out_offset=None, in_=m.h_table,
                        in_offset=bass.IndirectOffsetOnAxis(ap=m.idx[q][:, k:k + 1], axis=0)).then_inc(s["xs_loaded"][q], 16)
            steps_ring(pool, NG, gather)

        @block.scalar
        def _(act):
            def hidden(g, q):
                b = q % 2
                act.wait_ge(s["pre_done"], g + 1)
                if from_step(g, 2):
                    act.wait_ge(s["w_done"], 2 * g - 2)
                nc.scalar.activation(m.hid[b], pre[b][:, 0:2 * P], ACT.Silu, scale=1.0 / np.sqrt(NB)).then_inc(s["hid_ready"], 1)

            def select(g, q, k):
                b = q % 2
                if k == DVE_SEL:
                    act.wait_ge(s["onehot_ready"], g + 1)
                    if from_step(g, 2):
                        act.wait_ge(s["seg_done"], g - 1)
                for c in range(4):
                    last = nc.scalar.activation(m.sel[b][:, (k * 4 + c) * WIN:(k * 4 + c + 1) * WIN],
                                                m.onehot[b][:, k * WIN:(k + 1) * WIN], ACT.Copy,
                                                scale=m.ea[:, ds(g * 4 * GT + 4 * k + c, 1)])
                if k == GT - 1:
                    last.then_inc(s["sel_scaled"], 1)

            def indices(g, q):
                if from_step(g, RING):
                    act.wait_ge(s["product_done"], 2 * (g - RING) + 2)
                nc.scalar.copy(m.idx[q], m.src[:, ds(g * GT, GT)]).then_inc(s["idx_ready"], 1)
            for g in range(RING - 1):
                indices(g, g)
            hidden(0, 0)
            hidden(1, 1)
            for k in range(DVE_SEL, GT):
                select(0, 0, k)

            def step(g, q):
                ahead = not isinstance(g, int) or g < NG - 1
                if not isinstance(g, int) or g < NG - 2:
                    hidden(g + 2, q + 2)
                if ahead:
                    for k in range(DVE_SEL, GT):
                        select(g + 1, q + 1, k)
                if not isinstance(g, int) or g < NG - RING + 1:
                    indices(g + RING - 1, (q - 1) % RING)
            steps_ring(act, NG, step)

        @block.vector
        def _(dve):
            def onehot(g, q):
                b = q % 2
                if from_step(g, 2):
                    dve.wait_ge(s["sel_scaled"], g - 1)
                nc.vector.tensor_tensor(
                    m.onehot[b].rearrange("p (k n) -> p k n", k=GT),
                    m.iota[:, 0:WIN].unsqueeze(1).broadcast_to([P, GT, WIN]),
                    m.rel[:, ds(g * GT, GT)].unsqueeze(2).broadcast_to([P, GT, WIN]), ALU.is_equal).then_inc(s["onehot_ready"], 1)

            def select(g, q):
                b = q % 2
                dve.wait_ge(s["onehot_ready"], g + 1)
                if from_step(g, 2):
                    dve.wait_ge(s["seg_done"], g - 1)
                nc.vector.tensor_tensor(
                    m.sel[b][:, 0:DVE_SEL * 4 * WIN].rearrange("p (k c n) -> p k c n", k=DVE_SEL, c=4),
                    m.onehot[b][:, 0:DVE_SEL * WIN].rearrange("p (k n) -> p k n", k=DVE_SEL).unsqueeze(2).broadcast_to([P, DVE_SEL, 4, WIN]),
                    m.ea[:, ds(g * 4 * GT, 4 * DVE_SEL)].rearrange("p (k c) -> p k c", k=DVE_SEL).unsqueeze(3).broadcast_to([P, DVE_SEL, 4, WIN]),
                    ALU.mult).then_inc(s["sel_ready"], 1)

            def products(g, q):
                b = q % 2
                dve.wait_ge(s["xs_loaded"][q], 16 * GT // RING * (g - q) + 16 * GT)
                if from_step(g, 2):
                    dve.wait_ge(s["seg_done"], g - 1)
                for h in range(2):
                    dve.wait_ge(s["w_done"], 2 * g + h + 1)
                    form_products(nc, m.prod[b], wp[b][h], m.xs[q], h, s)

            def add_window(g, q):
                b = q % 2
                base = dve.value_load(m.base_i[0:1, ds(g, 1)], min_val=0, max_val=NPAD - WIN)
                dve.wait_ge(s["seg_done"], g + 1)
                if from_step(g, 1):
                    dve.wait_ge(s["added"], 2 * g)
                wins = seg[b][:, 0:8 * WIN].rearrange("p (w n) -> p w n", w=8)
                for half, w in ((slice(0, MUL), slice(4, 8)), (slice(MUL, P), slice(0, 4))):
                    y = ysum[half, :, ds(base, WIN)]
                    nc.vector.tensor_tensor(y, wins[half, w, :], y, ALU.add).then_inc(s["added"], 1)

            onehot(0, 0)
            select(0, 0)

            def step(g, q):
                ahead = not isinstance(g, int) or g < NG - 1
                if ahead:
                    onehot(g + 1, q + 1)
                products(g, q)
                if ahead:
                    select(g + 1, q + 1)
                if from_step(g, 1):
                    add_window(g - 1, q + 1)
            steps_ring(dve, NG, step)
            add_window(NG - 1, NG - 1)

        @block.tensor
        def _(pe):
            def radial_in(g, q):
                b = q % 2
                pe.wait_ge(s["e8_loaded"][b], 8 * (g - b) + 16)
                if from_step(g, 2):
                    pe.wait_ge(s["hid_ready"], g - 1)
                nc.tensor.matmul(pre[b][:, 0:2 * P], m.fc0, m.e8[b], start=True, stop=True).then_inc(s["pre_done"], 1)

            def radial_out(g, q):
                b = q % 2
                pe.wait_ge(s["hid_ready"], g + 1)
                if from_step(g, 2):
                    pe.wait_ge(s["product_done"], 2 * g - 2)
                for k in range(GT):
                    h = slice((k // 2) * RN, (k // 2 + 1) * RN)
                    last = nc.tensor.matmul(wp[b][k // 2][:, (k % 2) * D:(k % 2 + 1) * D], m.hid[b][h, (k % 2) * P:(k % 2 + 1) * P],
                                            m.fc1[h, :], start=True, stop=True)
                    if k % 2:
                        last.then_inc(s["w_done"], 1)

            def segments(g, q):
                b = q % 2
                pe.wait_ge(s["sel_ready"], g + 1)
                pe.wait_ge(s["sel_scaled"], g + 1)
                if from_step(g, 2):
                    pe.wait_ge(s["added"], 2 * g - 2)
                for k in range(GT):
                    if k % 2 == 0:
                        pe.wait_ge(s["product_done"], 2 * g + k // 2 + 1)
                    last = sum_tile(nc, seg[b], m.prod[b], m.sel[b], k, k == GT - 1)
                last.then_inc(s["seg_done"], 1)

            radial_in(0, 0)
            radial_in(1, 1)
            radial_out(0, 0)

            def step(g, q):
                if not isinstance(g, int) or g < NG - 2:
                    radial_in(g + 2, q + 2)
                if not isinstance(g, int) or g < NG - 1:
                    radial_out(g + 1, q + 1)
                segments(g, q)
            steps_ring(pe, NG, step)


def steps_even(eng, n, step):
    assert n % 2 == 0
    step(0, 0)
    step(1, 1)
    with eng.Fori(1, n // 2 - 1) as i:
        step(i * 2, 0)
        step(i * 2 + 1, 1)
    step(n - 2, 0)
    step(n - 1, 1)


def stage_nodes(nc, m, s):
    x = m.x.rearrange("p (t d) -> p t d", t=NT)
    st = m.st.rearrange("p (t s) -> p t s", t=NT)
    ysum = m.ysum.rearrange("p (q n) -> p q n", q=CH)
    po, pt, pl = m.bank[0:2], m.bank[2:4], m.bank[4]
    gate = m.gate.rearrange("p (k f) -> p k f", k=2)
    with nc.Block() as block:
        @block.scalar
        def _(act):
            def stage(t, b):
                if from_step(t, 2):
                    act.wait_ge(s["out_done"], t - 1)
                nc.scalar.copy(m.y_t[b].rearrange("p (q n) -> p q n", q=CH), ysum[:, :, ds(t * P, P)]).then_inc(s["staged"], 1)
            steps(act, NT, stage)
            row_std(act, m, s)

            def normalise(t, b):
                if from_step(t, 2):
                    act.wait_ge(s["turned"], t - 1)
                nc.scalar.activation(m.yn[b], x[:, ds(t, 1), :].rearrange("p a d -> p (a d)"), ACT.Identity,
                                     bias=m.shift[:, ds(t, 1)], scale=m.rstd[:, ds(t, 1)]).then_inc(s["yn_ready"], 1)
            steps(act, NT, normalise)

        @block.tensor
        def _(pe):
            def second_map(t, b):
                pe.wait_ge(s["staged"], t + 1)
                if from_step(t, 2):
                    pe.wait_ge(s["x_ready"], t - 1)
                for q in range(CH):
                    w = m.wlin2[:, 0:MUL] if q == 0 else m.wlin2[:, MUL:P]
                    last = nc.tensor.matmul(po[b][:, q * MUL:(q + 1) * MUL], m.y_t[b][:, q * P:(q + 1) * P], w, start=True, stop=True)
                last.then_inc(s["out_done"], 1)
            steps(pe, NT, second_map)

            def turn(t, b):
                pe.wait_ge(s["yn_ready"], t + 1)
                if from_step(t, 2):
                    pe.wait_ge(s["ynt_ready"], t - 1)
                nc.tensor.transpose(pt[b][:, 0:P], m.yn[b][:, 0:P], m.ident)
                nc.tensor.transpose(pt[b][:, P:2 * P], m.yn[b][:, P:2 * P], m.ident).then_inc(s["turned"], 1)

            def logits(t, b):
                pe.wait_ge(s["ynt_ready"], t + 1)
                for k in range(2):
                    last = nc.tensor.matmul(pl[:, ds(t * E, E)], m.yn_t[b][:, k * P:(k + 1) * P], gate[:, k, :],
                                            start=k == 0, stop=k == 1)
                last.then_inc(s["logits_done"], 1)
            turn(0, 0)

            def step(t, b):
                if not isinstance(t, int) or t < NT - 1:
                    turn(t + 1, 1 - b)
                logits(t, b)
            steps(pe, NT, step)

        @block.vector
        def _(dve):
            link = chain(dve, s["dve_chain"])

            def residual(t, b):
                xt = x[:, ds(t, 1), :].rearrange("p a d -> p (a d)")
                dve.wait_ge(s["out_done"], t + 1)
                nc.vector.scalar_tensor_tensor(xt, po[b][:, 0:D], m.z[:, ds(t, 1)], xt, ALU.mult, ALU.add).then_inc(s["x_ready"], 1)
                dve.wait_ge(s["x_ready"], t + 1)
                nc.vector.bn_stats(st[:, ds(t, 1), :].rearrange("p a s -> p (a s)"), xt).then_inc(s["bn_done"], 1)
            steps(dve, NT, residual)
            dve.wait_ge(s["bn_done"], NT)
            row_stats(dve, link, m, st, s)

            def copy(t, b):
                dve.wait_ge(s["turned"], t + 1)
                if from_step(t, 2):
                    dve.wait_ge(s["logits_done"], t - 1)
                nc.vector.tensor_copy(m.yn_t[b], pt[b][:, 0:2 * P]).then_inc(s["ynt_ready"], 1)
            steps(dve, NT, copy)

            dve.wait_ge(s["logits_done"], NT)
            lg = m.logits.rearrange("p (t e) -> p t e", t=NT)
            link(nc.vector.tensor_tensor(lg, pl[:, 0:NT * E].rearrange("p (t e) -> p t e", t=NT),
                                         m.gateb.unsqueeze(1).broadcast_to([P, NT, E]), ALU.add))


def stage_route(nc, m, s):
    lg = m.logits.rearrange("p (t e) -> p t e", t=NT)
    ohs = [v.rearrange("p (t e) -> p t e", t=NT) for v in m.oh]
    both = m.both.rearrange("p (t e) -> p t e", t=NT)
    pos = m.pos.rearrange("p (t e) -> p t e", t=NT)
    tot = m.tot.rearrange("p (t e) -> p t e", t=NT)
    top = m.top.rearrange("p (t j) -> p t j", t=NT)
    topi = m.topi.rearrange("p (t j) -> p t j", t=NT)
    ppre, ptot = m.bank[0], m.bank[1]
    iota_e = m.iota[:, 0:E].unsqueeze(1).broadcast_to([P, NT, E])
    with nc.Block() as block:
        @block.sync
        def _(sp):
            for e in range(EARLY, E, 2):
                load_w1(sp, m, e)
            for e in range(0, E, 2):
                sp.dma_start(m.w2[:, e * 1024:(e + 2) * 1024].rearrange("p (e k f) -> p e k f", e=2, k=4),
                             m.ins["w2"][e:e + 2].rearrange("e (k p) f -> p e k f", p=P)).then_inc(m.w2_loaded, 16)
            sp.dma_start(m.b1, m.ins["b1"]).then_inc(m.w2_loaded, 16)
            sp.dma_start(m.b2, m.ins["b2"].broadcast_to([P, m.ins["b2"].shape[1]])).then_inc(m.w2_loaded, 16)
            sp.dma_start(m.gamma, m.ins["gamma"].broadcast_to([P, m.ins["gamma"].shape[1]])).then_inc(m.w2_loaded, 16)
            sp.dma_start(m.beta, m.ins["beta"].broadcast_to([P, m.ins["beta"].shape[1]])).then_inc(m.w2_loaded, 16)

        @block.scalar
        def _(act):
            act.wait_ge(s["gap_ready"], 1)
            nc.scalar.activation(m.gw[1], m.gap, ACT.Exp).then_inc(s["exp_done"], 1)

        @block.tensor
        def _(pe):
            pe.wait_ge(s["both_ready"], 1)
            nc.tensor.matmul(ppre[:, 0:NT * E], m.upper, m.both, start=True, stop=True)
            nc.tensor.matmul(ptot[:, 0:NT * E], m.ones, m.both, start=True, stop=True).then_inc(s["counted"], 1)

        @block.vector
        def _(dve):
            link = chain(dve, s["dve_chain"])
            for t in range(NT):
                last = nc.vector.max(top[:, t, :], lg[:, t, :])
            link(last)
            for t in range(NT):
                last = nc.vector.max_index(topi[:, t, :], top[:, t, :], lg[:, t, :])
            nc.vector.tensor_tensor(m.gap, top[:, :, 1], top[:, :, 0], ALU.subtract).then_inc(s["gap_ready"], 1)
            link(last)
            for k in range(2):
                link(nc.vector.tensor_copy(m.tmp_a, topi[:, :, k]))
                link(nc.vector.tensor_tensor(ohs[k], iota_e, m.tmp_a.unsqueeze(2).broadcast_to([P, NT, E]), ALU.is_equal))
                link(nc.vector.tensor_tensor(ohs[k], ohs[k], m.valid.unsqueeze(2).broadcast_to([P, NT, E]), ALU.mult))
            nc.vector.tensor_tensor(both, ohs[0], ohs[1], ALU.add).then_inc(s["both_ready"], 1)
            dve.wait_ge(s["exp_done"], 1)
            link(nc.vector.tensor_scalar(m.tmp_a, m.gw[1], 1.0, None, ALU.add))
            link(nc.vector.reciprocal(m.gw[0], m.tmp_a))
            link(nc.vector.tensor_tensor(m.gw[1], m.gw[1], m.gw[0], ALU.mult))
            dve.wait_ge(s["counted"], 1)
            link(nc.vector.tensor_copy(m.tot, ptot[:, 0:NT * E]))
            for t in range(1, NT):
                link(nc.vector.tensor_tensor(tot[:, t, :], tot[:, t, :], tot[:, t - 1, :], ALU.add))
            more = m.more.rearrange("p (e j) -> p e j", e=E)
            link(nc.vector.tensor_tensor(more, tot[:, NT - 1, :].unsqueeze(2).broadcast_to([P, E, NT]),
                                         m.steps_of.unsqueeze(1).broadcast_to([P, E, NT]), ALU.is_gt))
            link(nc.vector.tensor_reduce(m.nblk, more, AX, ALU.add))
            link(nc.vector.tensor_tensor_scan(m.blk_end, m.ones[:, 0:E], m.nblk, 0.0, ALU.mult, ALU.add))
            link(nc.vector.tensor_tensor(m.nblk, m.blk_end, m.nblk, ALU.subtract))
            link(nc.vector.tensor_scalar(m.nblk, m.nblk, float(P), None, ALU.mult))
            link(nc.vector.tensor_tensor(pos, ppre[:, 0:NT * E].rearrange("p (t e) -> p t e", t=NT),
                                         m.nblk.unsqueeze(1).broadcast_to([P, NT, E]), ALU.add))
            link(nc.vector.tensor_tensor(pos[:, 1:NT, :], pos[:, 1:NT, :], tot[:, 0:NT - 1, :], ALU.add))
            link(nc.vector.tensor_scalar(m.gap, m.valid, -float(FAR_SLOT), float(FAR_SLOT), ALU.mult, ALU.add))
            for k in range(2):
                link(nc.vector.tensor_tensor(ohs[k], ohs[k], pos, ALU.mult))
                link(nc.vector.tensor_reduce(m.tmp_a, ohs[k], AX, ALU.add))
                link(nc.vector.tensor_tensor(m.tmp_a, m.tmp_a, m.gap, ALU.add))
                link(nc.vector.tensor_copy(m.slot[:, :, k], m.tmp_a))
            before = m.before.rearrange("p (j e) -> p j e", j=NBLK)
            link(nc.vector.tensor_tensor(before, m.blk_end.unsqueeze(1).broadcast_to([P, NBLK, E]),
                                         m.iota[:, 0:NBLK].unsqueeze(2).broadcast_to([P, NBLK, E]), ALU.is_le))
            link(nc.vector.tensor_reduce(m.blk_f, before, AX, ALU.add))
            link(nc.vector.tensor_scalar(m.blk_f, m.blk_f, float(E - 1), None, ALU.min))
            link(nc.vector.tensor_copy(m.blk_expert, m.blk_f))


def stage_dispatch(nc, m, s):
    x = m.x.rearrange("p (t d) -> p t d", t=NT)
    with nc.Block() as block:
        @block.scalar
        def _(act):
            def step(t, b):
                if from_step(t, 2):
                    act.wait_ge(s["sent"][b], 16 * (t - b))
                nc.scalar.activation(m.yn[b], x[:, ds(t, 1), :].rearrange("p a d -> p (a d)"), ACT.Identity,
                                     bias=m.shift[:, ds(t, 1)], scale=m.rstd[:, ds(t, 1)]).then_inc(s["yn_ready"], 1)
            steps(act, NT, step)

        @block.gpsimd
        def _(pool):
            pool.wait_ge(m.zeroed, 16 * (NBLK // 8))

            def step(t, b):
                if from_step(t, 2):
                    pool.wait_ge(s["sent"][b], 16 * (t - b))
                nc.gpsimd.tensor_copy(m.slot_t[b], m.slot[:, ds(t, 1), :].rearrange("p a k -> p (a k)")).then_inc(s["idx_ready"], 1)
                pool.wait_ge(s["idx_ready"], t + 1)
                pool.wait_ge(s["yn_ready"], t + 1)
                passed(pool, m)
                for k in range(2):
                    nc.gpsimd.indirect_dma_start(
                        out=m.slots_in, out_offset=bass.IndirectOffsetOnAxis(ap=m.slot_t[b][:, k:k + 1], axis=0),
                        in_=m.yn[b], in_offset=None, bounds_check=NSLOT - 1, oob_is_err=False).then_inc(s["sent"][b], 16)
            steps(pool, NT, step)
            pool.wait_ge(s["sent"][0], 32 * (NT - NT // 2))
            pool.wait_ge(s["sent"][1], 32 * (NT // 2))


def stage_experts(nc, m, s):
    px, ph, py = m.bank[0:2], m.bank[2:4], m.bank[6:8]
    with nc.Block() as block:
        @block.sync
        def _(sp):
            def load(j, q):
                if from_step(j, RING):
                    sp.wait_ge(s["x_turned"], j - RING + 1)
                sp.dma_start(m.xb[q], m.slots_in[ds(j * P, P), :]).then_inc(s["x_loaded"][q], 16)

            def store(j, b):
                sp.wait_ge(s["y_ready"], j + 1)
                sp.dma_start(m.slots_out[ds(j * P, P), :], m.yb[b]).then_inc(s["y_stored"][b], 16)
            for j in range(RING - 1):
                load(j, j)

            def step(j, q):
                if not isinstance(j, int) or j < NBLK - RING + 1:
                    load(j + RING - 1, (q - 1) % RING)
                store(j, q % 2)
            steps_ring(sp, NBLK, step)
            sp.wait_ge(s["y_stored"][0], 8 * NBLK)
            sp.wait_ge(s["y_stored"][1], 8 * NBLK)

        @block.tensor
        def _(pe):
            pe.wait_ge(m.w1_loaded, 16 * (E // 2))
            pe.wait_ge(m.w2_loaded, 16 * (E // 2 + 4))

            def turn_x(j, q):
                b = q % 2
                pe.wait_ge(s["x_loaded"][q], 16 // RING * (j - q) + 16)
                if from_step(j, 2):
                    pe.wait_ge(s["xt_ready"], j - 1)
                nc.tensor.transpose(px[b][:, 0:P], m.xb[q][:, 0:P], m.ident)
                nc.tensor.transpose(px[b][:, P:2 * P], m.xb[q][:, P:2 * P], m.ident).then_inc(s["x_turned"], 1)

            def first(j, b):
                pe.wait_ge(s["xt_ready"], j + 1)
                pe.wait_ge(s["w1_staged"], j + 1)
                if from_step(j, 2):
                    pe.wait_ge(s["ht_ready"], j - 1)
                for f in range(4):
                    for k in range(2):
                        last = nc.tensor.matmul(ph[b][:, f * P:(f + 1) * P], m.w1_t[b][:, k * FF + f * P:k * FF + (f + 1) * P],
                                                m.xbt[b][:, k * P:(k + 1) * P], start=k == 0, stop=k == 1)
                last.then_inc(s["h_done"], 1)

            def second(j, b):
                e = pe.value_load(m.blk_expert[0:1, ds(j, 1)], min_val=0, max_val=E - 1)
                pe.wait_ge(s["ht_ready"], j + 1)
                if from_step(j, 2):
                    pe.wait_ge(s["y_ready"], j - 1)
                for k in range(4):
                    last = nc.tensor.matmul(py[b][:, 0:D], m.hbt[b][:, k * P:(k + 1) * P], m.w2[:, ds(e * 1024 + k * D, D)],
                                            start=k == 0, stop=k == 3)
                last.then_inc(s["y_done"], 1)

            turn_x(0, 0)
            turn_x(1, 1)
            first(0, 0)

            def step(j, q):
                b = q % 2
                if not isinstance(j, int) or j < NBLK - 2:
                    turn_x(j + 2, (q + 2) % RING)
                if not isinstance(j, int) or j < NBLK - 1:
                    first(j + 1, 1 - b)
                second(j, b)
            steps_ring(pe, NBLK, step)

        @block.scalar
        def _(act):
            act.wait_ge(m.w2_loaded, 16 * (E // 2 + 4))

            def copy_xt(j, b):
                act.wait_ge(s["x_turned"], j + 1)
                if from_step(j, 2):
                    act.wait_ge(s["h_done"], j - 1)
                nc.scalar.copy(m.xbt[b], px[b][:, 0:2 * P]).then_inc(s["xt_ready"], 1)

            def relu(j, b):
                e = act.value_load(m.blk_expert[0:1, ds(j, 1)], min_val=0, max_val=E - 1)
                act.wait_ge(s["h_done"], j + 1)
                if from_step(j, 2):
                    act.wait_ge(s["y_done"], j - 1)
                for k in range(4):
                    last = nc.scalar.activation(m.hbt[b][:, k * P:(k + 1) * P], ph[b][:, k * P:(k + 1) * P], ACT.Relu,
                                                bias=m.b1[:, ds(e * 4 + k, 1)])
                last.then_inc(s["ht_ready"], 1)
            copy_xt(0, 0)
            copy_xt(1, 1)

            def step(j, b):
                relu(j, b)
                if not isinstance(j, int) or j < NBLK - 2:
                    copy_xt(j + 2, b)
            steps_even(act, NBLK, step)

        @block.vector
        def _(dve):
            dve.wait_ge(m.w1_loaded, 16 * (E // 2))
            dve.wait_ge(m.w2_loaded, 16 * (E // 2 + 4))

            def stage_w1(j, b):
                e = dve.value_load(m.blk_expert[0:1, ds(j, 1)], min_val=0, max_val=E - 1)
                if from_step(j, 2):
                    dve.wait_ge(s["h_done"], j - 1)
                nc.vector.tensor_copy(m.w1_t[b], m.w1[:, ds(e * 1024, 1024)]).then_inc(s["w1_staged"], 1)

            def rows_out(j, b):
                e = dve.value_load(m.blk_expert[0:1, ds(j, 1)], min_val=0, max_val=E - 1)
                dve.wait_ge(s["y_done"], j + 1)
                if from_step(j, 2):
                    dve.wait_ge(s["y_stored"][b], 8 * (j - b))
                nc.vector.tensor_tensor(m.yb[b], py[b][:, 0:D], m.b2[:, ds(e * D, D)], ALU.add).then_inc(s["y_ready"], 1)
            stage_w1(0, 0)
            stage_w1(1, 1)

            def step(j, b):
                if not isinstance(j, int) or j < NBLK - 2:
                    stage_w1(j + 2, b)
                rows_out(j, b)
            steps_even(dve, NBLK, step)


def stage_combine(nc, m, s):
    x = m.x.rearrange("p (t d) -> p t d", t=NT)
    u = m.u.rearrange("p (t d) -> p t d", t=NT)
    st = m.st.rearrange("p (t s) -> p t s", t=NT)

    def row(v, t):
        return v[:, ds(t, 1), :].rearrange("p a d -> p (a d)")
    with nc.Block() as block:
        @block.gpsimd
        def _(pool):
            def fetch(t, q):
                if from_step(t, RING):
                    pool.wait_ge(s["summed"], t - RING + 1)
                nc.gpsimd.tensor_copy(m.slot_q[q], m.slot[:, ds(t, 1), :].rearrange("p a k -> p (a k)")).then_inc(s["idx_ready"], 1)
                pool.wait_ge(s["idx_ready"], t + 1)
                passed(pool, m)
                for k in range(2):
                    nc.gpsimd.indirect_dma_start(
                        out=m.got[q][k], out_offset=None, in_=m.slots_out,
                        in_offset=bass.IndirectOffsetOnAxis(ap=m.slot_q[q][:, k:k + 1], axis=0),
                        bounds_check=NSLOT - 1, oob_is_err=False).then_inc(s["got"][q], 16)
            pool.wait_ge(s["cleared"], 2 * RING)
            steps_tiles(pool, fetch)

        @block.scalar
        def _(act):
            def normalise(t, q):
                nc.scalar.activation(row(u, t), row(x, t), ACT.Identity,
                                     bias=m.shift[:, ds(t, 1)], scale=m.rstd[:, ds(t, 1)]).then_inc(s["yn_ready"], 1)
            steps_tiles(act, normalise)
            row_std(act, m, s)

            def norm_sum(t, q):
                nc.scalar.activation(row(u, t), row(u, t), ACT.Identity,
                                     bias=m.shift[:, ds(t, 1)], scale=m.rstd[:, ds(t, 1)]).then_inc(s["normed"], 1)
            steps_tiles(act, norm_sum)

        @block.vector
        def _(dve):
            for q in range(RING):
                for k in range(2):
                    nc.vector.memset(m.got[q][k], 0.0).then_inc(s["cleared"], 1)

            def sums(t, q):
                dve.wait_ge(s["got"][q], 32 // RING * (t - q) + 32)
                dve.wait_ge(s["yn_ready"], t + 1)
                nc.vector.scalar_tensor_tensor(row(u, t), m.got[q][0], m.gw[0][:, ds(t, 1)], row(u, t), ALU.mult,
                                               ALU.add).then_inc(s["one_in"], 1)
                nc.vector.tensor_tensor(row(x, t), row(x, t), m.beta, ALU.add).then_inc(s["x_beta"], 1)
                dve.wait_ge(s["one_in"], t + 1)
                nc.vector.scalar_tensor_tensor(row(u, t), m.got[q][1], m.gw[1][:, ds(t, 1)], row(u, t), ALU.mult,
                                               ALU.add).then_inc(s["summed"], 1)
                dve.wait_ge(s["summed"], t + 1)
                nc.vector.bn_stats(row(st, t), row(u, t)).then_inc(s["bn_done"], 1)
            steps_tiles(dve, sums)
            dve.wait_ge(s["bn_done"], NT)
            row_stats(dve, chain(dve, s["dve_chain"]), m, st, s)
            dve.wait_ge(s["x_beta"], NT)

            def finish(t, q):
                dve.wait_ge(s["normed"], t + 1)
                nc.vector.tensor_tensor(row(u, t), row(u, t), m.gamma, ALU.mult).then_inc(s["scaled"], 1)
                dve.wait_ge(s["scaled"], t + 1)
                nc.vector.tensor_tensor(row(x, t), row(u, t), row(x, t), ALU.add).then_inc(s["x_out"], 1)
            steps_tiles(dve, finish)

        @block.sync
        def _(sp):
            def step(t, q):
                sp.wait_ge(s["x_out"], t + 1)
                sp.dma_start(m.out[ds(t * P, P), :], row(x, t)).then_inc(s["stored"], 16)
            steps_tiles(sp, step)
            sp.wait_ge(s["stored"], 16 * NT)


def build(nc, m):
    m.nc = nc
    with ExitStack() as ctx:
        def sb(name, n, dt=F32):
            return ctx.enter_context(nc.sbuf_tensor(name, [P, n], dt))

        def sem(name):
            return ctx.enter_context(nc.semaphore(name))

        def sems(prefix, names, pairs=(), rings=()):
            found = {n: sem(f"{prefix}_{n}") for n in names.split()}
            found.update({n: [sem(f"{prefix}_{n}{b}") for b in range(2)] for n in pairs})
            found.update({n: [sem(f"{prefix}_{n}{q}") for q in range(RING)] for n in rings})
            return found

        m.bank = [ctx.enter_context(nc.psum_tensor(f"bank{i}", [P, 512], F32)) for i in range(8)]
        m.h_table = nc.dram_tensor("h_table", [NPAD, D], F32, kind="Internal").ap()
        m.slots_in = nc.dram_tensor("slots_in", [NSLOT, D], F32, kind="Internal").ap()
        m.slots_out = nc.dram_tensor("slots_out", [NSLOT, D], F32, kind="Internal").ap()

        m.x = sb("x", NT * D)[:]
        keep = Region(sb("keep", 128 * 3 + 6 * NT + NT + 5 * 128 + 32 + 16 + 4 * NT + 6 * NT + 64))
        m.ident, m.upper, m.ones = keep.take(P), keep.take(P), keep.take(P)
        m.st = keep.take(6 * NT)
        m.z = keep.take(NT)
        m.wlin2 = keep.take(P)
        m.gate, m.gateb = keep.take(2 * E), keep.take(E)
        m.rstd, m.shift, m.valid, m.node_f = keep.take(NT), keep.take(NT), keep.take(NT), keep.take(NT)
        m.tmp_a, m.tmp_b, m.gap = keep.take(NT), keep.take(NT), keep.take(NT)
        m.gw = [keep.take(NT), keep.take(NT)]
        m.steps_of, m.eps = keep.take(NT), keep.take(1)
        m.iota = sb("iota", P)[:]
        m.slot = sb("slot", NT * 2, I32)[:].rearrange("p (t k) -> p t k", k=2)
        m.slot_q = [sb(f"slot_q{q}", 2, I32)[:] for q in range(RING)]
        m.slot_t = [sb(f"slot_t{b}", 2, I32)[:] for b in range(2)]
        m.blk_expert = sb("blk_expert", NBLK, I32)[:]

        low = sb("low", E * 1024)[:]
        m.ysum, m.w2 = low[:, 0:CH * NPAD], low
        high = sb("high", E * 1024)
        m.w1 = high[:]
        r = Region(high)
        m.wkv, m.wq, m.wout = r.take(2 * 2 * INNER), r.take(4 * D), r.take(4 * D)
        m.wlin1, m.wsc, m.bout, m.zeros = r.take(2 * P), r.take(2 * P), r.take(D), r.take(8 * D)
        m.wmean = r.take(4 * HEADS)
        m.dots, m.g, m.mix = r.take(4 * P), r.take(4 * D), r.take(2 * D)
        m.sumsq, m.stds = ([r.take(2 * HEADS) for _ in range(2)] for _ in range(2))
        m.rk = r.take(HEADS)
        m.xn, m.xnt_t, m.h_out = ([r.take(D) for _ in range(2)] for _ in range(3))
        m.sq = [r.take(2 * INNER) for _ in range(2)]
        m.vs, m.kc = ([r.take(INNER) for _ in range(2)] for _ in range(2))
        m.iota_i, m.node_i, m.steps_i = (r.take(n).bitcast(I32) for n in (P, NT, NT))
        m.dst_i, m.base_bc, m.base_f = r.take(ET).bitcast(I32), r.take(NG).bitcast(I32), r.take(NG)

        mid = sb("mid", max(2 * GT * (PCOLS + 4 * WIN), 2 * NPAD))
        m.xnt = mid[:, 0:2 * NPAD]
        r = Region(mid)
        m.prod = [r.take(GT * PCOLS) for _ in range(2)]
        m.sel = [r.take(GT * 4 * WIN) for _ in range(2)]
        r = Region(mid)
        m.b2, m.b1 = r.take(E * D), r.take(E * 4)
        m.gamma, m.beta = r.take(D), r.take(D)

        edge = sb("edge", 5430)
        r = Region(edge)
        m.ea, m.src, m.rel = r.take(4 * ET), r.take(ET).bitcast(I32), r.take(ET)
        m.base_i = r.take(NG).bitcast(I32)
        m.fc0, m.fc1 = r.take(P)[0:2 * NB], r.take(D)
        m.e8 = [v[0:2 * NB] for v in (r.take(2 * P), r.take(2 * P))]
        m.hid = [r.take(2 * P) for _ in range(2)]
        m.onehot = [r.take(GT * WIN) for _ in range(2)]
        m.idx = [r.take(GT).bitcast(I32) for _ in range(RING)]
        r = Region(high)
        r.take(EARLY * 1024)
        m.xs = [r.take(GT * D) for _ in range(RING)]
        r = Region(high)
        r.take(EARLY * 1024)
        m.y_t = [r.take(CH * P) for _ in range(2)]
        r = Region(edge)
        m.yn, m.yn_t = ([r.take(D) for _ in range(2)] for _ in range(2))
        m.logits, m.both, m.pos, m.tot = (r.take(NT * E) for _ in range(4))
        m.oh = [r.take(NT * E) for _ in range(2)]
        m.top, m.topi = r.take(NT * 8), r.take(NT * 8).bitcast(U32)
        m.more, m.before = r.take(E * NT), r.take(NBLK * E)[:, 0:NBLK * E]
        r = Region(mid)
        r.take(E * D + E * 4 + 2 * D)
        m.nblk, m.blk_end, m.blk_f = r.take(E), r.take(E), r.take(NBLK)
        r = Region(edge)
        m.w1_t = [r.take(2 * FF) for _ in range(2)]
        m.xb = [r.take(D) for _ in range(RING)]
        m.xbt, m.yb = ([r.take(D) for _ in range(2)] for _ in range(2))
        m.hbt = [r.take(FF) for _ in range(2)]
        r = Region(edge)
        m.got = [[r.take(D) for _ in range(2)] for _ in range(RING)]
        m.u = low[:, 0:NT * D]

        m.passed = sem("passed")
        m.zeroed, m.w1_loaded, m.w2_loaded = sem("zeroed"), sem("w1_loaded"), sem("w2_loaded")
        stage_load(nc, m)
        s = sems("att", "dve_chain bn_done var_ready std_ready stats_ready squared sumsq_ready stds_ready v_chain dots_done vs_ready turned kv_done xnt_kept "
                 "xnt_ready xn_ready k_ready h_done h_ready", ["h_stored"])
        stage_attention(nc, m, s)
        stage_mix(nc, m, sems("mix", "cleared dots_ready g_done g_ready m_done mix_ready mixed x_mixed x_ready staged"))
        s = sems("edge", "pre_done product_done idx_ready onehot_ready seg_done sel_ready sel_scaled w_done hid_ready added",
                 ["e8_loaded"])
        s["xs_loaded"] = [sem(f"edge_xs{q}") for q in range(RING)]
        stage_edges(nc, m, s)
        stage_nodes(nc, m, sems("node", "out_done staged var_ready std_ready stats_ready turned yn_ready x_ready ynt_ready logits_done "
                                "dve_chain bn_done"))
        stage_route(nc, m, sems("route", "gap_ready exp_done both_ready counted dve_chain"))
        stage_dispatch(nc, m, sems("send", "yn_ready idx_ready", ["sent"]))
        stage_experts(nc, m, sems("moe", "x_turned y_ready xt_ready w1_staged h_done ht_ready y_done",
                                  ["y_stored"], ["x_loaded"]))
        stage_combine(nc, m, sems("comb", "summed idx_ready cleared normed scaled x_beta yn_ready one_in bn_done dve_chain "
                                  "var_ready std_ready stats_ready x_out stored", [], ["got"]))


def kernel(x, src, dst, edge_attr_4, edge_attr_8, node_vec1, L0_gnn_W_sc0, L0_gnn_W_sc1, L0_gnn_W_lin1_0,
           L0_gnn_W_lin1_1, L0_gnn_fc_w0, L0_gnn_fc_w1, L0_gnn_W_lin2_0, L0_gnn_W_lin2_1, L0_mix_Wqkv, L0_mix_Wout,
           L0_mix_bout, L0_ffn_gate_w, L0_ffn_gate_b, L0_ffn_w1, L0_ffn_b1, L0_ffn_w2, L0_ffn_b2, L0_ffn_gamma,
           L0_ffn_beta):
    from concourse import bacc
    from concourse.bass_utils import run_bass_kernel_spmd

    perm = np.concatenate([np.arange(MUL)] + [MUL + c + COMP * np.arange(MUL) for c in range(COMP)])
    back = np.argsort(perm)
    f = np.float32

    def padded(a, rows, fill=0):
        out = np.full((rows,) + a.shape[1:], fill, a.dtype)
        out[:a.shape[0]] = a
        return out

    def diagonal(a, b):
        out = np.zeros((P, P), f)
        out[:MUL, :MUL], out[MUL:, MUL:] = a, b
        return out

    x, src, dst, ea, e8, z = (np.asarray(v) for v in (x, src, dst, edge_attr_4, edge_attr_8, node_vec1))
    src_t = np.ascontiguousarray(padded(src, ET * P).reshape(ET, P).T)
    dst_p = padded(dst, ET * P, N - 1)
    wqkv = np.asarray(L0_mix_Wqkv)
    lin2_0, lin2_1 = np.asarray(L0_gnn_W_lin2_0), np.asarray(L0_gnn_W_lin2_1)
    fc0 = np.zeros((2 * NB, 2 * RN), f)
    fc0[:NB, :RN] = fc0[NB:, RN:] = np.asarray(L0_gnn_fc_w0)
    arrays = {
        "x": padded(x[:, perm], NPAD), "z": padded(z, NPAD).reshape(NT, P).T,
        "src": src_t, "dst": dst_p.reshape(ET, P).T, "base": dst_p[::GE].reshape(1, NG),
        "ea": padded(ea[:, [1, 2, 3, 0]], ET * P).reshape(ET, P, 4).transpose(1, 0, 2).reshape(P, ET * 4),
        "e8": padded(e8, ET * P).reshape(NG, 2, 2 * P, NB).transpose(1, 3, 0, 2).reshape(2 * NB, NG * 2 * P),
        "wkv": wqkv[INNER:].T[perm], "wq": wqkv[:INNER][:, perm], "wout": np.asarray(L0_mix_Wout).T[:, perm],
        "bout": np.asarray(L0_mix_bout)[perm].reshape(1, D),
        "wlin1": np.concatenate([diagonal(L0_gnn_W_lin1_0, L0_gnn_W_lin1_1), diagonal(L0_gnn_W_lin1_1, L0_gnn_W_lin1_1)]),
        "wsc": np.concatenate([diagonal(L0_gnn_W_sc0, L0_gnn_W_sc1), diagonal(L0_gnn_W_sc1, L0_gnn_W_sc1)]),
        "wlin2": np.concatenate([lin2_0, np.concatenate([lin2_1[MUL:], lin2_1[:MUL]])]),
        "fc0": fc0, "fc1": np.concatenate([np.asarray(L0_gnn_fc_w1)] * 2),
        "gate": np.asarray(L0_ffn_gate_w)[perm], "gateb": np.asarray(L0_ffn_gate_b).reshape(1, E),
        "w1": np.asarray(L0_ffn_w1)[:, perm], "w2": np.asarray(L0_ffn_w2)[:, :, perm],
        "b1": np.asarray(L0_ffn_b1).reshape(E, 4, P).transpose(2, 0, 1).reshape(P, E * 4),
        "b2": np.asarray(L0_ffn_b2)[:, perm].reshape(1, E * D),
        "gamma": np.asarray(L0_ffn_gamma)[perm].reshape(1, D), "beta": np.asarray(L0_ffn_beta)[perm].reshape(1, D),
    }
    nc = bacc.Bacc("TRN2", target_bir_lowering=False, num_devices=1)
    held, fed = {}, {}
    for name, a in arrays.items():
        a = np.ascontiguousarray(a)
        fed[f"in_{name}"] = a
        held[name] = nc.dram_tensor(f"in_{name}", a.shape, mybir.dt.from_np(a.dtype), kind="ExternalInput").ap()
    m = Memory()
    m.ins = held
    m.out = nc.dram_tensor("out", (NPAD, D), F32, kind="ExternalOutput").ap()
    build(nc, m)
    r = run_bass_kernel_spmd(nc, [fed], core_ids=[0])
    return r.results[0]["out"][:N, back]
```

```python
from contextlib import ExitStack

import numpy as np

import concourse.bass as bass
import concourse.mybir as mybir

P = 128
N, D = 3125, 256
MUL, COMP, NB, RN = 64, 3, 8, 64
HEADS, DH = 8, 64
INNER = HEADS * DH
FF, E = 512, 16
E_ALL = 53125
NT = -(-N // P)
NPAD = NT * P
GT = 4
GE = GT * P
NG = -(-E_ALL // GE)
ET = NG * GT
WIN = 48
FAR_WIN = 64
RING = 4
CH = 4
NBLK = (2 * N + E * (P - 1)) // P
CAP = (NT + 1) * P
SPARE = NBLK - 2 * N // P
NSLOT = E * CAP + SPARE * P
FAR_SLOT = 2 * NSLOT
CK = 5
EPS = 1e-5
C_S = float(np.float32(np.sin(np.pi / 8)))
C_X = float(np.float32(np.cos(np.pi / 8)))
SC_SCALE = C_S / np.sqrt(MUL)
LIN2_SCALE = C_X / np.sqrt(2 * MUL) / 4.0 / np.sqrt(MUL) / np.sqrt(RN)

F32 = mybir.dt.float32
I32 = mybir.dt.int32
U32 = mybir.dt.uint32
ALU = mybir.AluOpType
ACT = mybir.ActivationFunctionType
AX = mybir.AxisListType.X
ds = bass.ds


def from_step(t, k):
    return not isinstance(t, int) or t >= k


def steps(eng, n, step):
    step(0, 0)
    step(1, 1)
    with eng.Fori(1, n // 2) as i:
        step(i * 2, 0)
        step(i * 2 + 1, 1)
    if n % 2:
        step(n - 1, 0)


def steps_ahead(eng, n, step):
    step(0, 0)
    step(1, 1)
    with eng.Fori(1, n // 2 - 1) as i:
        step(i * 2, 0)
        step(i * 2 + 1, 1)
    for t in range(n // 2 * 2 - 2, n):
        step(t, t % 2)


def steps_ring(eng, n, step):
    assert n % RING == 0
    for g in range(RING):
        step(g, g)
    with eng.Fori(1, n // RING - 1) as i:
        for q in range(RING):
            step(i * RING + q, q)
    for q in range(RING):
        step(n - RING + q, q)


def steps_tiles(eng, step):
    for t in range(RING):
        step(t, t)
    with eng.Fori(1, NT // RING) as i:
        for q in range(RING):
            step(i * RING + q, q)
    for t in range(NT // RING * RING, NT):
        step(t, t % RING)


def passed(eng, m):
    eng.sem_inc(m.passed, 1)


class Memory:
    pass


class Region:

    def __init__(self, whole):
        self.whole, self.at, self.size = whole, 0, whole.shape[1]

    def take(self, n):
        assert self.at + n <= self.size, (self.at, n, self.size)
        self.at += n
        return self.whole[:, self.at - n:self.at]


def row_stats(dve, link, m, st, s, n=1):
    nc = m.nc
    even, odd, a, b = st[:, :, 1], st[:, :, 4], m.tmp_a, m.tmp_b
    link(nc.vector.tensor_tensor(a, even, odd, ALU.subtract))
    link(nc.vector.scalar_tensor_tensor(b, a, 0.25, a, ALU.mult, ALU.mult))
    link(nc.vector.tensor_tensor(a, st[:, :, 2], st[:, :, 5], ALU.add))
    nc.vector.scalar_tensor_tensor(b, a, 1.0 / D, b, ALU.mult, ALU.add).then_inc(s["var_ready"], 1)
    link(nc.vector.tensor_tensor(m.gap, even, odd, ALU.add))
    dve.wait_ge(s["std_ready"], n)
    if not isinstance(n, int):
        passed(dve, m)
    link(nc.vector.reciprocal(m.rstd, a))
    nc.vector.scalar_tensor_tensor(m.shift, m.gap, -0.5, m.rstd, ALU.mult, ALU.mult).then_inc(s["stats_ready"], 1)


def row_std(act, m, s, n=1):
    act.wait_ge(s["var_ready"], n)
    m.nc.scalar.activation(m.tmp_a, m.tmp_b, ACT.Sqrt, bias=m.eps).then_inc(s["std_ready"], 1)
    act.wait_ge(s["stats_ready"], n)


def chain(dve, sem):
    count = [0]

    def link(ins):
        count[0] += 1
        ins.then_inc(sem, 1)
        dve.wait_ge(sem, count[0])
    return link


def load_first(m):
    return [
        (m.wkv.rearrange("p (k f) -> p k f", k=2), m.ins["wkv"].rearrange("(k p) f -> p k f", p=P)),
        (m.wlin1.rearrange("p (k f) -> p k f", k=2), m.ins["wlin1"].rearrange("(k p) f -> p k f", p=P)),
        (m.z, m.ins["z"]),
        (m.bout, m.ins["bout"].broadcast_to([P, m.ins["bout"].shape[1]])),
    ]


def load_later(m):
    return [
        (m.wq.rearrange("p (k f) -> p k f", k=4), m.ins["wq"].rearrange("(k p) f -> p k f", p=P)),
        (m.wout.rearrange("p (k f) -> p k f", k=4), m.ins["wout"].rearrange("(k p) f -> p k f", p=P)),
        (m.wsc.rearrange("p (k f) -> p k f", k=2), m.ins["wsc"].rearrange("(k p) f -> p k f", p=P)),
        (m.wlin2.rearrange("p (k f) -> p k f", k=2), m.ins["wlin2"].rearrange("(k p) f -> p k f", p=P)),
        (m.src, m.ins["src"]), (m.dst_i, m.ins["dst"]), (m.base_i[0:1], m.ins["base"]),
        (m.base_bc, m.ins["base"].broadcast_to([P, m.ins["base"].shape[1]])),
        (m.ea, m.ins["ea"]), (m.fc0, m.ins["fc0"]), (m.fc1, m.ins["fc1"]),
        (m.gate.rearrange("p (k f) -> p k f", k=2), m.ins["gate"].rearrange("(k p) f -> p k f", p=P)),
        (m.gateb, m.ins["gateb"].broadcast_to([P, m.ins["gateb"].shape[1]])),
    ]


def stage_load(nc, m, s):
    first = load_first(m)
    x = m.x.rearrange("p (t d) -> p t d", t=NT)
    st = m.st.rearrange("p (t s) -> p t s", t=NT)
    with nc.Block() as block:
        @block.sync
        def _(sp):
            for k in range(NT // CK):
                tiles = slice(k * CK, (k + 1) * CK)
                sp.dma_start(x[:, tiles, :], m.ins["x"].rearrange("(t p) d -> p t d", p=P)[:, tiles, :]).then_inc(s["x_loaded"][k], 16)
            for i, (dst, src) in enumerate(first):
                sp.dma_start(dst, src).then_inc(s["wkv_loaded"] if i == 0 else s["loaded"], 16)
            for dst, src in load_later(m):
                sp.dma_start(dst, src).then_inc(m.later_loaded, 16)

        @block.gpsimd
        def _(pool):
            nc.gpsimd.memset(m.ident, 0.0).then_inc(s["made"], 1)
            nc.gpsimd.memset(m.upper, 1.0).then_inc(s["made"], 1)
            nc.gpsimd.memset(m.ones, 1.0).then_inc(s["made"], 1)
            nc.gpsimd.iota(m.iota_i, pattern=[[1, P]], base=0, channel_multiplier=0).then_inc(s["made"], 1)
            nc.gpsimd.iota(m.node_i, pattern=[[P, NT]], base=0, channel_multiplier=1).then_inc(s["made"], 1)
            nc.gpsimd.iota(m.steps_i, pattern=[[P, NT]], base=0, channel_multiplier=0).then_inc(s["made"], 1)
            pool.wait_ge(s["made"], 2)
            nc.gpsimd.affine_select(out=m.ident, in_=m.ident, compare_op=ALU.not_equal, fill=1.0, base=0,
                                    pattern=[[-1, P]], channel_multiplier=1).then_inc(s["made"], 1)
            nc.gpsimd.affine_select(out=m.upper, in_=m.upper, compare_op=ALU.is_gt, fill=0.0, base=0,
                                    pattern=[[1, P]], channel_multiplier=-1).then_inc(s["made"], 1)
            nc.gpsimd.memset(m.eps, EPS).then_inc(s["made"], 1)
            nc.gpsimd.memset(m.zeros, 0.0).then_inc(s["made"], 1)
            pool.wait_ge(s["made"], 10)

        @block.scalar
        def _(act):
            act.wait_ge(s["made"], 10)
            row_std(act, m, s)

        @block.vector
        def _(dve):
            link = chain(dve, s["dve_chain"])
            dve.wait_ge(s["made"], 6)
            nc.vector.tensor_copy(m.iota, m.iota_i)
            nc.vector.tensor_copy(m.steps_of, m.steps_i)
            link(nc.vector.tensor_copy(m.node_f, m.node_i))
            nc.vector.tensor_scalar(m.valid, m.node_f, float(N), None, ALU.is_lt)
            for t in range(NT):
                if t % CK == 0:
                    dve.wait_ge(s["x_loaded"][t // CK], 16)
                nc.vector.bn_stats(st[:, t, :], x[:, t, :]).then_inc(s["bn_done"], 1)
            dve.wait_ge(s["bn_done"], NT)
            row_stats(dve, link, m, st, s)
            dve.wait_ge(s["wkv_loaded"], 16)
            w = m.wkv.rearrange("p (g d) -> p g d", d=DH)
            link(nc.vector.tensor_reduce(m.wmean, w, AX, ALU.add))
            link(nc.vector.tensor_scalar(m.wmean, m.wmean, 1.0 / DH, None, ALU.mult))
            nc.vector.tensor_tensor(w, w, m.wmean.unsqueeze(2).broadcast_to([P, 4 * HEADS, DH]), ALU.subtract)
            dve.wait_ge(s["loaded"], 16 * (len(first) - 1))


def stage_attention(nc, m, s):
    x = m.x.rearrange("p (t d) -> p t d", t=NT)
    xnt = m.xnt.rearrange("p (k n) -> p k n", k=2)
    pt, pk, pv, ph, pd = m.bank[0:2], m.bank[2:4], m.bank[4:6], m.bank[6], m.bank[7]
    with nc.Block() as block:
        @block.sync
        def _(sp):
            for j in range(0, SPARE, 8):
                sp.dma_start(m.slots_in[E * CAP + j * P:E * CAP + (j + 8) * P, :].rearrange("(p r) d -> p (r d)", p=P),
                             m.zeros).then_inc(m.zeroed, 16)

            def store_h(t, b):
                sp.wait_ge(s["h_ready"], t + 1)
                sp.dma_start(m.h_table[ds(t * P, P), :], m.h_out[b]).then_inc(s["h_stored"][b], 16)
            steps(sp, NT, store_h)
            sp.wait_ge(s["h_stored"][0], 16 * (NT - NT // 2))
            sp.wait_ge(s["h_stored"][1], 16 * (NT // 2))

        @block.vector
        def _(dve):
            def scaled_values(t, b):
                dve.wait_ge(s["stds_ready"], t + 1)
                nc.vector.tensor_tensor(m.rk, m.stds[b][:, 0:HEADS], m.stds[b][:, HEADS:2 * HEADS], ALU.mult).then_inc(s["v_chain"], 1)
                dve.wait_ge(s["v_chain"], 2 * t + 1)
                nc.vector.reciprocal(m.rk, m.rk).then_inc(s["v_chain"], 1)
                dve.wait_ge(s["v_chain"], 2 * t + 2)
                if from_step(t, 2):
                    dve.wait_ge(s["dots_done"], t - 1)
                nc.vector.tensor_tensor(m.vs[b].rearrange("p (g d) -> p g d", d=DH),
                                        pv[b][:].rearrange("p (g d) -> p g d", d=DH),
                                        m.rk.unsqueeze(2).broadcast_to([P, HEADS, DH]), ALU.mult).then_inc(s["vs_ready"], 1)

            def copy_xnt(t, b):
                dve.wait_ge(s["turned"], t + 1)
                if from_step(t, 2):
                    dve.wait_ge(s["kv_done"], t - 1)
                    dve.wait_ge(s["xnt_kept"], t - 1)
                nc.vector.tensor_copy(m.xnt_t[b], pt[b][:, 0:2 * P]).then_inc(s["xnt_ready"], 1)

            copy_xnt(0, 0)
            copy_xnt(1, 1)

            def step(t, b):
                dve.wait_ge(s["squared"], t + 1)
                nc.vector.tensor_reduce(m.sumsq[b], m.sq[b].rearrange("p (g d) -> p g d", d=DH), AX,
                                        ALU.add).then_inc(s["sumsq_ready"], 1)
                if not isinstance(t, int) or t < NT - 2:
                    copy_xnt(t + 2, b)
                scaled_values(t, b)
            steps_ahead(dve, NT, step)

        @block.scalar
        def _(act):
            def normalise(t, b):
                if from_step(t, 2):
                    act.wait_ge(s["turned"], t - 1)
                nc.scalar.activation(m.xn[b], x[:, ds(t, 1), :].rearrange("p a d -> p (a d)"), ACT.Identity,
                                     bias=m.shift[:, ds(t, 1)], scale=m.rstd[:, ds(t, 1)]).then_inc(s["xn_ready"], 1)
            normalise(0, 0)
            normalise(1, 1)

            def step(t, b):
                if not isinstance(t, int) or t < NT - 2:
                    normalise(t + 2, b)
                act.wait_ge(s["kv_done"], t + 1)
                if from_step(t, 2):
                    act.wait_ge(s["vs_ready"], t - 1)
                nc.scalar.activation(m.sq[b][:, 0:INNER], pk[b][:], ACT.Square)
                nc.scalar.activation(m.sq[b][:, INNER:2 * INNER], pv[b][:], ACT.Square).then_inc(s["squared"], 1)
                if from_step(t, 2):
                    act.wait_ge(s["dots_done"], t - 1)
                nc.scalar.copy(m.kc[b], pk[b][:]).then_inc(s["k_ready"], 1)
                act.wait_ge(s["sumsq_ready"], t + 1)
                nc.scalar.activation(m.stds[b], m.sumsq[b], ACT.Sqrt, bias=m.eps, scale=1.0 / DH).then_inc(s["stds_ready"], 1)
                act.wait_ge(s["h_done"], t + 1)
                if from_step(t, 2):
                    act.wait_ge(s["h_stored"][b], 8 * (t - b))
                nc.scalar.activation(m.h_out[b], ph[:, 0:D], ACT.Copy, scale=m.z[:, ds(t, 1)]).then_inc(s["h_ready"], 1)
            steps_ahead(act, NT, step)

        @block.gpsimd
        def _(pool):
            def step(t, b):
                pool.wait_ge(s["xnt_ready"], t + 1)
                nc.gpsimd.tensor_copy(xnt[:, :, ds(t * P, P)], m.xnt_t[b].rearrange("p (k n) -> p k n", k=2)).then_inc(s["xnt_kept"], 1)
                pool.wait_ge(s["xn_ready"], t + 1)
                xt = x[:, ds(t, 1), :].rearrange("p a d -> p (a d)")
                nc.gpsimd.tensor_tensor(xt, xt, m.bout, ALU.add)
            nc.gpsimd.memset(m.ysum, 0.0)
            steps(pool, NT, step)
            pool.wait_ge(m.later_loaded, 16 * len(load_later(m)))
            nc.gpsimd.tensor_scalar(m.wsc, m.wsc, SC_SCALE, None, ALU.mult).then_inc(s["scaled"], 1)
            nc.gpsimd.tensor_scalar(m.wlin2, m.wlin2, LIN2_SCALE, None, ALU.mult).then_inc(s["scaled"], 1)
            nc.gpsimd.tensor_copy(m.base_f, m.base_bc).then_inc(s["scaled"], 1)
            nc.gpsimd.tensor_copy(m.rel, m.dst_i).then_inc(s["scaled"], 1)
            pool.wait_ge(s["scaled"], 4)
            rel = m.rel.rearrange("p (g k) -> p g k", k=GT)
            nc.gpsimd.tensor_tensor(rel, rel, m.base_f.unsqueeze(2).broadcast_to([P, NG, GT]), ALU.subtract).then_inc(s["scaled"], 1)
            pool.wait_ge(s["scaled"], 5)
            d_rows = m.wlin2[MUL:P, 0:MUL]
            nc.gpsimd.tensor_scalar(d_rows, d_rows, 1.0 / np.sqrt(3.0), None, ALU.mult)

        @block.tensor
        def _(pe):
            wkv = m.wkv.rearrange("p (k f) -> p k f", k=2)
            wl = m.wlin1.rearrange("p (k f) -> p k f", k=2)

            def turn(t, b):
                pe.wait_ge(s["xn_ready"], t + 1)
                if from_step(t, 2):
                    pe.wait_ge(s["xnt_ready"], t - 1)
                nc.tensor.transpose(pt[b][:, 0:P], m.xn[b][:, 0:P], m.ident)
                nc.tensor.transpose(pt[b][:, P:2 * P], m.xn[b][:, P:2 * P], m.ident).then_inc(s["turned"], 1)

            def keys_values(t, b):
                pe.wait_ge(s["xnt_ready"], t + 1)
                if from_step(t, 2):
                    pe.wait_ge(s["k_ready"], t - 1)
                    pe.wait_ge(s["vs_ready"], t - 1)
                for k in range(2):
                    nc.tensor.matmul(pk[b][:], m.xnt_t[b][:, k * P:(k + 1) * P], wkv[:, k, 0:INNER], start=k == 0, stop=k == 1)
                for k in range(2):
                    last = nc.tensor.matmul(pv[b][:], m.xnt_t[b][:, k * P:(k + 1) * P], wkv[:, k, INNER:2 * INNER],
                                            start=k == 0, stop=k == 1)
                last.then_inc(s["kv_done"], 1)
                if from_step(t, 1):
                    pe.wait_ge(s["h_ready"], t)
                for k in range(2):
                    last = nc.tensor.matmul(ph[:, k * P:(k + 1) * P], m.xnt_t[b][:, k * P:(k + 1) * P], wl[:, k, :],
                                            start=True, stop=True)
                last.then_inc(s["h_done"], 1)

            def dots(t, b, final=False):
                pe.wait_ge(s["vs_ready"], t + 1)
                pe.wait_ge(s["k_ready"], t + 1)
                for p in range(4):
                    last = nc.tensor.matmul(pd[:, p * P:(p + 1) * P], m.vs[b][:, p * P:(p + 1) * P], m.kc[b][:, p * P:(p + 1) * P],
                                            start=isinstance(t, int) and t == 0 and p == 0, stop=final,
                                            skip_group_check=True)
                last.then_inc(s["dots_done"], 1)

            turn(0, 0)
            turn(1, 1)

            def step(t, b):
                keys_values(t, b)
                if not isinstance(t, int) or t < NT - 2:
                    turn(t + 2, b)
                if from_step(t, 1):
                    dots(t - 1, 1 - b)
            steps_ahead(pe, NT, step)
            dots(NT - 1, (NT - 1) % 2, True)


def stage_mix(nc, m, s):
    x = m.x.rearrange("p (t d) -> p t d", t=NT)
    xnt = m.xnt.rearrange("p (k n) -> p k n", k=2)
    pd, pg, pm = m.bank[7], m.bank[0:2], m.bank[2]
    mix = m.mix.rearrange("p (k f) -> p k f", k=2)
    wsc = m.wsc.rearrange("p (k f) -> p k f", k=2)
    px, pf = [m.bank[3], m.bank[4], m.bank[6], m.bank[0]], m.bank[5]
    with nc.Block() as block:
        @block.vector
        def _(dve):
            nc.vector.memset(m.dots, 0.0).then_inc(s["cleared"], 1)
            dve.wait_ge(s["cleared"], 1)
            for hh in range(2):
                q = slice(hh * DH, (hh + 1) * DH)
                d = m.dots.rearrange("p (a d) -> p a d", a=4)[q, :, q]
                last = nc.vector.tensor_scalar(d, pd[:].rearrange("p (a d) -> p a d", a=4)[q, :, q], 1.0 / N, None, ALU.mult)
                last.then_inc(s["dots_ready"], 1)
            link = chain(dve, s["dve_chain"])
            nc.vector.tensor_scalar(m.far_a, m.rel, 0.0, None, ALU.is_lt)
            link(nc.vector.tensor_scalar(m.far_c, m.rel, float(WIN), None, ALU.is_ge))
            link(nc.vector.tensor_tensor(m.far_a, m.far_a, m.far_c, ALU.add))
            nc.vector.tensor_reduce(m.far_rows, m.far_a, AX, ALU.add).then_inc(s["far_ready"], 1)
            for a in range(2):
                dve.wait_ge(s["g_done"], a + 1)
                nc.vector.tensor_copy(m.g[:, a * 512:(a + 1) * 512], pg[a][:]).then_inc(s["g_ready"], 1)
            dve.wait_ge(s["m_done"], 1)
            nc.vector.tensor_copy(m.mix, pm[:]).then_inc(s["mix_ready"], 1)
            dve.wait_ge(s["far_summed"], 1)
            nc.vector.tensor_copy(m.far_flag, pf[:, 0:1])

            def row(t):
                return x[:, ds(t, 1), :].rearrange("p a d -> p (a d)")

            def add_mixed(t, q):
                dve.wait_ge(s["mixed"], t + 1)
                nc.vector.tensor_tensor(row(t), px[q][:, 0:D], row(t), ALU.add).then_inc(s["x_mixed"], 1)

            def add_own(t, q):
                dve.wait_ge(s["x_mixed"], t + 1)
                nc.vector.scalar_tensor_tensor(row(t), px[q][:, D:2 * D], m.z[:, ds(t, 1)], row(t), ALU.mult,
                                               ALU.add).then_inc(s["x_ready"], 1)
            add_mixed(0, 0)

            def step(t, q):
                if not isinstance(t, int) or t < NT - 1:
                    add_mixed(t + 1, (q + 1) % RING)
                add_own(t, q)
            steps_tiles(dve, step)

        @block.scalar
        def _(act):
            def step(t, b):
                if from_step(t, 2):
                    act.wait_ge(s["mixed"], t - 1)
                nc.scalar.copy(m.xnt_t[b].rearrange("p (k n) -> p k n", k=2), xnt[:, :, ds(t * P, P)]).then_inc(s["staged"], 1)
            steps(act, NT, step)

        @block.tensor
        def _(pe):
            pe.wait_ge(s["dots_ready"], 2)
            for p in range(4):
                last = nc.tensor.matmul(pg[p // 2][:, (p % 2) * D:(p % 2 + 1) * D], m.dots[:, p * P:(p + 1) * P],
                                        m.wout[:, p * D:(p + 1) * D], start=True, stop=True)
                if p % 2:
                    last.then_inc(s["g_done"], 1)
            pe.wait_ge(s["g_ready"], 2)
            for c in range(2):
                for p in range(4):
                    last = nc.tensor.matmul(pm[:, c * D:(c + 1) * D], m.wq[:, p * D + c * P:p * D + (c + 1) * P],
                                            m.g[:, p * D:(p + 1) * D], start=p == 0, stop=p == 3)
            last.then_inc(s["m_done"], 1)
            pe.wait_ge(s["far_ready"], 1)
            nc.tensor.matmul(pf[:, 0:1], m.ones, m.far_rows, start=True, stop=True).then_inc(s["far_summed"], 1)
            pe.wait_ge(s["mix_ready"], 1)

            def step(t, q):
                b = q % 2
                pe.wait_ge(s["staged"], t + 1)
                if from_step(t, RING):
                    pe.wait_ge(s["x_ready"], t - RING + 1)
                for k in range(2):
                    nc.tensor.matmul(px[q][:, 0:D], m.xnt_t[b][:, k * P:(k + 1) * P], mix[:, k, :], start=k == 0, stop=k == 1)
                for k in range(2):
                    last = nc.tensor.matmul(px[q][:, D + k * P:D + (k + 1) * P], m.xnt_t[b][:, k * P:(k + 1) * P], wsc[:, k, :],
                                            start=False, stop=True, skip_group_check=True)
                last.then_inc(s["mixed"], 1)
            steps_tiles(pe, step)


PCOLS = 8 * MUL


EARLY = E - 4


EARLY2 = E - 2


def load_w2(sp, m, e):
    sp.dma_start(m.w2[:, e * 1024:(e + 2) * 1024].rearrange("p (e k f) -> p e k f", e=2, k=4),
                 m.ins["w2"][e:e + 2].rearrange("e (k p) f -> p e k f", p=P)).then_inc(m.w2_loaded, 16)


def load_w1(sp, m, e):
    sp.dma_start(m.w1[:, e * 1024:(e + 2) * 1024].rearrange("p (e k f) -> p e k f", e=2, k=2),
                 m.ins["w1"][e:e + 2].rearrange("e (k p) f -> p e k f", p=P)).then_inc(m.w1_loaded, 16)


DVE_SEL = 2


def form_products(nc, prod, w, xs, h, s):
    w = w[:].rearrange("p (k q d) -> p k q d", k=2, q=4)
    xs = xs[:, 2 * h * D:2 * (h + 1) * D].rearrange("p (k q d) -> p k q d", k=2, q=4)
    pr = prod[:, 2 * h * PCOLS:2 * (h + 1) * PCOLS].rearrange("p (k q d) -> p k q d", k=2, q=8)
    nc.vector.tensor_tensor(pr[:, :, 0:2, :], w[:, :, 0:2, :], xs[:, :, 0:1, :].broadcast_to([P, 2, 2, MUL]), ALU.mult)
    for q in range(2):
        last = nc.vector.tensor_tensor(pr[:, :, 2 + q:8:2, :], w[:, :, 2 + q:3 + q, :].broadcast_to([P, 2, 3, MUL]),
                                       xs[:, :, 1:4, :], ALU.mult)
    last.then_inc(s["product_done"], 1)


def radial_weights(nc, wp, hid, fc1, k):
    h = slice((k // 2) * RN, (k // 2 + 1) * RN)
    return nc.tensor.matmul(wp[k // 2][:, (k % 2) * D:(k % 2 + 1) * D], hid[h, (k % 2) * P:(k % 2 + 1) * P], fc1[h, :],
                            start=True, stop=True)


def sum_tile(nc, seg, prod, sel, win, k, last_tile):
    wins = seg[:, 0:8 * win].rearrange("p (w n) -> p w n", w=8)
    sel = sel.rearrange("p (k c n) -> p k c n", k=GT, c=4)
    pr = prod[:, k * PCOLS:(k + 1) * PCOLS]
    nc.tensor.matmul(wins[:, 1:5, :], pr[:, 0:P], sel[:, k, :, :], start=k == 0, stop=last_tile, skip_group_check=True)
    for c in range(COMP):
        last = nc.tensor.matmul(wins[:, 0:6 + c:5 + c, :], pr[:, (c + 1) * P:(c + 2) * P], sel[:, k, c:4:3 - c, :],
                                start=False, stop=last_tile, skip_group_check=True)
    return last


def add_sums(nc, ysum, seg, at, win, s):
    wins = seg[:, 0:8 * win].rearrange("p (w n) -> p w n", w=8)
    for half, w in ((slice(0, MUL), slice(4, 8)), (slice(MUL, P), slice(0, 4))):
        y = ysum[half, :, ds(at, win)]
        nc.vector.tensor_tensor(y, wins[half, w, :], y, ALU.add).then_inc(s["added"], 1)


def stage_edges(nc, m, s):
    pre, wp, seg = m.bank[0:2], [m.bank[2:4], m.bank[4:6]], m.bank[6:8]
    ysum = m.ysum.rearrange("p (n q) -> p q n", q=CH)
    with nc.Block() as block:
        @block.sync
        def _(sp):
            def load_e8(g, q):
                b = q % 2
                if from_step(g, 2):
                    sp.wait_ge(s["pre_done"], g - 1)
                sp.dma_start(m.e8[b], m.ins["e8"][:, ds(g * 2 * P, 2 * P)]).then_inc(s["e8_loaded"][b], 16)
                if isinstance(g, int) and g >= NG - RING:
                    for e in range((g - NG + RING) * 4, min((g - NG + RING + 1) * 4, EARLY), 2):
                        load_w1(sp, m, e)
                    if g == NG - 1:
                        load_w2(sp, m, EARLY2)
            steps_ring(sp, NG, load_e8)

        @block.gpsimd
        def _(pool):
            def gather(g, q):
                if from_step(g, RING):
                    pool.wait_ge(s["product_done"], 2 * (g - RING) + 2)
                pool.wait_ge(s["idx_ready"], g + 1)
                passed(pool, m)
                for k in range(GT):
                    nc.gpsimd.indirect_dma_start(
                        out=m.xs[q][:, k * D:(k + 1) * D], out_offset=None, in_=m.h_table,
                        in_offset=bass.IndirectOffsetOnAxis(ap=m.idx[q][:, k:k + 1], axis=0)).then_inc(s["xs_loaded"][q], 16)
            steps_ring(pool, NG, gather)

        @block.scalar
        def _(act):
            def hidden(g, q):
                b = q % 2
                act.wait_ge(s["pre_done"], g + 1)
                if from_step(g, 2):
                    act.wait_ge(s["w_done"], 2 * g - 2)
                nc.scalar.activation(m.hid[b], pre[b][:, 0:2 * P], ACT.Silu, scale=1.0 / np.sqrt(NB)).then_inc(s["hid_ready"], 1)

            def select(g, q, k):
                b = q % 2
                if k == DVE_SEL:
                    act.wait_ge(s["onehot_ready"], g + 1)
                    if from_step(g, 2):
                        act.wait_ge(s["seg_done"], g - 1)
                for c in range(4):
                    last = nc.scalar.activation(m.sel[b][:, (k * 4 + c) * WIN:(k * 4 + c + 1) * WIN],
                                                m.onehot[b][:, k * WIN:(k + 1) * WIN], ACT.Copy,
                                                scale=m.ea[:, ds(g * 4 * GT + 4 * k + c, 1)])
                if k == GT - 1:
                    last.then_inc(s["sel_scaled"], 1)

            def indices(g, q):
                if from_step(g, RING):
                    act.wait_ge(s["product_done"], 2 * (g - RING) + 2)
                nc.scalar.copy(m.idx[q], m.src[:, ds(g * GT, GT)]).then_inc(s["idx_ready"], 1)
            for g in range(RING - 1):
                indices(g, g)
            hidden(0, 0)
            hidden(1, 1)
            for k in range(DVE_SEL, GT):
                select(0, 0, k)

            def step(g, q):
                ahead = not isinstance(g, int) or g < NG - 1
                if not isinstance(g, int) or g < NG - 2:
                    hidden(g + 2, q + 2)
                if ahead:
                    for k in range(DVE_SEL, GT):
                        select(g + 1, q + 1, k)
                if not isinstance(g, int) or g < NG - RING + 1:
                    indices(g + RING - 1, (q - 1) % RING)
            steps_ring(act, NG, step)

        @block.vector
        def _(dve):
            def onehot(g, q):
                b = q % 2
                if from_step(g, 2):
                    dve.wait_ge(s["sel_scaled"], g - 1)
                nc.vector.tensor_tensor(
                    m.onehot[b].rearrange("p (k n) -> p k n", k=GT),
                    m.iota[:, 0:WIN].unsqueeze(1).broadcast_to([P, GT, WIN]),
                    m.rel[:, ds(g * GT, GT)].unsqueeze(2).broadcast_to([P, GT, WIN]), ALU.is_equal).then_inc(s["onehot_ready"], 1)

            def select(g, q):
                b = q % 2
                dve.wait_ge(s["onehot_ready"], g + 1)
                if from_step(g, 2):
                    dve.wait_ge(s["seg_done"], g - 1)
                nc.vector.tensor_tensor(
                    m.sel[b][:, 0:DVE_SEL * 4 * WIN].rearrange("p (k c n) -> p k c n", k=DVE_SEL, c=4),
                    m.onehot[b][:, 0:DVE_SEL * WIN].rearrange("p (k n) -> p k n", k=DVE_SEL).unsqueeze(2).broadcast_to([P, DVE_SEL, 4, WIN]),
                    m.ea[:, ds(g * 4 * GT, 4 * DVE_SEL)].rearrange("p (k c) -> p k c", k=DVE_SEL).unsqueeze(3).broadcast_to([P, DVE_SEL, 4, WIN]),
                    ALU.mult).then_inc(s["sel_ready"], 1)

            def products(g, q):
                b = q % 2
                dve.wait_ge(s["xs_loaded"][q], 16 * GT // RING * (g - q) + 16 * GT)
                if from_step(g, 2):
                    dve.wait_ge(s["seg_done"], g - 1)
                for h in range(2):
                    dve.wait_ge(s["w_done"], 2 * g + h + 1)
                    form_products(nc, m.prod[b], wp[b][h], m.xs[q], h, s)

            def add_window(g, q):
                b = q % 2
                base = dve.value_load(m.base_i[0:1, ds(g, 1)], min_val=0, max_val=NPAD - WIN)
                dve.wait_ge(s["seg_done"], g + 1)
                if from_step(g, 1):
                    dve.wait_ge(s["added"], 2 * g)
                add_sums(nc, ysum, seg[b], base, WIN, s)

            onehot(0, 0)
            select(0, 0)

            def step(g, q):
                ahead = not isinstance(g, int) or g < NG - 1
                if ahead:
                    onehot(g + 1, q + 1)
                products(g, q)
                if ahead:
                    select(g + 1, q + 1)
                if from_step(g, 1):
                    add_window(g - 1, q + 1)
            steps_ring(dve, NG, step)
            add_window(NG - 1, NG - 1)

        @block.tensor
        def _(pe):
            def radial_in(g, q):
                b = q % 2
                pe.wait_ge(s["e8_loaded"][b], 8 * (g - b) + 16)
                if from_step(g, 2):
                    pe.wait_ge(s["hid_ready"], g - 1)
                nc.tensor.matmul(pre[b][:, 0:2 * P], m.fc0, m.e8[b], start=True, stop=True).then_inc(s["pre_done"], 1)

            def radial_tile(g, q, k):
                b = q % 2
                if k == 0:
                    pe.wait_ge(s["hid_ready"], g + 1)
                    if from_step(g, 2):
                        pe.wait_ge(s["product_done"], 2 * g - 2)
                last = radial_weights(nc, wp[b], m.hid[b], m.fc1, k)
                if k % 2:
                    last.then_inc(s["w_done"], 1)

            def segment_tile(g, q, k):
                b = q % 2
                if k == 0:
                    pe.wait_ge(s["sel_ready"], g + 1)
                    pe.wait_ge(s["sel_scaled"], g + 1)
                    if from_step(g, 2):
                        pe.wait_ge(s["added"], 2 * g - 2)
                if k % 2 == 0:
                    pe.wait_ge(s["product_done"], 2 * g + k // 2 + 1)
                last = sum_tile(nc, seg[b], m.prod[b], m.sel[b], WIN, k, k == GT - 1)
                if k == GT - 1:
                    last.then_inc(s["seg_done"], 1)

            radial_in(0, 0)
            radial_in(1, 1)
            for k in range(GT):
                radial_tile(0, 0, k)

            def step(g, q):
                if not isinstance(g, int) or g < NG - 2:
                    radial_in(g + 2, q + 2)
                for k in range(GT):
                    if not isinstance(g, int) or g < NG - 1:
                        radial_tile(g + 1, q + 1, k)
                    segment_tile(g, q, k)
            steps_ring(pe, NG, step)


def stage_far(nc, m, s):
    pre, wp, seg = m.bank[0], m.bank[2:4], m.bank[6]
    ysum = m.ysum.rearrange("p (n q) -> p q n", q=CH)
    windows = NPAD // FAR_WIN

    def if_far(eng, body):
        with eng.If(eng.value_load(m.far_flag[0:1, 0:1], min_val=0, max_val=P * ET) > 0):
            body()
        with eng.Else():
            passed(eng, m)

    with nc.Block() as block:
        @block.sync
        def _(sp):
            def body():
                sp.dma_start(m.far_dst_i, m.ins["dst"]).then_inc(s["dst_loaded"], 16)
                with sp.Fori(0, NG) as g:
                    sp.wait_ge(s["pre_done"], g + 1)
                    sp.dma_start(m.e8[0], m.ins["e8"][:, ds(g * 2 * P, 2 * P)]).then_inc(s["e8_loaded"], 16)
            if_far(sp, body)

        @block.gpsimd
        def _(pool):
            def body():
                with pool.Fori(0, NG) as g:
                    pool.wait_ge(s["product_done"], g * 2 + 1)
                    passed(pool, m)
                    nc.gpsimd.tensor_copy(m.idx[0], m.src[:, ds(g * GT, GT)]).then_inc(s["idx_ready"], 1)
                    pool.wait_ge(s["idx_ready"], g + 1)
                    passed(pool, m)
                    for k in range(GT):
                        nc.gpsimd.indirect_dma_start(
                            out=m.xs[0][:, k * D:(k + 1) * D], out_offset=None, in_=m.h_table,
                            in_offset=bass.IndirectOffsetOnAxis(ap=m.idx[0][:, k:k + 1], axis=0)).then_inc(s["xs_loaded"], 16)
            if_far(pool, body)

        @block.scalar
        def _(act):
            def body():
                with act.Fori(0, NG) as g:
                    act.wait_ge(s["pre_done"], g + 2)
                    act.wait_ge(s["w_tiles"], g * GT + 1)
                    nc.scalar.activation(m.hid[0], pre[:, 0:2 * P], ACT.Silu, scale=1.0 / np.sqrt(NB)).then_inc(s["hid_ready"], 1)
            if_far(act, body)

        @block.tensor
        def _(pe):
            def body():
                pe.sem_inc(s["pre_done"], 1)
                pe.sem_inc(s["w_tiles"], 1)
                with pe.Fori(0, NG) as g:
                    pe.wait_ge(s["e8_loaded"], g * 16 + 16)
                    nc.tensor.matmul(pre[:, 0:2 * P], m.fc0, m.e8[0], start=True, stop=True).then_inc(s["pre_done"], 1)
                    pe.wait_ge(s["hid_ready"], g + 1)
                    for k in range(GT):
                        radial_weights(nc, wp, m.hid[0], m.fc1, k).then_inc(s["w_tiles"], 1)
                    pe.wait_ge(s["product_done"], g * 2 + 3)
                    passed(pe, m)
                    with pe.Fori(0, windows) as w:
                        pe.wait_ge(s["sel_ready"], g * windows + w + 1)
                        for k in range(GT):
                            last = sum_tile(nc, seg, m.prod[0], m.far_sel, FAR_WIN, k, k == GT - 1)
                        last.then_inc(s["seg_done"], 1)
            if_far(pe, body)

        @block.vector
        def _(dve):
            def body():
                dve.sem_inc(s["product_done"], 1)
                link = chain(dve, s["dve_chain"])
                dve.wait_ge(s["dst_loaded"], 16)
                nc.vector.tensor_scalar(m.far, m.rel, 0.0, None, ALU.is_lt)
                link(nc.vector.tensor_scalar(m.far_b, m.rel, float(WIN), None, ALU.is_ge))
                nc.vector.tensor_copy(m.far_dst, m.far_dst_i)
                link(nc.vector.tensor_tensor(m.far, m.far, m.far_b, ALU.add))
                link(nc.vector.scalar_tensor_tensor(m.far_dst, m.far_dst, 1.0, m.far, ALU.add, ALU.mult))
                with dve.Fori(0, NG) as g:
                    dve.wait_ge(s["w_tiles"], g * GT + GT + 1)
                    dve.wait_ge(s["xs_loaded"], g * 16 * GT + 16 * GT)
                    passed(dve, m)
                    for h in range(2):
                        form_products(nc, m.prod[0], wp[h], m.xs[0], h, s)
                    nc.vector.tensor_scalar(m.far_rel, m.far_dst[:, ds(g * GT, GT)], float(FAR_WIN - 1), None,
                                            ALU.add).then_inc(s["rel_ready"], 1)
                    with dve.Fori(0, windows) as w:
                        dve.wait_ge(s["rel_ready"], g * (windows + 1) + w + 1)
                        passed(dve, m)
                        nc.vector.tensor_scalar(m.far_rel, m.far_rel, -float(FAR_WIN), None, ALU.add).then_inc(s["rel_ready"], 1)
                        dve.wait_ge(s["rel_ready"], g * (windows + 1) + w + 2)
                        passed(dve, m)
                        nc.vector.tensor_tensor(m.far_onehot.rearrange("p (k n) -> p k n", k=GT),
                                                m.iota[:, 0:FAR_WIN].unsqueeze(1).broadcast_to([P, GT, FAR_WIN]),
                                                m.far_rel.unsqueeze(2).broadcast_to([P, GT, FAR_WIN]),
                                                ALU.is_equal).then_inc(s["onehot_ready"], 1)
                        dve.wait_ge(s["onehot_ready"], g * windows + w + 1)
                        passed(dve, m)
                        nc.vector.tensor_tensor(
                            m.far_sel.rearrange("p (k c n) -> p k c n", k=GT, c=4),
                            m.far_onehot.rearrange("p (k n) -> p k n", k=GT).unsqueeze(2).broadcast_to([P, GT, 4, FAR_WIN]),
                            m.ea[:, ds(g * 4 * GT, 4 * GT)].rearrange("p (k c) -> p k c", k=GT).unsqueeze(3).broadcast_to([P, GT, 4, FAR_WIN]),
                            ALU.mult).then_inc(s["sel_ready"], 1)
                        dve.wait_ge(s["seg_done"], g * windows + w + 1)
                        add_sums(nc, ysum, seg, w * FAR_WIN, FAR_WIN, s)
                        dve.wait_ge(s["added"], g * 2 * windows + w * 2 + 2)
            if_far(dve, body)


def stage_tokens(nc, m, s):
    x = m.x.rearrange("p (t d) -> p t d", t=NT)
    ysum = m.ysum.rearrange("p (n q) -> p q n", q=CH)
    banks, back = (0, 1, 0, 1, 2), (3, 3, 2, 2, 5)
    po, pt = ([m.bank[first + i][:, 0:D] for i in banks] for first in (0, 3))
    pl, pc = m.bank[6], m.bank[7]
    ppre, ptot = pc[:, 0:CK * E], pc[:, CK * E:2 * CK * E]
    gate = m.gate.rearrange("p (k f) -> p k f", k=2)
    v = m.chunk
    chunks = NT // CK

    def row(c, j):
        return x[:, ds(c * CK + j, 1), :].rearrange("p a d -> p (a d)")

    def tiles(a):
        return a.rearrange("p (t e) -> p t e", t=CK)

    def zero_tails(eng, part):
        first, end, zeroed = TAILS[part], TAILS[part + 1], s["tail_zeroed"][part]
        eng.wait_ge(s["tails_ready"], 1)
        with eng.Fori(first, end) as e:
            at = eng.value_load(m.tail[0:1, ds(e, 1)], min_val=0, max_val=E * CAP - P)
            eng.dma_start(m.slots_in[ds(at, P), :], m.zero_row).then_inc(zeroed, 16)
        eng.wait_ge(zeroed, 16 * (end - first))

    with nc.Block() as block:
        @block.sync
        def _(sp):
            for dst, src in ((m.b1, m.ins["b1"]), (m.b2, m.ins["b2"].broadcast_to([P, E * D])),
                             (m.gamma, m.ins["gamma"].broadcast_to([P, D])), (m.beta, m.ins["beta"].broadcast_to([P, D]))):
                sp.dma_start(dst, src).then_inc(m.w2_loaded, 16)
            for e in range(0, EARLY2, 2):
                sp.wait_ge(s["out_done"], min(-(-(e + 2) * 1024 // (CH * P)), NT))
                load_w2(sp, m, e)
            for e in range(EARLY, E, 2):
                load_w1(sp, m, e)
            zero_tails(sp, 0)

        @block.scalar
        def _(act):
            def stage(c, j):
                if from_step(c, 1):
                    act.wait_ge(s["out_done"], c * CK + j + 1 - CK)
                nc.scalar.copy(m.y_t[j].rearrange("p (q n) -> p q n", q=CH),
                               ysum[:, :, ds((c * CK + j) * P, P)]).then_inc(s["staged"], 1)

            def copy(c, j):
                act.wait_ge(s["turned"], c * CK + j + 1)
                if from_step(c, 1):
                    act.wait_ge(s["logits_done"], c * CK + j + 1 - CK)
                nc.scalar.copy(m.xt[j], pt[j]).then_inc(s["xt_ready"], 1)
                nc.scalar.copy(row(c, j), m.x_t[j]).then_inc(s["x_kept"], 1)

            def send(c, j):
                if j == 0:
                    act.wait_ge(s["slots_ready"], c + 1)
                act.wait_ge(s["x_kept"], c * CK + j + 1)
                if from_step(c, 1):
                    act.wait_ge(s["sent"][j], c * 32)
                passed(act, m)
                nc.scalar.copy(m.slot_q[j], m.slot[:, ds(c * CK + j, 1), :].rearrange("p a k -> p (a k)"))
                nc.scalar.activation(m.yn_q[j], row(c, j), ACT.Identity, bias=m.shift[:, ds(c * CK + j, 1)],
                                     scale=m.rstd[:, ds(c * CK + j, 1)]).then_inc(s["yn_ready"], 1)

            def step(c, last=False):
                for j in range(CK):
                    copy(c, j)
                    if j < CK - AHEAD:
                        stage(c, j + AHEAD)
                    elif not last:
                        stage(c + 1, j + AHEAD - CK)
                    if from_step(c, 1) and j == CK - 2:
                        send(c - 1, 0)
                        send(c - 1, 1)
                act.wait_ge(s["var_ready"], c + 1)
                passed(act, m)
                nc.scalar.activation(v.tmp_a, v.tmp_b, ACT.Sqrt, bias=m.eps).then_inc(s["std_ready"], 1)
                if from_step(c, 1):
                    for j in range(2, CK):
                        send(c - 1, j)
            for j in range(AHEAD):
                stage(0, j)
            step(0)
            step(1)
            with act.Fori(2, chunks - 1) as c:
                step(c)
            step(chunks - 1, True)
            for j in range(CK):
                send(chunks - 1, j)
            act.wait_ge(s["gap_ready"], chunks)
            nc.scalar.activation(m.gw[1], m.gap, ACT.Exp).then_inc(s["exp_done"], 1)
            zero_tails(act, 1)

        @block.gpsimd
        def _(pool):
            with pool.Fori(0, chunks) as c:
                for j in range(CK):
                    pool.wait_ge(s["yn_ready"], c * CK + j + 1)
                    passed(pool, m)
                    for k in range(2):
                        nc.gpsimd.indirect_dma_start(
                            out=m.slots_in, out_offset=bass.IndirectOffsetOnAxis(ap=m.slot_q[j][:, k:k + 1], axis=0),
                            in_=m.yn_q[j], in_offset=None, bounds_check=NSLOT - 1, oob_is_err=False).then_inc(s["sent"][j], 16)
            zero_tails(pool, 2)
            pool.wait_ge(m.zeroed, 16 * (SPARE // 8))

        @block.tensor
        def _(pe):
            for k in range(2):
                last = nc.tensor.matmul(pl[:, 0:E], m.ones, gate[:, k, :], start=k == 0, stop=k == 1)
            last.then_inc(s["gate_summed"], 1)

            def second_map(c, j):
                pe.wait_ge(s["staged"], c * CK + j + 1)
                if from_step(c * CK + j, back[j]):
                    pe.wait_ge(s["x_ready"], c * CK + j + 1 - back[j])
                for q in range(CH):
                    w = m.wlin2[:, 0:MUL] if q == 0 else m.wlin2[:, MUL:P]
                    last = nc.tensor.matmul(po[j][:, q * MUL:(q + 1) * MUL], m.y_t[j][:, q * P:(q + 1) * P], w, start=True, stop=True)
                last.then_inc(s["out_done"], 1)

            def turn(c, j):
                pe.wait_ge(s["x_ready"], c * CK + j + 1)
                if from_step(c * CK + j, back[j]):
                    pe.wait_ge(s["xt_ready"], c * CK + j + 1 - back[j])
                nc.tensor.transpose(pt[j][:, 0:P], m.x_t[j][:, 0:P], m.ident)
                nc.tensor.transpose(pt[j][:, P:2 * P], m.x_t[j][:, P:2 * P], m.ident).then_inc(s["turned"], 1)

            def logits(c, j):
                pe.wait_ge(s["xt_ready"], c * CK + j + 1)
                if j == 0 and from_step(c, 1):
                    pe.wait_ge(s["logits_read"], c)
                for k in range(2):
                    last = nc.tensor.matmul(pl[:, j * E:(j + 1) * E], m.xt[j][:, k * P:(k + 1) * P], gate[:, k, :],
                                            start=k == 0, stop=k == 1)
                last.then_inc(s["logits_done"], 1)

            def count(c):
                pe.wait_ge(s["both_ready"], c + 1)
                nc.tensor.matmul(ppre, m.upper, v.both, start=True, stop=True)
                nc.tensor.matmul(ptot, m.ones, v.both, start=True, stop=True).then_inc(s["counted"], 1)

            def step(c):
                for j in range(CK):
                    second_map(c, j)
                    if j == 2 and from_step(c, 1):
                        count(c - 1)
                    if j >= 1:
                        turn(c, j - 1)
                    if j == 2 and not from_step(c, 1):
                        pe.wait_ge(s["gate_centred"], 1)
                    if j >= 2:
                        logits(c, j - 2)
                turn(c, CK - 1)
                logits(c, CK - 2)
                logits(c, CK - 1)
            step(0)
            with pe.Fori(1, chunks) as c:
                step(c)
            count(chunks - 1)

        @block.vector
        def _(dve):
            def plain(ins):
                plain_count[0] += 1
                ins.then_inc(s["dve_chain"], 1)
                dve.wait_ge(s["dve_chain"], plain_count[0])
            plain_count = [0]

            def residual(c, j):
                dve.wait_ge(s["out_done"], c * CK + j + 1)
                if from_step(c, 1):
                    dve.wait_ge(s["turned"], c * CK + j + 1 - CK)
                    dve.wait_ge(s["x_kept"], c * CK + j + 1 - CK)
                nc.vector.scalar_tensor_tensor(m.x_t[j], po[j], m.z[:, ds(c * CK + j, 1)], row(c, j), ALU.mult,
                                               ALU.add).then_inc(s["x_ready"], 1)
                dve.wait_ge(s["x_ready"], c * CK + j + 1)
                nc.vector.bn_stats(v.st[:, j * 6:(j + 1) * 6], m.x_t[j]).then_inc(s["bn_done"], 1)

            def choose(c, link):
                chunk = ds(c * CK, CK)
                dve.wait_ge(s["bn_done"], c * CK + CK)
                row_stats(dve, link, v, v.st.rearrange("p (t s) -> p t s", t=CK), s, c + 1)
                dve.wait_ge(s["stats_ready"], c + 1)
                passed(dve, m)
                nc.vector.tensor_copy(m.rstd[:, chunk], v.rstd)
                nc.vector.tensor_copy(m.shift[:, chunk], v.shift)
                dve.wait_ge(s["logits_done"], c * CK + CK)
                lg, top, topi = tiles(v.logits), tiles(v.top), tiles(v.topi)
                nc.vector.tensor_tensor(lg, tiles(pl[:, 0:CK * E]), v.rstd.unsqueeze(2).broadcast_to([P, CK, E]),
                                        ALU.mult).then_inc(s["logits_read"], 1)
                dve.wait_ge(s["logits_read"], c + 1)
                link(nc.vector.tensor_tensor(lg, lg, m.gateb.unsqueeze(1).broadcast_to([P, CK, E]), ALU.add))
                passed(dve, m)
                for j in range(CK):
                    last = nc.vector.max(top[:, j, :], lg[:, j, :])
                link(last)
                passed(dve, m)
                for j in range(CK):
                    last = nc.vector.max_index(topi[:, j, :], top[:, j, :], lg[:, j, :])
                link(last)
                nc.vector.tensor_tensor(m.gap[:, chunk], top[:, :, 1], top[:, :, 0], ALU.subtract).then_inc(s["gap_ready"], 1)
                for k in range(2):
                    last = nc.vector.tensor_copy(v.one[k], topi[:, :, k])
                link(last)
                for k in range(2):
                    last = nc.vector.tensor_tensor(tiles(v.oh[k]), m.iota[:, 0:E].unsqueeze(1).broadcast_to([P, CK, E]),
                                                   v.one[k].unsqueeze(2).broadcast_to([P, CK, E]), ALU.is_equal)
                for k in range(2):
                    nc.vector.tensor_copy(m.top_f[k][:, chunk], v.one[k])
                link(last)
                for k in range(2):
                    last = nc.vector.tensor_tensor(tiles(v.oh[k]), tiles(v.oh[k]),
                                                   m.valid[:, chunk].unsqueeze(2).broadcast_to([P, CK, E]), ALU.mult)
                link(last)
                nc.vector.tensor_tensor(v.both, v.oh[0], v.oh[1], ALU.add).then_inc(s["both_ready"], 1)

            def slots(c, link):
                dve.wait_ge(s["counted"], c + 1)
                tot, before = tiles(ptot), v.before.rearrange("p (t e) -> p t e", t=CK + 1)
                link(nc.vector.tensor_copy(before[:, 0, :], before[:, CK, :]))
                for j in range(CK):
                    link(nc.vector.tensor_tensor(before[:, j + 1, :], before[:, j, :], tot[:, j, :], ALU.add))
                link(nc.vector.tensor_tensor(v.pos, ppre, v.before[:, 0:CK * E], ALU.add))
                for k in range(2):
                    last = nc.vector.tensor_tensor(v.oh[k], v.oh[k], v.pos, ALU.mult)
                link(last)
                for k in range(2):
                    last = nc.vector.tensor_reduce(v.one[k], tiles(v.oh[k]), AX, ALU.add)
                link(last)
                for k in range(2):
                    last = nc.vector.tensor_tensor(v.slot_f[k], v.one[k], m.far_off[:, ds(c * CK, CK)], ALU.add)
                link(last)
                passed(dve, m)
                for k in range(2):
                    last = nc.vector.tensor_copy(m.slot[:, ds(c * CK, CK), k], v.slot_f[k])
                last.then_inc(s["slots_ready"], 1)

            dve.wait_ge(s["gate_summed"], 1)
            plain(nc.vector.tensor_scalar(m.gate_mean, pl[:, 0:E], 1.0 / D, None, ALU.mult))
            nc.vector.tensor_tensor(gate, gate, m.gate_mean.unsqueeze(1).broadcast_to([P, 2, E]),
                                    ALU.subtract).then_inc(s["gate_centred"], 1)
            nc.vector.tensor_scalar(v.before[:, CK * E:(CK + 1) * E], m.iota[:, 0:E], float(CAP), None, ALU.mult)
            nc.vector.tensor_scalar(m.far_off, m.valid, -float(FAR_SLOT), float(FAR_SLOT), ALU.mult, ALU.add)
            plain(nc.vector.memset(m.zero_row, 0.0))
            for j in range(CK):
                residual(0, j)
            choose(0, plain)
            with dve.Fori(1, chunks) as c:
                count = [0]

                def link(ins):
                    count[0] += 1
                    ins.then_inc(s["loop_chain"], 1)
                    dve.wait_ge(s["loop_chain"], (c - 1) * LINKS + count[0])
                for j in range(3):
                    residual(c, j)
                slots(c - 1, link)
                for j in range(3, CK):
                    residual(c, j)
                choose(c, link)
                assert count[0] == LINKS, count[0]
            link = plain
            slots(chunks - 1, link)

            end = v.before[:, CK * E:(CK + 1) * E]
            nc.vector.tensor_copy(m.tail, end).then_inc(s["tails_ready"], 1)
            link(nc.vector.tensor_scalar(m.starts, m.iota[:, 0:E], float(CAP), None, ALU.mult))
            link(nc.vector.tensor_tensor(m.counts, end, m.starts, ALU.subtract))
            link(nc.vector.tensor_tensor(m.more.rearrange("p (e j) -> p e j", e=E), m.counts.unsqueeze(2).broadcast_to([P, E, NT]),
                                         m.steps_of.unsqueeze(1).broadcast_to([P, E, NT]), ALU.is_gt))
            link(nc.vector.tensor_reduce(m.nblk, m.more.rearrange("p (e j) -> p e j", e=E), AX, ALU.add))
            link(nc.vector.tensor_tensor_scan(m.blk_end, m.ones[:, 0:E], m.nblk, 0.0, ALU.mult, ALU.add))
            before = m.before.rearrange("p (j e) -> p j e", j=NBLK)
            link(nc.vector.tensor_tensor(before, m.blk_end.unsqueeze(1).broadcast_to([P, NBLK, E]),
                                         m.iota[:, 0:NBLK].unsqueeze(2).broadcast_to([P, NBLK, E]), ALU.is_le))
            link(nc.vector.tensor_reduce(m.blk_f, before, AX, ALU.add))
            link(nc.vector.tensor_scalar(m.blk_f, m.blk_f, float(E - 1), None, ALU.min))
            nc.vector.tensor_copy(m.blk_expert, m.blk_f)
            link(nc.vector.tensor_tensor(m.left, m.blk_end, m.nblk, ALU.subtract))
            link(nc.vector.scalar_tensor_tensor(m.left, m.left, -float(P), m.starts, ALU.mult, ALU.add))
            link(nc.vector.tensor_scalar(m.nblk, m.nblk, -float(P), float(CAP), ALU.mult, ALU.add))
            link(nc.vector.tensor_tensor(before, before, m.nblk.unsqueeze(1).broadcast_to([P, NBLK, E]), ALU.mult))
            link(nc.vector.tensor_reduce(m.blk_f, before, AX, ALU.add))
            link(nc.vector.scalar_tensor_tensor(m.blk_f, m.iota[:, 0:NBLK], float(P), m.blk_f, ALU.mult, ALU.add))
            nc.vector.tensor_copy(m.blk_row, m.blk_f)
            oh = m.before[:, 0:NT * E].rearrange("p (t e) -> p t e", t=NT)
            for k in range(2):
                link(nc.vector.tensor_tensor(oh, m.iota[:, 0:E].unsqueeze(1).broadcast_to([P, NT, E]),
                                             m.top_f[k].unsqueeze(2).broadcast_to([P, NT, E]), ALU.is_equal))
                link(nc.vector.tensor_tensor(oh, oh, m.left.unsqueeze(1).broadcast_to([P, NT, E]), ALU.mult))
                link(nc.vector.tensor_reduce(m.tmp_a, oh, AX, ALU.add))
                link(nc.vector.tensor_copy(m.tmp_b, m.slot[:, :, k]))
                link(nc.vector.tensor_tensor(m.tmp_b, m.tmp_b, m.tmp_a, ALU.subtract))
                nc.vector.tensor_copy(m.slot_out[:, :, k], m.tmp_b)
            dve.wait_ge(s["exp_done"], 1)
            link(nc.vector.tensor_scalar(m.tmp_a, m.gw[1], 1.0, None, ALU.add))
            link(nc.vector.reciprocal(m.gw[0], m.tmp_a))
            link(nc.vector.tensor_tensor(m.gw[1], m.gw[1], m.gw[0], ALU.mult))


TAILS = (0, 9, 13, E)
AHEAD = 3
LINKS = 21


def stage_experts(nc, m, s):
    px, ph, py = m.bank[0:2], m.bank[2:4], m.bank[6:8]
    with nc.Block() as block:
        @block.sync
        def _(sp):
            def load(j, q):
                at = sp.value_load(m.blk_row[0:1, ds(j, 1)], min_val=0, max_val=NSLOT - P)
                if from_step(j, RING):
                    sp.wait_ge(s["x_turned"], j - RING + 1)
                sp.dma_start(m.xb[q], m.slots_in[ds(at, P), :]).then_inc(s["x_loaded"][q], 16)

            for j in range(RING - 1):
                load(j, j)

            def step(j, q):
                if not isinstance(j, int) or j < NBLK - RING + 1:
                    load(j + RING - 1, (q - 1) % RING)
            steps_ring(sp, NBLK, step)

        @block.gpsimd
        def _(pool):
            def store(j, b):
                pool.wait_ge(s["y_ready"], j + 1)
                nc.gpsimd.dma_start(m.slots_out[ds(j * P, P), :], m.yb[b]).then_inc(s["y_stored"][b], 16)
            steps(pool, NBLK, store)
            pool.wait_ge(s["y_stored"][0], 8 * NBLK)
            pool.wait_ge(s["y_stored"][1], 8 * NBLK)

        @block.tensor
        def _(pe):
            pe.wait_ge(m.w1_loaded, 16 * (E // 2))
            pe.wait_ge(m.w2_loaded, 16 * (E // 2 + 4))

            def turn_x(j, q):
                b = q % 2
                pe.wait_ge(s["x_loaded"][q], 16 // RING * (j - q) + 16)
                if from_step(j, 2):
                    pe.wait_ge(s["xt_ready"], j - 1)
                nc.tensor.transpose(px[b][:, 0:P], m.xb[q][:, 0:P], m.ident)
                nc.tensor.transpose(px[b][:, P:2 * P], m.xb[q][:, P:2 * P], m.ident).then_inc(s["x_turned"], 1)

            def first(j, b):
                pe.wait_ge(s["xt_ready"], j + 1)
                pe.wait_ge(s["w1_staged"], j + 1)
                if from_step(j, 2):
                    pe.wait_ge(s["ht_ready"], j - 1)
                for f in range(4):
                    for k in range(2):
                        last = nc.tensor.matmul(ph[b][:, f * P:(f + 1) * P], m.w1_t[b][:, k * FF + f * P:k * FF + (f + 1) * P],
                                                m.xbt[b][:, k * P:(k + 1) * P], start=k == 0, stop=k == 1)
                last.then_inc(s["h_done"], 1)

            def second(j, b):
                e = pe.value_load(m.blk_expert[0:1, ds(j, 1)], min_val=0, max_val=E - 1)
                pe.wait_ge(s["ht_ready"], j + 1)
                if from_step(j, 2):
                    pe.wait_ge(s["y_ready"], j - 1)
                for k in range(4):
                    last = nc.tensor.matmul(py[b][:, 0:D], m.hbt[b][:, k * P:(k + 1) * P], m.w2[:, ds(e * 1024 + k * D, D)],
                                            start=k == 0, stop=k == 3)
                last.then_inc(s["y_done"], 1)

            turn_x(0, 0)
            turn_x(1, 1)
            first(0, 0)

            def step(j, q):
                b = q % 2
                if not isinstance(j, int) or j < NBLK - 2:
                    turn_x(j + 2, (q + 2) % RING)
                if not isinstance(j, int) or j < NBLK - 1:
                    first(j + 1, 1 - b)
                second(j, b)
            steps_ring(pe, NBLK, step)

        @block.scalar
        def _(act):
            act.wait_ge(m.w2_loaded, 16 * (E // 2 + 4))

            def copy_xt(j, b):
                act.wait_ge(s["x_turned"], j + 1)
                if from_step(j, 2):
                    act.wait_ge(s["h_done"], j - 1)
                nc.scalar.copy(m.xbt[b], px[b][:, 0:2 * P]).then_inc(s["xt_ready"], 1)

            def relu(j, b):
                e = act.value_load(m.blk_expert[0:1, ds(j, 1)], min_val=0, max_val=E - 1)
                act.wait_ge(s["h_done"], j + 1)
                if from_step(j, 2):
                    act.wait_ge(s["y_done"], j - 1)
                for k in range(4):
                    last = nc.scalar.activation(m.hbt[b][:, k * P:(k + 1) * P], ph[b][:, k * P:(k + 1) * P], ACT.Relu,
                                                bias=m.b1[:, ds(e * 4 + k, 1)])
                last.then_inc(s["ht_ready"], 1)
            copy_xt(0, 0)
            copy_xt(1, 1)

            def step(j, b):
                relu(j, b)
                if not isinstance(j, int) or j < NBLK - 2:
                    copy_xt(j + 2, b)
            steps_ahead(act, NBLK, step)

        @block.vector
        def _(dve):
            dve.wait_ge(m.w1_loaded, 16 * (E // 2))
            dve.wait_ge(m.w2_loaded, 16 * (E // 2 + 4))

            def stage_w1(j, b):
                e = dve.value_load(m.blk_expert[0:1, ds(j, 1)], min_val=0, max_val=E - 1)
                if from_step(j, 2):
                    dve.wait_ge(s["h_done"], j - 1)
                nc.vector.tensor_copy(m.w1_t[b], m.w1[:, ds(e * 1024, 1024)]).then_inc(s["w1_staged"], 1)

            def rows_out(j, b):
                e = dve.value_load(m.blk_expert[0:1, ds(j, 1)], min_val=0, max_val=E - 1)
                dve.wait_ge(s["y_done"], j + 1)
                if from_step(j, 2):
                    dve.wait_ge(s["y_stored"][b], 8 * (j - b))
                nc.vector.tensor_tensor(m.yb[b], py[b][:, 0:D], m.b2[:, ds(e * D, D)], ALU.add).then_inc(s["y_ready"], 1)
            stage_w1(0, 0)
            stage_w1(1, 1)

            def step(j, b):
                if not isinstance(j, int) or j < NBLK - 2:
                    stage_w1(j + 2, b)
                rows_out(j, b)
            steps_ahead(dve, NBLK, step)


HALF = NT // 2


def stage_combine(nc, m, s):
    x = m.x.rearrange("p (t d) -> p t d", t=NT)
    u = m.u.rearrange("p (t d) -> p t d", t=NT)
    st = m.st.rearrange("p (t s) -> p t s", t=NT)

    def row(v, t):
        return v[:, ds(t, 1), :].rearrange("p a d -> p (a d)")

    def tiles(eng, first, end, step):
        assert first % RING == 0
        if first == 0:
            for t in range(RING):
                step(t, t)
            first = RING
        if end - first >= RING:
            with eng.Fori(first // RING, end // RING) as i:
                for q in range(RING):
                    step(i * RING + q, q)
        for t in range(max(first, end // RING * RING), end):
            step(t, t % RING)

    with nc.Block() as block:
        @block.gpsimd
        def _(pool):
            def fetch(t, q):
                if from_step(t, RING):
                    pool.wait_ge(s["summed"], t - RING + 1)
                pool.wait_ge(s["idx_ready"], t + 1)
                passed(pool, m)
                for k in range(2):
                    nc.gpsimd.indirect_dma_start(
                        out=m.got[q][k], out_offset=None, in_=m.slots_out,
                        in_offset=bass.IndirectOffsetOnAxis(ap=m.slot_q[q][:, k:k + 1], axis=0),
                        bounds_check=NBLK * P - 1, oob_is_err=False).then_inc(s["got"][q], 16)
            pool.wait_ge(s["cleared"], 2 * RING)
            steps_tiles(pool, fetch)

        @block.scalar
        def _(act):
            def normalise(t, q):
                if from_step(t, RING):
                    act.wait_ge(s["summed"], t - RING + 1)
                nc.scalar.copy(m.slot_q[q], m.slot_out[:, ds(t, 1), :].rearrange("p a k -> p (a k)")).then_inc(s["idx_ready"], 1)
                nc.scalar.activation(row(u, t), row(x, t), ACT.Identity,
                                     bias=m.shift[:, ds(t, 1)], scale=m.rstd[:, ds(t, 1)]).then_inc(s["yn_ready"], 1)

            def norm_sum(t, q):
                nc.scalar.activation(row(u, t), row(u, t), ACT.Identity,
                                     bias=m.shift[:, ds(t, 1)], scale=m.rstd[:, ds(t, 1)]).then_inc(s["normed"], 1)

            def both(t, q):
                normalise(t, q)
                norm_sum(t - HALF, q)
            tiles(act, 0, HALF, normalise)
            row_std(act, m.halves[0], s)
            tiles(act, HALF, 2 * HALF, both)
            tiles(act, 2 * HALF, NT, normalise)
            row_std(act, m.halves[1], s, 2)
            tiles(act, HALF, NT, norm_sum)

        @block.vector
        def _(dve):
            for q in range(RING):
                for k in range(2):
                    nc.vector.memset(m.got[q][k], 0.0).then_inc(s["cleared"], 1)

            def sums(t, q, between=None):
                dve.wait_ge(s["got"][q], 32 // RING * (t - q) + 32)
                dve.wait_ge(s["yn_ready"], t + 1)
                nc.vector.scalar_tensor_tensor(row(u, t), m.got[q][0], m.gw[0][:, ds(t, 1)], row(u, t), ALU.mult,
                                               ALU.add).then_inc(s["one_in"], 1)
                nc.vector.tensor_tensor(row(x, t), row(x, t), m.beta, ALU.add).then_inc(s["x_beta"], 1)
                dve.wait_ge(s["one_in"], t + 1)
                nc.vector.scalar_tensor_tensor(row(u, t), m.got[q][1], m.gw[1][:, ds(t, 1)], row(u, t), ALU.mult,
                                               ALU.add).then_inc(s["summed"], 1)
                if between is not None:
                    scale(between)
                dve.wait_ge(s["summed"], t + 1)
                nc.vector.bn_stats(row(st, t), row(u, t)).then_inc(s["bn_done"], 1)
                if between is not None:
                    add(between)

            def scale(t):
                dve.wait_ge(s["normed"], t + 1)
                nc.vector.tensor_tensor(row(u, t), row(u, t), m.gamma, ALU.mult).then_inc(s["scaled"], 1)

            def add(t):
                dve.wait_ge(s["scaled"], t + 1)
                nc.vector.tensor_tensor(row(x, t), row(u, t), row(x, t), ALU.add).then_inc(s["x_out"], 1)

            def both(t, q):
                sums(t, q, t - HALF)

            def finish(t, q):
                scale(t)
                if from_step(t, HALF + 1):
                    add(t - 1)
            link = chain(dve, s["dve_chain"])
            tiles(dve, 0, HALF, sums)
            dve.wait_ge(s["bn_done"], HALF)
            dve.wait_ge(s["x_beta"], HALF)
            row_stats(dve, link, m.halves[0], st[:, 0:HALF, :], s)
            tiles(dve, HALF, 2 * HALF, both)
            tiles(dve, 2 * HALF, NT, sums)
            dve.wait_ge(s["bn_done"], NT)
            dve.wait_ge(s["x_beta"], NT)
            row_stats(dve, link, m.halves[1], st[:, HALF:NT, :], s, 2)
            scale(HALF)
            for t in range(HALF + 1, HALF + RING):
                finish(t, t % RING)
            tiles(dve, HALF + RING, NT, finish)
            add(NT - 1)

        @block.sync
        def _(sp):
            def step(t, q):
                sp.wait_ge(s["x_out"], t + 1)
                sp.dma_start(m.out[ds(t * P, P), :], row(x, t)).then_inc(s["stored"], 16)
            steps_tiles(sp, step)
            sp.wait_ge(s["stored"], 16 * NT)


def build(nc, m):
    m.nc = nc
    with ExitStack() as ctx:
        def sb(name, n, dt=F32):
            return ctx.enter_context(nc.sbuf_tensor(name, [P, n], dt))

        def sem(name):
            return ctx.enter_context(nc.semaphore(name))

        def sems(prefix, names, pairs=(), rings=()):
            found = {n: sem(f"{prefix}_{n}") for n in names.split()}
            found.update({n: [sem(f"{prefix}_{n}{b}") for b in range(2)] for n in pairs})
            found.update({n: [sem(f"{prefix}_{n}{q}") for q in range(RING)] for n in rings})
            return found

        m.bank = [ctx.enter_context(nc.psum_tensor(f"bank{i}", [P, 512], F32)) for i in range(8)]
        m.h_table = nc.dram_tensor("h_table", [NPAD, D], F32, kind="Internal").ap()
        m.slots_in = nc.dram_tensor("slots_in", [NSLOT, D], F32, kind="Internal").ap()
        m.slots_out = nc.dram_tensor("slots_out", [NBLK * P, D], F32, kind="Internal").ap()

        m.x = sb("x", NT * D)[:]
        keep = Region(sb("keep", 128 * 3 + 6 * NT + NT + 5 * 128 + 32 + 16 + 4 * NT + 6 * NT + 64))
        m.ident, m.upper, m.ones = keep.take(P), keep.take(P), keep.take(P)
        m.st = keep.take(6 * NT)
        m.z = keep.take(NT)
        m.wlin2 = keep.take(P)
        m.gate, m.gateb = keep.take(2 * E), keep.take(E)
        m.rstd, m.shift, m.valid, m.node_f = keep.take(NT), keep.take(NT), keep.take(NT), keep.take(NT)
        m.tmp_a, m.tmp_b, m.gap = keep.take(NT), keep.take(NT), keep.take(NT)
        m.gw = [keep.take(NT), keep.take(NT)]
        m.steps_of, m.eps = keep.take(NT), keep.take(1)
        m.iota = sb("iota", P)[:]
        m.slot_out = sb("slot_out", NT * 2, I32)[:].rearrange("p (t k) -> p t k", k=2)
        m.slot = sb("slot", NT * 2, I32)[:].rearrange("p (t k) -> p t k", k=2)
        m.slot_q = [sb(f"slot_q{q}", 2, I32)[:] for q in range(CK)]
        m.far_flag = sb("far_flag", 1, I32)[:]
        m.blk_row, m.tail = sb("blk_row", NBLK, I32)[:], sb("tail", E, I32)[:]
        m.blk_expert = sb("blk_expert", NBLK, I32)[:]

        low = sb("low", E * 1024)[:]
        m.ysum, m.w2 = low[:, 0:CH * NPAD], low
        high = sb("high", E * 1024)
        m.w1 = high[:]
        r = Region(high)
        m.wkv, m.wq, m.wout = r.take(2 * 2 * INNER), r.take(4 * D), r.take(4 * D)
        m.wlin1, m.wsc, m.bout, m.zeros = r.take(2 * P), r.take(2 * P), r.take(D), r.take(8 * D)
        m.wmean = r.take(4 * HEADS)
        m.dots, m.g, m.mix = r.take(4 * P), r.take(4 * D), r.take(2 * D)
        m.sumsq, m.stds = ([r.take(2 * HEADS) for _ in range(2)] for _ in range(2))
        m.rk = r.take(HEADS)
        m.xn, m.xnt_t, m.h_out = ([r.take(D) for _ in range(2)] for _ in range(3))
        m.sq = [r.take(2 * INNER) for _ in range(2)]
        m.vs, m.kc = ([r.take(INNER) for _ in range(2)] for _ in range(2))
        m.far_a, m.far_c, m.far_rows = r.take(ET), r.take(ET), r.take(1)
        m.iota_i, m.node_i, m.steps_i = (r.take(n).bitcast(I32) for n in (P, NT, NT))
        m.dst_i, m.base_bc, m.base_f = r.take(ET).bitcast(I32), r.take(NG).bitcast(I32), r.take(NG)

        mid = sb("mid", max(2 * GT * (PCOLS + 4 * WIN), 2 * NPAD))
        m.xnt = mid[:, 0:2 * NPAD]
        r = Region(mid)
        m.prod = [r.take(GT * PCOLS) for _ in range(2)]
        m.sel = [r.take(GT * 4 * WIN) for _ in range(2)]
        r = Region(mid)
        r.take(GT * PCOLS)
        m.far, m.far_b, m.far_dst, m.far_dst_i = r.take(ET), r.take(ET), r.take(ET), r.take(ET).bitcast(I32)
        m.far_sel, m.far_onehot, m.far_rel = r.take(GT * 4 * FAR_WIN), r.take(GT * FAR_WIN), r.take(GT)
        r = Region(mid)
        m.b2, m.b1 = r.take(E * D), r.take(E * 4)
        m.gamma, m.beta = r.take(D), r.take(D)

        edge = sb("edge", 5430)
        r = Region(edge)
        m.ea, m.src, m.rel = r.take(4 * ET), r.take(ET).bitcast(I32), r.take(ET)
        m.base_i = r.take(NG).bitcast(I32)
        m.fc0, m.fc1 = r.take(P)[0:2 * NB], r.take(D)
        m.e8 = [v[0:2 * NB] for v in (r.take(2 * P), r.take(2 * P))]
        m.hid = [r.take(2 * P) for _ in range(2)]
        m.onehot = [r.take(GT * WIN) for _ in range(2)]
        m.idx = [r.take(GT).bitcast(I32) for _ in range(RING)]
        r = Region(high)
        r.take(EARLY * 1024)
        m.xs = [r.take(GT * D) for _ in range(RING)]
        r = Region(high)
        r.take(EARLY * 1024)
        m.y_t = [r.take(CH * P) for _ in range(CK)]
        r = Region(edge)
        m.x_t, m.xt, m.yn_q = ([r.take(D) for _ in range(CK)] for _ in range(3))
        m.zero_row, m.far_off, m.gate_mean = r.take(D), r.take(NT), r.take(E)
        v = m.chunk = Memory()
        v.nc, v.st, v.logits, v.both, v.pos = nc, r.take(CK * 6), r.take(CK * E), r.take(CK * E), r.take(CK * E)
        v.oh, v.before = [r.take(CK * E), r.take(CK * E)], r.take((CK + 1) * E)
        v.top, v.topi = r.take(CK * 8), r.take(CK * 8).bitcast(U32)
        v.one, v.slot_f = ([r.take(CK) for _ in range(2)] for _ in range(2))
        v.tmp_a, v.tmp_b, v.gap, v.rstd, v.shift = (r.take(CK) for _ in range(5))
        m.starts, m.counts, m.nblk, m.blk_end = (r.take(E) for _ in range(4))
        m.blk_f, m.left = r.take(NBLK), r.take(E)
        m.top_f = [r.take(NT), r.take(NT)]
        r = Region(mid)
        r.take(E * D + E * 4 + 2 * D)
        m.more, m.before = r.take(E * NT), r.take(NBLK * E)
        r = Region(edge)
        m.w1_t = [r.take(2 * FF) for _ in range(2)]
        m.xb = [r.take(D) for _ in range(RING)]
        m.xbt, m.yb = ([r.take(D) for _ in range(2)] for _ in range(2))
        m.hbt = [r.take(FF) for _ in range(2)]
        r = Region(edge)
        m.got = [[r.take(D) for _ in range(2)] for _ in range(RING)]
        m.u = low[:, 0:NT * D]

        m.passed = v.passed = sem("passed")
        m.halves = [Memory(), Memory()]
        for half, part in zip(m.halves, (slice(0, HALF), slice(HALF, NT))):
            half.nc, half.passed, half.eps, half.gap = nc, m.passed, m.eps, m.gap[:, part]
            half.tmp_a, half.tmp_b, half.rstd, half.shift = m.tmp_a[:, part], m.tmp_b[:, part], m.rstd[:, part], m.shift[:, part]
        m.zeroed, m.w1_loaded, m.w2_loaded = sem("zeroed"), sem("w1_loaded"), sem("w2_loaded")
        m.later_loaded = sem("later_loaded")
        stage_load(nc, m, {"x_loaded": [sem(f"load_x{k}") for k in range(NT // CK)],
                           **sems("load", "wkv_loaded loaded made bn_done var_ready std_ready stats_ready dve_chain")})
        s = sems("att", "scaled squared sumsq_ready stds_ready v_chain dots_done vs_ready turned kv_done xnt_kept "
                 "xnt_ready xn_ready k_ready h_done h_ready", ["h_stored"])
        stage_attention(nc, m, s)
        stage_mix(nc, m, sems("mix", "dve_chain far_ready far_summed cleared dots_ready g_done g_ready m_done mix_ready mixed x_mixed x_ready staged"))
        s = sems("edge", "pre_done product_done idx_ready onehot_ready seg_done sel_ready sel_scaled w_done hid_ready added",
                 ["e8_loaded"])
        s["xs_loaded"] = [sem(f"edge_xs{q}") for q in range(RING)]
        stage_edges(nc, m, s)
        stage_far(nc, m, sems("far", "dst_loaded e8_loaded pre_done product_done idx_ready xs_loaded w_tiles hid_ready "
                              "dve_chain rel_ready onehot_ready sel_ready seg_done added"))
        s = sems("token", "out_done staged gate_summed gate_centred var_ready std_ready stats_ready turned x_ready x_kept xt_ready "
                 "logits_done logits_read both_ready counted slots_ready tails_ready gap_ready exp_done yn_ready "
                 "dve_chain loop_chain bn_done")
        s["tail_zeroed"] = [sem(f"token_tail_zeroed{part}") for part in range(3)]
        s["sent"] = [sem(f"token_sent{j}") for j in range(CK)]
        stage_tokens(nc, m, s)
        stage_experts(nc, m, sems("moe", "x_turned y_ready xt_ready w1_staged h_done ht_ready y_done",
                                  ["y_stored"], ["x_loaded"]))
        stage_combine(nc, m, sems("comb", "summed idx_ready cleared normed scaled x_beta yn_ready one_in bn_done dve_chain "
                                  "var_ready std_ready stats_ready x_out stored", [], ["got"]))


def kernel(x, src, dst, edge_attr_4, edge_attr_8, node_vec1, L0_gnn_W_sc0, L0_gnn_W_sc1, L0_gnn_W_lin1_0,
           L0_gnn_W_lin1_1, L0_gnn_fc_w0, L0_gnn_fc_w1, L0_gnn_W_lin2_0, L0_gnn_W_lin2_1, L0_mix_Wqkv, L0_mix_Wout,
           L0_mix_bout, L0_ffn_gate_w, L0_ffn_gate_b, L0_ffn_w1, L0_ffn_b1, L0_ffn_w2, L0_ffn_b2, L0_ffn_gamma,
           L0_ffn_beta):
    from concourse import bacc
    from concourse.bass_utils import run_bass_kernel_spmd

    perm = np.concatenate([np.arange(MUL)] + [MUL + c + COMP * np.arange(MUL) for c in range(COMP)])
    back = np.argsort(perm)
    f = np.float32

    def padded(a, rows, fill=0):
        out = np.full((rows,) + a.shape[1:], fill, a.dtype)
        out[:a.shape[0]] = a
        return out

    def diagonal(a, b):
        out = np.zeros((P, P), f)
        out[:MUL, :MUL], out[MUL:, MUL:] = a, b
        return out

    x, src, dst, ea, e8, z = (np.asarray(v) for v in (x, src, dst, edge_attr_4, edge_attr_8, node_vec1))
    src_t = np.ascontiguousarray(padded(src, ET * P).reshape(ET, P).T)
    dst_p = padded(dst, ET * P, N - 1)
    wqkv = np.asarray(L0_mix_Wqkv)
    lin2_0, lin2_1 = np.asarray(L0_gnn_W_lin2_0), np.asarray(L0_gnn_W_lin2_1)
    fc0 = np.zeros((2 * NB, 2 * RN), f)
    fc0[:NB, :RN] = fc0[NB:, RN:] = np.asarray(L0_gnn_fc_w0)
    arrays = {
        "x": padded(x[:, perm], NPAD), "z": padded(z, NPAD).reshape(NT, P).T,
        "src": src_t, "dst": dst_p.reshape(ET, P).T, "base": dst_p[::GE].reshape(1, NG),
        "ea": padded(ea[:, [1, 2, 3, 0]], ET * P).reshape(ET, P, 4).transpose(1, 0, 2).reshape(P, ET * 4),
        "e8": padded(e8, ET * P).reshape(NG, 2, 2 * P, NB).transpose(1, 3, 0, 2).reshape(2 * NB, NG * 2 * P),
        "wkv": wqkv[INNER:].T[perm], "wq": wqkv[:INNER][:, perm], "wout": np.asarray(L0_mix_Wout).T[:, perm],
        "bout": np.asarray(L0_mix_bout)[perm].reshape(1, D),
        "wlin1": np.concatenate([diagonal(L0_gnn_W_lin1_0, L0_gnn_W_lin1_1), diagonal(L0_gnn_W_lin1_1, L0_gnn_W_lin1_1)]),
        "wsc": np.concatenate([diagonal(L0_gnn_W_sc0, L0_gnn_W_sc1), diagonal(L0_gnn_W_sc1, L0_gnn_W_sc1)]),
        "wlin2": np.concatenate([lin2_0, np.concatenate([lin2_1[MUL:], lin2_1[:MUL]])]),
        "fc0": fc0, "fc1": np.concatenate([np.asarray(L0_gnn_fc_w1)] * 2),
        "gate": np.asarray(L0_ffn_gate_w)[perm], "gateb": np.asarray(L0_ffn_gate_b).reshape(1, E),
        "w1": np.asarray(L0_ffn_w1)[:, perm], "w2": np.asarray(L0_ffn_w2)[:, :, perm],
        "b1": np.asarray(L0_ffn_b1).reshape(E, 4, P).transpose(2, 0, 1).reshape(P, E * 4),
        "b2": np.asarray(L0_ffn_b2)[:, perm].reshape(1, E * D),
        "gamma": np.asarray(L0_ffn_gamma)[perm].reshape(1, D), "beta": np.asarray(L0_ffn_beta)[perm].reshape(1, D),
    }
    nc = bacc.Bacc("TRN2", target_bir_lowering=False, num_devices=1)
    held, fed = {}, {}
    for name, a in arrays.items():
        a = np.ascontiguousarray(a)
        fed[f"in_{name}"] = a
        held[name] = nc.dram_tensor(f"in_{name}", a.shape, mybir.dt.from_np(a.dtype), kind="ExternalInput").ap()
    m = Memory()
    m.ins = held
    m.out = nc.dram_tensor("out", (NPAD, D), F32, kind="ExternalOutput").ap()
    build(nc, m)
    r = run_bass_kernel_spmd(nc, [fed], core_ids=[0])
    return r.results[0]["out"][:N, back]
```
